# Optimizing a Trainium2 kernel written in Bass

```python
import numpy as np
import jax
import jax.numpy as jnp

def _softmax(x, axis=-1):
    return jax.nn.softmax(x, axis=axis)

def _gelu(x):
    return jax.nn.gelu(x, approximate=True)

def _silu(x):
    return jax.nn.silu(x)

def _sigmoid(x):
    return jax.nn.sigmoid(x)

def _layernorm(x, axis=-1, eps=1e-05):
    m = jnp.mean(x, axis=axis, keepdims=True)
    v = jnp.var(x, axis=axis, keepdims=True)
    return (x - m) / jnp.sqrt(v + eps)

def _scatter_add(tgt, idx, src, axis=0):
    return tgt.at[idx].add(src)

def _segment_sum(src, seg, n):
    return jax.ops.segment_sum(src, seg, n)
kernel_name = 'mk_flamingo_gated_d4_seqx_r8_0c566b'

def setup_inputs(seed: int=0):
    np.random.seed(seed)
    _w = jnp.asarray

    def _rec_inputs():
        import jax
        import jax.numpy as jnp
        _rk = jax.random.key(seed)
        x = -0.0003929 + 0.9999 * jax.random.normal(jax.random.fold_in(_rk, 1), (4, 512, 128), jnp.float32)
        _lenS = 512 - jax.random.randint(jax.random.fold_in(_rk, 7), (4,), 0, max(1, 512 // 4) + 1, jnp.int32)
        _lenS2 = 32 - jax.random.randint(jax.random.fold_in(_rk, 8), (4,), 0, max(1, 32 // 4) + 1, jnp.int32)
        _ctx_1024P = jax.random.normal(jax.random.fold_in(_rk, 11), (4, 16, 128), jnp.float32)
        _ctx_1024c = jax.random.dirichlet(jax.random.fold_in(_rk, 511), 0.3 * jnp.ones((16,), jnp.float32), (4, 32))
        _ctx_1024t = jnp.einsum('bsk,bkd->bsd', _ctx_1024c, _ctx_1024P)
        _ctx_1024t = _ctx_1024t * jax.lax.rsqrt(jnp.mean(jnp.square(_ctx_1024t)) + 1e-12) * 0.953939
        ctx_1024 = 0.00191187 + 0.999416 * (_ctx_1024t + 0.3 * jax.random.normal(jax.random.fold_in(_rk, 611), (4, 32, 128), jnp.float32))
        _validS = jnp.arange(512)[None, :] < _lenS[:, None]
        _validS2 = jnp.arange(32)[None, :] < _lenS2[:, None]
        _causal = jnp.tril(jnp.ones((512, 512), dtype=bool))
        mask_1x1xSxS2_ik0 = jnp.where(jnp.broadcast_to(_validS2[0:1, None, None, :], (1, 1, 512, 32)), 0, 1).astype(jnp.int32)
        _g = jax.random.normal(jax.random.fold_in(_rk, 9001), (2, 4), jnp.float32)
        _g = jnp.sign(_g) * jnp.maximum(jnp.abs(_g), 1.0) + (_g == 0) * 1.0
        g_xattn = _g[0]
        g_ffn = _g[1]
        return (x, ctx_1024, mask_1x1xSxS2_ik0, g_xattn, g_ffn)
    x, ctx_1024, mask_1x1xSxS2_ik0, g_xattn, g_ffn = _rec_inputs()

    def _L0_xattn_setup():
        import jax, jax.numpy as jnp
        import numpy as np
        B, S, P, H, R = (4, 512, 64, 128, 8)
        SCALING = 16.0 / R

        def _lora_linear(x, W, b, A, Bm):
            return x @ W.T + b + x @ A.T @ Bm.T * SCALING
        key = jax.random.key(seed)
        ks = jax.random.split(key, 20)
        d = {'hidden_states': jax.random.normal(ks[0], (B, S, H), jnp.float32), 'past_key': jax.random.normal(ks[1], (B, P, H), jnp.float32), 'past_value': jax.random.normal(ks[2], (B, P, H), jnp.float32)}
        i = 3
        for name in ('q', 'k', 'v', 'o'):
            d[f'W{name}'] = jax.random.normal(ks[i], (H, H), jnp.float32) * (1.0 / np.sqrt(H))
            i += 1
            d[f'b{name}'] = jax.random.normal(ks[i], (H,), jnp.float32) * 0.01
            i += 1
            d[f'A{name}'] = jax.random.normal(ks[i], (R, H), jnp.float32) * 0.02
            i += 1
            d[f'B{name}'] = jax.random.normal(ks[i], (H, R), jnp.float32) * 0.02
            i += 1
        return d
    _L0_xattn_all = _L0_xattn_setup()
    _L0_xattn_in = {k: v for k, v in _L0_xattn_all.items() if k in ('Wq', 'bq', 'Aq', 'Bq', 'Wk', 'bk', 'Ak', 'Bk', 'Wv', 'bv', 'Av', 'Bv', 'Wo', 'bo', 'Ao', 'Bo')}
    del _L0_xattn_all

    def _L0_ffn_setup():
        import jax, jax.numpy as jnp
        import numpy as np
        N_EXPERTS = 32
        TOP_K = 8
        N_GROUP = 4
        TOPK_GROUP = 2
        ROUTED_SCALING = 2.5

        def _gate(x, gate_w, gate_bias):
            T, E = (x.shape[0], gate_w.shape[0])
            logits = jnp.einsum('th,eh->te', x, gate_w)
            scores = jax.nn.sigmoid(logits)
            scores_choice = scores + gate_bias[None, :]
            grp = scores_choice.reshape(T, N_GROUP, E // N_GROUP)
            top2, _ = jax.lax.top_k(grp, 2)
            group_scores = top2.sum(-1)
            _, grp_idx = jax.lax.top_k(group_scores, TOPK_GROUP)
            group_mask = jax.nn.one_hot(grp_idx, N_GROUP, dtype=scores.dtype).sum(1)
            expert_mask = jnp.repeat(group_mask, E // N_GROUP, axis=1)
            masked = jnp.where(expert_mask > 0, scores_choice, 0.0)
            _, topk_idx = jax.lax.top_k(masked, TOP_K)
            topk_w = jnp.take_along_axis(scores, topk_idx, axis=1)
            topk_w = topk_w / (topk_w.sum(-1, keepdims=True) + 1e-20)
            topk_w = topk_w * ROUTED_SCALING
            return (topk_idx, topk_w)

        def _mlp(x, wg, wu, wd):
            return jnp.einsum('...i,hi->...h', jax.nn.silu(jnp.einsum('...h,ih->...i', x, wg)) * jnp.einsum('...h,ih->...i', x, wu), wd)
        key = jax.random.key(seed)
        ks = jax.random.split(key, 9)
        B, S, H, I = (2, 64, 128, 64)
        w = 0.02
        return {'hidden_states': jax.random.normal(ks[0], (B, S, H), jnp.float32), 'gate_w': jax.random.normal(ks[1], (N_EXPERTS, H), jnp.float32) * w, 'gate_bias': jax.random.normal(ks[2], (N_EXPERTS,), jnp.float32) * w, 'expert_gate': jax.random.normal(ks[3], (N_EXPERTS, I, H), jnp.float32) * w, 'expert_up': jax.random.normal(ks[4], (N_EXPERTS, I, H), jnp.float32) * w, 'expert_down': jax.random.normal(ks[5], (N_EXPERTS, H, I), jnp.float32) * w, 'shared_gate': jax.random.normal(ks[6], (2 * I, H), jnp.float32) * w, 'shared_up': jax.random.normal(ks[7], (2 * I, H), jnp.float32) * w, 'shared_down': jax.random.normal(ks[8], (H, 2 * I), jnp.float32) * w}
    _L0_ffn_all = _L0_ffn_setup()
    _L0_ffn_in = {k: v for k, v in _L0_ffn_all.items() if k in ('gate_w', 'gate_bias', 'expert_gate', 'expert_up', 'expert_down', 'shared_gate', 'shared_up', 'shared_down')}
    del _L0_ffn_all

    def _L1_xattn_setup():
        import jax, jax.numpy as jnp
        import numpy as np
        D_MODEL = 128
        HEADS = 16
        D_K = D_MODEL // HEADS
        B, S = (4, 256)
        key = jax.random.key(seed)
        ks = jax.random.split(key, 12)
        xav = float(np.sqrt(6.0 / (D_MODEL + D_MODEL)))
        inp = {'query': jax.random.normal(ks[0], (B, S, D_MODEL), jnp.float32), 'key': jax.random.normal(ks[1], (B, S, D_MODEL), jnp.float32), 'value': jax.random.normal(ks[2], (B, S, D_MODEL), jnp.float32), 'mask': jnp.tril(jnp.ones((S, S), jnp.int32))[None, None], 'Wq': jax.random.uniform(ks[3], (D_MODEL, D_MODEL), jnp.float32, -xav, xav), 'bq': jnp.zeros((D_MODEL,), jnp.float32), 'Wk': jax.random.uniform(ks[4], (D_MODEL, D_MODEL), jnp.float32, -xav, xav), 'bk': jnp.zeros((D_MODEL,), jnp.float32), 'Wv': jax.random.uniform(ks[5], (D_MODEL, D_MODEL), jnp.float32, -xav, xav), 'bv': jnp.zeros((D_MODEL,), jnp.float32), 'Wo': jax.random.uniform(ks[6], (D_MODEL, D_MODEL), jnp.float32, -xav, xav), 'bo': jnp.zeros((D_MODEL,), jnp.float32)}
        return inp
    _L1_xattn_all = _L1_xattn_setup()
    _L1_xattn_in = {k: v for k, v in _L1_xattn_all.items() if k in ('Wq', 'bq', 'Wk', 'bk', 'Wv', 'bv', 'Wo', 'bo')}
    del _L1_xattn_all

    def _L1_ffn_setup():
        import math
        import jax, jax.numpy as jnp
        import numpy as np
        TOP_K = 2
        _GELU_C = math.sqrt(2.0 / math.pi)

        def gelu_new(x):
            return 0.5 * x * (1.0 + jnp.tanh(_GELU_C * (x + 0.044715 * x * x * x)))
        key = jax.random.key(seed)
        ks = jax.random.split(key, 6)
        B, T, C, E, H = (2, 256, 128, 8, 512)
        s_in = 1.0 / math.sqrt(C)
        s_hid = 1.0 / math.sqrt(H)
        return {'x': jax.random.normal(ks[0], (B, T, C), dtype=jnp.float32), 'router_w': jax.random.normal(ks[1], (E, C), dtype=jnp.float32) * s_in, 'w_fc': jax.random.normal(ks[2], (E, C, H), dtype=jnp.float32) * s_in, 'b_fc': jax.random.normal(ks[3], (E, H), dtype=jnp.float32) * 0.02, 'w_proj': jax.random.normal(ks[4], (E, H, C), dtype=jnp.float32) * s_hid, 'b_proj': jax.random.normal(ks[5], (E, C), dtype=jnp.float32) * 0.02}
    _L1_ffn_all = _L1_ffn_setup()
    _L1_ffn_in = {k: v for k, v in _L1_ffn_all.items() if k in ('router_w', 'w_fc', 'b_fc', 'w_proj', 'b_proj')}
    del _L1_ffn_all

    def _L2_xattn_setup():
        import jax, jax.numpy as jnp
        import numpy as np
        B, N, D, K = (4, 512, 128, 128)
        key = jax.random.key(seed)
        ks = jax.random.split(key, 5)
        q = jax.random.normal(ks[0], (B, N, D), dtype=jnp.float32)
        k = jax.random.normal(ks[1], (B, N, D), dtype=jnp.float32)
        weight = jax.random.normal(ks[2], (D, K), dtype=jnp.float32)
        kp_w = jax.random.normal(ks[3], (D, D), dtype=jnp.float32) * (1.0 / np.sqrt(D))
        kp_b = jax.random.normal(ks[4], (D,), dtype=jnp.float32) * 0.01
        return {'q': q, 'k': k, 'weight': weight, 'kp_w': kp_w, 'kp_b': kp_b}
    _L2_xattn_all = _L2_xattn_setup()
    _L2_xattn_in = {k: v for k, v in _L2_xattn_all.items() if k in ('weight', 'kp_w', 'kp_b')}
    del _L2_xattn_all

    def _L2_ffn_setup():
        import jax, jax.numpy as jnp
        import numpy as np
        D = 128
        I = 64
        E = 32
        K = 4
        T = 2 * 256
        C = 2 * T * K // E
        key = jax.random.key(seed)
        ks = jax.random.split(key, 9)
        bf = jnp.bfloat16
        std = 0.02
        x = jax.random.normal(ks[0], (2, 256, D), dtype=jnp.float32).astype(bf)
        gate_w = (std * jax.random.normal(ks[1], (E, D), dtype=jnp.float32)).astype(bf)
        bias = jnp.zeros((E,), jnp.float32)
        W1 = (std * jax.random.normal(ks[2], (E, D, I), dtype=jnp.float32)).astype(bf)
        W3 = (std * jax.random.normal(ks[3], (E, D, I), dtype=jnp.float32)).astype(bf)
        W2 = (std * jax.random.normal(ks[4], (E, I, D), dtype=jnp.float32)).astype(bf)
        sw1 = (std * jax.random.normal(ks[5], (I, D), dtype=jnp.float32)).astype(bf)
        sw3 = (std * jax.random.normal(ks[6], (I, D), dtype=jnp.float32)).astype(bf)
        sw2 = (std * jax.random.normal(ks[7], (D, I), dtype=jnp.float32)).astype(bf)
        return {'x': x, 'gate_w': gate_w, 'bias': bias, 'W1': W1, 'W3': W3, 'W2': W2, 'sw1': sw1, 'sw3': sw3, 'sw2': sw2}
    _L2_ffn_all = _L2_ffn_setup()
    _L2_ffn_in = {k: v for k, v in _L2_ffn_all.items() if k in ('gate_w', 'bias', 'W1', 'W3', 'W2', 'sw1', 'sw3', 'sw2')}
    del _L2_ffn_all

    def _L3_xattn_setup():
        import jax, jax.numpy as jnp
        import numpy as np
        D_MODEL = 128
        B, S = (4, 256)
        key = jax.random.key(seed)
        ks = jax.random.split(key, 10)
        s = 1.0 / np.sqrt(D_MODEL)
        return {'k': jax.random.normal(ks[0], (B, S, D_MODEL), jnp.float32), 'v': jax.random.normal(ks[1], (B, S, D_MODEL), jnp.float32), 'q': jax.random.normal(ks[2], (B, S, D_MODEL), jnp.float32), 'Wk': jax.random.normal(ks[3], (D_MODEL, D_MODEL), jnp.float32) * s, 'Wv': jax.random.normal(ks[4], (D_MODEL, D_MODEL), jnp.float32) * s, 'bv': jnp.zeros((D_MODEL,), jnp.float32), 'Wq': jax.random.normal(ks[5], (D_MODEL, D_MODEL), jnp.float32) * s, 'bq': jnp.zeros((D_MODEL,), jnp.float32), 'Wo': jax.random.normal(ks[6], (D_MODEL, D_MODEL), jnp.float32) * s, 'bo': jnp.zeros((D_MODEL,), jnp.float32)}
    _L3_xattn_all = _L3_xattn_setup()
    _L3_xattn_in = {k: v for k, v in _L3_xattn_all.items() if k in ('Wk', 'Wv', 'bv', 'Wq', 'bq', 'Wo', 'bo')}
    del _L3_xattn_all

    def _L3_ffn_setup():
        import jax, jax.numpy as jnp
        import numpy as np
        B, S, D = (4, 512, 128)
        H = 512
        RH = 128
        E = 16
        K = 2
        NS = 1

        def _swiglu(x, w1, w2, w3):
            return jax.nn.silu(x @ w1) * (x @ w2) @ w3
        key = jax.random.key(seed)
        ks = jax.random.split(key, 9)
        s = 0.02
        return {'x': jax.random.normal(ks[0], (B, S, D), dtype=jnp.float32), 'router_w': jax.random.normal(ks[1], (D, E), dtype=jnp.float32) * s, 'expert_bias': jnp.zeros((E,), dtype=jnp.float32), 'shared_w1': jax.random.normal(ks[2], (NS, D, H), dtype=jnp.float32) * s, 'shared_w2': jax.random.normal(ks[3], (NS, D, H), dtype=jnp.float32) * s, 'shared_w3': jax.random.normal(ks[4], (NS, H, D), dtype=jnp.float32) * s, 'routed_w1': jax.random.normal(ks[5], (E, D, RH), dtype=jnp.float32) * s, 'routed_w2': jax.random.normal(ks[6], (E, D, RH), dtype=jnp.float32) * s, 'routed_w3': jax.random.normal(ks[7], (E, RH, D), dtype=jnp.float32) * s}
    _L3_ffn_all = _L3_ffn_setup()
    _L3_ffn_in = {k: v for k, v in _L3_ffn_all.items() if k in ('router_w', 'expert_bias', 'shared_w1', 'shared_w2', 'shared_w3', 'routed_w1', 'routed_w2', 'routed_w3')}
    del _L3_ffn_all
    return {'x': x, 'ctx_1024': ctx_1024, 'mask_1x1xSxS2_ik0': mask_1x1xSxS2_ik0, 'g_xattn': g_xattn, 'g_ffn': g_ffn, 'L0_xattn_Wq': _L0_xattn_in['Wq'], 'L0_xattn_bq': _L0_xattn_in['bq'], 'L0_xattn_Aq': _L0_xattn_in['Aq'], 'L0_xattn_Bq': _L0_xattn_in['Bq'], 'L0_xattn_Wk': _L0_xattn_in['Wk'], 'L0_xattn_bk': _L0_xattn_in['bk'], 'L0_xattn_Ak': _L0_xattn_in['Ak'], 'L0_xattn_Bk': _L0_xattn_in['Bk'], 'L0_xattn_Wv': _L0_xattn_in['Wv'], 'L0_xattn_bv': _L0_xattn_in['bv'], 'L0_xattn_Av': _L0_xattn_in['Av'], 'L0_xattn_Bv': _L0_xattn_in['Bv'], 'L0_xattn_Wo': _L0_xattn_in['Wo'], 'L0_xattn_bo': _L0_xattn_in['bo'], 'L0_xattn_Ao': _L0_xattn_in['Ao'], 'L0_xattn_Bo': _L0_xattn_in['Bo'], 'L0_ffn_gate_w': _L0_ffn_in['gate_w'], 'L0_ffn_gate_bias': _L0_ffn_in['gate_bias'], 'L0_ffn_expert_gate': _L0_ffn_in['expert_gate'], 'L0_ffn_expert_up': _L0_ffn_in['expert_up'], 'L0_ffn_expert_down': _L0_ffn_in['expert_down'], 'L0_ffn_shared_gate': _L0_ffn_in['shared_gate'], 'L0_ffn_shared_up': _L0_ffn_in['shared_up'], 'L0_ffn_shared_down': _L0_ffn_in['shared_down'], 'L1_xattn_Wq': _L1_xattn_in['Wq'], 'L1_xattn_bq': _L1_xattn_in['bq'], 'L1_xattn_Wk': _L1_xattn_in['Wk'], 'L1_xattn_bk': _L1_xattn_in['bk'], 'L1_xattn_Wv': _L1_xattn_in['Wv'], 'L1_xattn_bv': _L1_xattn_in['bv'], 'L1_xattn_Wo': _L1_xattn_in['Wo'], 'L1_xattn_bo': _L1_xattn_in['bo'], 'L1_ffn_router_w': _L1_ffn_in['router_w'], 'L1_ffn_w_fc': _L1_ffn_in['w_fc'], 'L1_ffn_b_fc': _L1_ffn_in['b_fc'], 'L1_ffn_w_proj': _L1_ffn_in['w_proj'], 'L1_ffn_b_proj': _L1_ffn_in['b_proj'], 'L2_xattn_weight': _L2_xattn_in['weight'], 'L2_xattn_kp_w': _L2_xattn_in['kp_w'], 'L2_xattn_kp_b': _L2_xattn_in['kp_b'], 'L2_ffn_gate_w': _L2_ffn_in['gate_w'], 'L2_ffn_bias': _L2_ffn_in['bias'], 'L2_ffn_W1': _L2_ffn_in['W1'], 'L2_ffn_W3': _L2_ffn_in['W3'], 'L2_ffn_W2': _L2_ffn_in['W2'], 'L2_ffn_sw1': _L2_ffn_in['sw1'], 'L2_ffn_sw3': _L2_ffn_in['sw3'], 'L2_ffn_sw2': _L2_ffn_in['sw2'], 'L3_xattn_Wk': _L3_xattn_in['Wk'], 'L3_xattn_Wv': _L3_xattn_in['Wv'], 'L3_xattn_bv': _L3_xattn_in['bv'], 'L3_xattn_Wq': _L3_xattn_in['Wq'], 'L3_xattn_bq': _L3_xattn_in['bq'], 'L3_xattn_Wo': _L3_xattn_in['Wo'], 'L3_xattn_bo': _L3_xattn_in['bo'], 'L3_ffn_router_w': _L3_ffn_in['router_w'], 'L3_ffn_expert_bias': _L3_ffn_in['expert_bias'], 'L3_ffn_shared_w1': _L3_ffn_in['shared_w1'], 'L3_ffn_shared_w2': _L3_ffn_in['shared_w2'], 'L3_ffn_shared_w3': _L3_ffn_in['shared_w3'], 'L3_ffn_routed_w1': _L3_ffn_in['routed_w1'], 'L3_ffn_routed_w2': _L3_ffn_in['routed_w2'], 'L3_ffn_routed_w3': _L3_ffn_in['routed_w3']}

def reference(x, ctx_1024, mask_1x1xSxS2_ik0, g_xattn, g_ffn, L0_xattn_Wq, L0_xattn_bq, L0_xattn_Aq, L0_xattn_Bq, L0_xattn_Wk, L0_xattn_bk, L0_xattn_Ak, L0_xattn_Bk, L0_xattn_Wv, L0_xattn_bv, L0_xattn_Av, L0_xattn_Bv, L0_xattn_Wo, L0_xattn_bo, L0_xattn_Ao, L0_xattn_Bo, L0_ffn_gate_w, L0_ffn_gate_bias, L0_ffn_expert_gate, L0_ffn_expert_up, L0_ffn_expert_down, L0_ffn_shared_gate, L0_ffn_shared_up, L0_ffn_shared_down, L1_xattn_Wq, L1_xattn_bq, L1_xattn_Wk, L1_xattn_bk, L1_xattn_Wv, L1_xattn_bv, L1_xattn_Wo, L1_xattn_bo, L1_ffn_router_w, L1_ffn_w_fc, L1_ffn_b_fc, L1_ffn_w_proj, L1_ffn_b_proj, L2_xattn_weight, L2_xattn_kp_w, L2_xattn_kp_b, L2_ffn_gate_w, L2_ffn_bias, L2_ffn_W1, L2_ffn_W3, L2_ffn_W2, L2_ffn_sw1, L2_ffn_sw3, L2_ffn_sw2, L3_xattn_Wk, L3_xattn_Wv, L3_xattn_bv, L3_xattn_Wq, L3_xattn_bq, L3_xattn_Wo, L3_xattn_bo, L3_ffn_router_w, L3_ffn_expert_bias, L3_ffn_shared_w1, L3_ffn_shared_w2, L3_ffn_shared_w3, L3_ffn_routed_w1, L3_ffn_routed_w2, L3_ffn_routed_w3):
    import jax
    import jax.numpy as jnp

    def _L0_xattn_ref(hidden_states, past_key, past_value, Wq, bq, Aq, Bq, Wk, bk, Ak, Bk, Wv, bv, Av, Bv, Wo, bo, Ao, Bo):
        import jax, jax.numpy as jnp
        import numpy as np
        B, S, P, H, R = (4, 512, 64, 128, 8)
        SCALING = 16.0 / R

        def _lora_linear(x, W, b, A, Bm):
            return x @ W.T + b + x @ A.T @ Bm.T * SCALING
        q = _lora_linear(hidden_states, Wq, bq, Aq, Bq)
        k = _lora_linear(hidden_states, Wk, bk, Ak, Bk)
        v = _lora_linear(hidden_states, Wv, bv, Av, Bv)
        k = jnp.concatenate([past_key, k], axis=1)
        v = jnp.concatenate([past_value, v], axis=1)
        scores = jnp.einsum('bsh,bth->bst', q, k) / jnp.sqrt(jnp.float32(H))
        probs = jax.nn.softmax(scores, axis=-1)
        ctx = jnp.einsum('bst,bth->bsh', probs, v)
        return _lora_linear(ctx, Wo, bo, Ao, Bo)

    def _L0_ffn_ref(hidden_states, gate_w, gate_bias, expert_gate, expert_up, expert_down, shared_gate, shared_up, shared_down):
        import jax, jax.numpy as jnp
        import numpy as np
        N_EXPERTS = 32
        TOP_K = 8
        N_GROUP = 4
        TOPK_GROUP = 2
        ROUTED_SCALING = 2.5

        def _gate(x, gate_w, gate_bias):
            T, E = (x.shape[0], gate_w.shape[0])
            logits = jnp.einsum('th,eh->te', x, gate_w)
            scores = jax.nn.sigmoid(logits)
            scores_choice = scores + gate_bias[None, :]
            grp = scores_choice.reshape(T, N_GROUP, E // N_GROUP)
            top2, _ = jax.lax.top_k(grp, 2)
            group_scores = top2.sum(-1)
            _, grp_idx = jax.lax.top_k(group_scores, TOPK_GROUP)
            group_mask = jax.nn.one_hot(grp_idx, N_GROUP, dtype=scores.dtype).sum(1)
            expert_mask = jnp.repeat(group_mask, E // N_GROUP, axis=1)
            masked = jnp.where(expert_mask > 0, scores_choice, 0.0)
            _, topk_idx = jax.lax.top_k(masked, TOP_K)
            topk_w = jnp.take_along_axis(scores, topk_idx, axis=1)
            topk_w = topk_w / (topk_w.sum(-1, keepdims=True) + 1e-20)
            topk_w = topk_w * ROUTED_SCALING
            return (topk_idx, topk_w)

        def _mlp(x, wg, wu, wd):
            return jnp.einsum('...i,hi->...h', jax.nn.silu(jnp.einsum('...h,ih->...i', x, wg)) * jnp.einsum('...h,ih->...i', x, wu), wd)
        orig_shape = hidden_states.shape
        H = orig_shape[-1]
        residuals = hidden_states
        x = hidden_states.reshape(-1, H)
        topk_idx, topk_w = _gate(x, gate_w, gate_bias)
        g = jnp.einsum('th,eih->eti', x, expert_gate)
        u = jnp.einsum('th,eih->eti', x, expert_up)
        outs = jnp.einsum('eti,ehi->eth', jax.nn.silu(g) * u, expert_down)
        outs_t = jnp.transpose(outs, (1, 0, 2))
        gathered = jnp.take_along_axis(outs_t, topk_idx[:, :, None], axis=1)
        final = (gathered * topk_w[:, :, None]).sum(1)
        shared = _mlp(residuals, shared_gate, shared_up, shared_down)
        return final.reshape(orig_shape) + shared

    def _L1_xattn_ref(query, key, value, mask, Wq, bq, Wk, bk, Wv, bv, Wo, bo):
        import jax, jax.numpy as jnp
        import numpy as np
        D_MODEL = 128
        HEADS = 16
        D_K = D_MODEL // HEADS
        B, S = (4, 256)
        b, s, d = query.shape
        Q = (jnp.einsum('bsd,ed->bse', query, Wq) + bq).reshape(b, s, HEADS, D_K).transpose(0, 2, 1, 3)
        K = (jnp.einsum('bsd,ed->bse', key, Wk) + bk).reshape(b, -1, HEADS, D_K).transpose(0, 2, 1, 3)
        V = (jnp.einsum('bsd,ed->bse', value, Wv) + bv).reshape(b, -1, HEADS, D_K).transpose(0, 2, 1, 3)
        scale = 1.0 / jnp.sqrt(jnp.asarray(D_K, query.dtype))
        scores = jnp.einsum('bhqd,bhkd->bhqk', Q, K) * scale
        scores = jnp.where(mask == 0, -jnp.inf, scores)
        attn = jax.nn.softmax(scores, axis=-1)
        attn = jnp.where(jnp.isnan(attn), jnp.zeros_like(attn), attn)
        out = jnp.einsum('bhqk,bhkd->bhqd', attn, V)
        out = out.transpose(0, 2, 1, 3).reshape(b, s, d)
        return jnp.einsum('bsd,ed->bse', out, Wo) + bo

    def _L1_ffn_ref(x, router_w, w_fc, b_fc, w_proj, b_proj):
        import math
        import jax, jax.numpy as jnp
        import numpy as np
        TOP_K = 2
        _GELU_C = math.sqrt(2.0 / math.pi)

        def gelu_new(x):
            return 0.5 * x * (1.0 + jnp.tanh(_GELU_C * (x + 0.044715 * x * x * x)))
        B, T, C = x.shape
        E = router_w.shape[0]
        N = B * T
        xf = x.reshape(N, C)
        logits = xf @ router_w.T
        probs = jax.nn.softmax(logits, axis=-1)
        topk_probs, topk_idx = jax.lax.top_k(probs, TOP_K)
        topk_probs = topk_probs / jnp.sum(topk_probs, axis=-1, keepdims=True)
        combine = jnp.zeros((N, E), dtype=x.dtype).at[jnp.arange(N)[:, None], topk_idx].add(topk_probs)
        h = gelu_new(jnp.einsum('nc,ech->neh', xf, w_fc) + b_fc)
        out = jnp.einsum('neh,ehc->nec', h, w_proj) + b_proj
        y = jnp.einsum('nec,ne->nc', out, combine)
        return y.reshape(B, T, C)

    def _L2_xattn_ref(q, k, weight, kp_w, kp_b):
        import jax, jax.numpy as jnp
        import numpy as np
        B, N, D, K = (4, 512, 128, 128)
        n = q.shape[1]
        k_mod = k.mean(axis=1) @ kp_w.T + kp_b
        dynamic_weight = weight[None, :, :] * k_mod[:, :, None]
        q_f = jnp.fft.rfft(q, axis=1)
        w_f = jnp.fft.rfft(dynamic_weight, n=n, axis=2)
        y_f = q_f * jnp.transpose(w_f, (0, 2, 1))
        y = jnp.fft.irfft(y_f, n=n, axis=1)
        return y.astype(q.dtype)

    def _L2_ffn_ref(x, gate_w, bias, W1, W3, W2, sw1, sw3, sw2):
        import jax, jax.numpy as jnp
        import numpy as np
        D = 128
        I = 64
        E = 32
        K = 4
        T = 2 * 256
        C = 2 * T * K // E
        X = x.reshape(-1, D)
        logits = (X @ gate_w.T).astype(jnp.float32)
        scores = jax.nn.sigmoid(logits)
        _, idx = jax.lax.top_k(scores + bias[None, :], K)
        w = jnp.take_along_axis(scores, idx, axis=-1)
        w = w / jnp.clip(jnp.sum(w, axis=-1, keepdims=True), 1e-12, None)
        w = w.astype(x.dtype)
        eid = idx.reshape(-1)
        onehot = (eid[:, None] == jnp.arange(E)[None, :]).astype(jnp.int32)
        pos = jnp.take_along_axis(jnp.cumsum(onehot, axis=0) - 1, eid[:, None], axis=1)[:, 0]
        valid = pos < C
        posc = jnp.minimum(pos, C - 1)
        Xrep = jnp.repeat(X, K, axis=0)
        xe = jnp.zeros((E, C, D), x.dtype).at[eid, posc].add(jnp.where(valid[:, None], Xrep, jnp.zeros((), x.dtype)))
        h = jax.nn.silu(jnp.einsum('ecd,edi->eci', xe, W1)) * jnp.einsum('ecd,edi->eci', xe, W3)
        ye = jnp.einsum('eci,eid->ecd', h, W2)
        gflat = jnp.where(valid, w.reshape(-1), jnp.zeros((), x.dtype))
        yrows = ye[eid, posc] * gflat[:, None]
        out = yrows.reshape(-1, K, D).sum(axis=1)
        out = out + jax.nn.silu(X @ sw1.T) * (X @ sw3.T) @ sw2.T
        return out.reshape(x.shape)

    def _L3_xattn_ref(k, v, q, Wk, Wv, bv, Wq, bq, Wo, bo):
        import jax, jax.numpy as jnp
        import numpy as np
        D_MODEL = 128
        B, S = (4, 256)
        kp = jnp.einsum('bsd,ed->bse', k, Wk)
        vp = jnp.einsum('bsd,ed->bse', v, Wv) + bv
        qp = jnp.einsum('bsd,ed->bse', q, Wq) + bq
        scale = 1.0 / jnp.sqrt(jnp.float32(kp.shape[-1]))
        scores = jnp.einsum('bqd,bkd->bqk', qp, kp) * scale
        probs = jax.nn.softmax(scores, axis=-1)
        ctx = jnp.einsum('bqk,bkd->bqd', probs, vp)
        return jnp.einsum('bqd,ed->bqe', ctx, Wo) + bo

    def _L3_ffn_ref(x, router_w, expert_bias, shared_w1, shared_w2, shared_w3, routed_w1, routed_w2, routed_w3):
        import jax, jax.numpy as jnp
        import numpy as np
        B, S, D = (4, 512, 128)
        H = 512
        RH = 128
        E = 16
        K = 2
        NS = 1

        def _swiglu(x, w1, w2, w3):
            return jax.nn.silu(x @ w1) * (x @ w2) @ w3
        shared_out = jnp.sum(jax.vmap(lambda w1, w2, w3: _swiglu(x, w1, w2, w3))(shared_w1, shared_w2, shared_w3), axis=0)
        scores = jax.nn.sigmoid(x @ router_w)
        sel_scores = scores + expert_bias
        _, top_idx = jax.lax.top_k(sel_scores, K)
        top_scores = jnp.take_along_axis(scores, top_idx, axis=-1)
        gates = jnp.sum(jax.nn.one_hot(top_idx, E, dtype=scores.dtype) * top_scores[..., None], axis=-2)
        xf = x.reshape(-1, D)
        gf = gates.reshape(-1, E).T

        def body(acc, ws):
            w1, w2, w3, g = ws
            return (acc + _swiglu(xf, w1, w2, w3) * g[:, None], None)
        routed_out, _ = jax.lax.scan(body, jnp.zeros_like(xf), (routed_w1, routed_w2, routed_w3, gf))
        return shared_out + routed_out.reshape(x.shape)
    x = x + jnp.tanh(g_xattn[0]) * _L0_xattn_ref(_layernorm(x, axis=-1), ctx_1024, ctx_1024, L0_xattn_Wq, L0_xattn_bq, L0_xattn_Aq, L0_xattn_Bq, L0_xattn_Wk, L0_xattn_bk, L0_xattn_Ak, L0_xattn_Bk, L0_xattn_Wv, L0_xattn_bv, L0_xattn_Av, L0_xattn_Bv, L0_xattn_Wo, L0_xattn_bo, L0_xattn_Ao, L0_xattn_Bo)
    x = x + jnp.tanh(g_ffn[0]) * _L0_ffn_ref(_layernorm(x, axis=-1), L0_ffn_gate_w, L0_ffn_gate_bias, L0_ffn_expert_gate, L0_ffn_expert_up, L0_ffn_expert_down, L0_ffn_shared_gate, L0_ffn_shared_up, L0_ffn_shared_down)
    x = x + jnp.tanh(g_xattn[1]) * _L1_xattn_ref(_layernorm(x, axis=-1), ctx_1024, ctx_1024, mask_1x1xSxS2_ik0, L1_xattn_Wq, L1_xattn_bq, L1_xattn_Wk, L1_xattn_bk, L1_xattn_Wv, L1_xattn_bv, L1_xattn_Wo, L1_xattn_bo)
    x = x + jnp.tanh(g_ffn[1]) * _L1_ffn_ref(_layernorm(x, axis=-1), L1_ffn_router_w, L1_ffn_w_fc, L1_ffn_b_fc, L1_ffn_w_proj, L1_ffn_b_proj)
    x = x + jnp.tanh(g_xattn[2]) * _L2_xattn_ref(_layernorm(x, axis=-1), ctx_1024, L2_xattn_weight, L2_xattn_kp_w, L2_xattn_kp_b)
    x = x + jnp.tanh(g_ffn[2]) * _L2_ffn_ref(_layernorm(x, axis=-1), L2_ffn_gate_w, L2_ffn_bias, L2_ffn_W1, L2_ffn_W3, L2_ffn_W2, L2_ffn_sw1, L2_ffn_sw3, L2_ffn_sw2)
    x = x + jnp.tanh(g_xattn[3]) * _L3_xattn_ref(ctx_1024, ctx_1024, _layernorm(x, axis=-1), L3_xattn_Wk, L3_xattn_Wv, L3_xattn_bv, L3_xattn_Wq, L3_xattn_bq, L3_xattn_Wo, L3_xattn_bo)
    x = x + jnp.tanh(g_ffn[3]) * _L3_ffn_ref(_layernorm(x, axis=-1), L3_ffn_router_w, L3_ffn_expert_bias, L3_ffn_shared_w1, L3_ffn_shared_w2, L3_ffn_shared_w3, L3_ffn_routed_w1, L3_ffn_routed_w2, L3_ffn_routed_w3)
    return x

_drawn_inputs = setup_inputs


def setup_inputs(seed=0):
    import zlib

    import numpy as np

    out = dict(_drawn_inputs(seed))
    spreads = {'L1_xattn_bq': (0.0, 0.1),
     'L1_xattn_bk': (0.0, 0.1),
     'L1_xattn_bv': (0.0, 0.1),
     'L1_xattn_bo': (0.0, 0.1),
     'L2_ffn_bias': (0.0, 0.8),
     'L3_xattn_bv': (0.0, 0.552),
     'L3_xattn_bq': (0.0, 0.8),
     'L3_xattn_bo': (0.0, 0.469),
     'L3_ffn_expert_bias': (0.0, 0.8)}
    factors = {'g_ffn': 30.768,
     'L0_xattn_bq': 8.0,
     'L0_xattn_Aq': 5.512,
     'L0_xattn_Bq': 8.0,
     'L0_xattn_bk': 8.0,
     'L0_xattn_Ak': 5.651,
     'L0_xattn_Bk': 6.768,
     'L0_xattn_bv': 2.939,
     'L0_xattn_Av': 5.617,
     'L0_xattn_Bv': 7.526,
     'L0_xattn_bo': 2.839,
     'L0_xattn_Ao': 6.197,
     'L0_xattn_Bo': 5.526,
     'L0_ffn_gate_w': 6.29,
     'L0_ffn_gate_bias': 8.0,
     'L0_ffn_expert_gate': 5.066,
     'L0_ffn_expert_up': 6.819,
     'L0_ffn_expert_down': 5.944,
     'L0_ffn_shared_gate': 3.917,
     'L0_ffn_shared_up': 3.471,
     'L0_ffn_shared_down': 3.317,
     'L1_ffn_b_fc': 6.59,
     'L1_ffn_b_proj': 4.662,
     'L2_xattn_kp_b': 2.894,
     'L2_ffn_gate_w': 8.0,
     'L2_ffn_W1': 8.0,
     'L2_ffn_W3': 8.0,
     'L2_ffn_W2': 8.0,
     'L2_ffn_sw1': 8.0,
     'L2_ffn_sw3': 8.0,
     'L2_ffn_sw2': 8.0,
     'L3_ffn_router_w': 8.0,
     'L3_ffn_shared_w1': 8.0,
     'L3_ffn_shared_w2': 8.0,
     'L3_ffn_shared_w3': 8.0,
     'L3_ffn_routed_w1': 8.0,
     'L3_ffn_routed_w2': 8.0,
     'L3_ffn_routed_w3': 8.0}
    for name, (base, spread) in spreads.items():
        noise = np.random.default_rng([zlib.crc32(name.encode()), seed]).standard_normal(out[name].shape)
        drawn = base * np.exp(spread * noise) if base else spread * noise
        out[name] = jnp.asarray(drawn.astype(out[name].dtype))
    for name, factor in factors.items():
        out[name] = (out[name] * factor).astype(out[name].dtype)
    return out
```

```python
from contextlib import ExitStack

import concourse.bass as bass
import numpy as np
from concourse import mybir

F32 = mybir.dt.float32
F32R = mybir.dt.float32r
BF16 = mybir.dt.bfloat16
I32 = mybir.dt.int32
ALU = mybir.AluOpType
ACT = mybir.ActivationFunctionType
AX = mybir.AxisListType.X

B, S, D = 4, 512, 128
TB = S // 128
KEYS = 32
HEADS, DK = 16, 8
R = 8
NO_KEY = -1.0e30
LOW, TAKEN = -3.0e38, 3.0e38
EPS = 1e-5
N_EXP = [32, 8, 32, 16]
TOP_K = [8, 2, 4, 2]
ROUTED = [16, 32, 16, 16]
SHARED = [1, 0, 1, 4]
NC = [r + s for r, s in zip(ROUTED, SHARED)]
CB = [B * sum(NC[:l]) for l in range(5)]
CAPACITY = 2 * 512 * 4 // 32
UB = [0, CB[1], CB[1] + B * 8, CB[1] + B * 8 + B * NC[2]]
TRANSPOSED = {0: 0, 1: 1, 2: 2, 3: 3, 5: 4, 6: 5, 7: 6}

C_ID, C_HEAD, C_TRI, C_SEL, C_SEL16, C_SEL8, C_DFT = 0, 128, 144, 272, 304, 320, 328
FWD_RE_E, FWD_IM_E, FWD_RE_O, FWD_IM_O, W_IM_E, W_RE_E2, INV_RE_E, INV_IM_E, INV_RE_O, INV_IM_O = 0, 2, 4, 6, 8, 9, 10, 12, 14, 16
N_DFT = 18
C_ALL = C_DFT + N_DFT * 128


def constants():
    c = np.zeros((128, C_ALL), np.float64)
    i = np.arange(128)
    c[:, C_ID:C_ID + 128] = np.eye(128)
    c[:, C_HEAD:C_HEAD + HEADS] = (i[:, None] // DK) == np.arange(HEADS)[None]
    c[:, C_TRI:C_TRI + 128] = i[:, None] <= i[None]
    c[0:96, C_SEL:C_SEL + 32] = (i[:96, None] % 32) == np.arange(32)[None]
    c[0:48, C_SEL16:C_SEL16 + 16] = (i[:48, None] % 16) == np.arange(16)[None]
    c[0:24, C_SEL8:C_SEL8 + 8] = (i[:24, None] % 8) == np.arange(8)[None]
    m = c[:, C_DFT:].reshape(128, N_DFT, 128)
    h = i[None]
    for blk in range(2):
        n = (i + 128 * blk)[:, None]
        even, odd = 2 * np.pi * n * (2 * h) / 512, 2 * np.pi * n * (2 * h + 1) / 512
        m[:, FWD_RE_E + blk], m[:, FWD_RE_O + blk], m[:, FWD_IM_O + blk] = np.cos(even), np.cos(odd), -np.sin(odd)
        m[:, FWD_IM_E + blk] = -np.sin(even)
        m[:, FWD_IM_E + blk, 0] = (-1.0) ** n[:, 0]
        m[:, INV_RE_E + blk], m[:, INV_IM_E + blk] = 2 / 512 * np.cos(even).T, -2 / 512 * np.sin(even).T
        m[0, INV_RE_E + blk] = 1 / 512
        m[0, INV_IM_E + blk] = (-1.0) ** n[:, 0] / 512
        m[:, INV_RE_O + blk], m[:, INV_IM_O + blk] = 2 / 512 * np.cos(odd).T, -2 / 512 * np.sin(odd).T
    m[:, W_IM_E] = m[:, FWD_IM_E]
    m[:, W_IM_E, 0] = 0
    m[:, W_RE_E2] = m[:, FWD_RE_E]
    m[:, W_RE_E2, 0] = (-1.0) ** i
    return c.astype(np.float32)


class Chain:

    def __init__(self, eng, sem):
        self.eng, self.sem, self.n = eng, sem, 0

    def link(self, ins):
        self.n += 1
        ins.then_inc(self.sem, 1)
        self.eng.wait_ge(self.sem, self.n)


def build(nc, a, out, stages=8):
    with ExitStack() as ctx:
        def sb(name, shape, dt=F32):
            return ctx.enter_context(nc.sbuf_tensor(name, shape, dt))

        def sem(name):
            return ctx.enter_context(nc.semaphore(name))

        psum = ctx.enter_context(nc.psum_tensor("psum", [128, 8, 512], F32))
        bank = [psum[:, i, :] for i in range(8)]
        G, U, W, ACC, T = bank[0:2], bank[2:4], bank[4:6], bank[6], bank[7]

        const = sb("const", [128, C_ALL])
        ident = const[:, C_ID:C_ID + 128]
        headmask = const[:, C_HEAD:C_HEAD + HEADS]
        dft = const[:, C_DFT:].rearrange("p (m h) -> p m h", m=N_DFT)
        ident_bf = sb("ident_bf", [128, 128], BF16)
        tri_bf = sb("tri_bf", [128, 128], BF16)
        ones_bf = sb("ones_bf", [128, 128], BF16)
        ones_row = sb("ones_row", [1, 128])
        pair_sel = sb("pair_sel", [96, 32, 64], mybir.dt.float8e4)
        sel16 = sb("sel16", [48, 16], BF16)
        sel8 = sb("sel8", [24, 8], BF16)
        neghalf = sb("neghalf", [128, TB])
        x = sb("x", [128, B * TB, D])
        xn = sb("xn", [128, B * TB, D])
        xt = sb("xt", [128, 2, S])
        xt_hi = sb("xt_hi", [128, 2, S], F32R)
        xt_lo = sb("xt_lo", [128, 2, S], F32R)
        wa_hi = sb("wa_hi", [128, 51, 128], F32R)
        wa_lo = sb("wa_lo", [128, 51, 128], F32R)
        wb_hi = sb("wb_hi", [128, 64, 128], F32R)
        wb_lo = sb("wb_lo", [128, 64, 128], F32R)
        stage = sb("stage", [128, 2, 512])
        hb = sb("hb", [128, 4, 512])
        h_hi = sb("h_hi", [128, 2, 512], F32R)
        h_lo = sb("h_lo", [128, 2, 512], F32R)
        comb_t = sb("comb_t", [96, 2, S], BF16)
        wk = sb("wk", [128, 6, 512])
        g_all = sb("g_all", [128, 8])
        tg = sb("tg", [128, 8])
        rb = sb("rb", [128, 80])
        rw = sb("rw", [128, 88])
        rw_hi = sb("rw_hi", [128, 88], F32R)
        rw_lo = sb("rw_lo", [128, 88], F32R)
        bfc = sb("bfc", [128, 32])
        bproj_bf = sb("bproj_bf", [24, 3, 128], BF16)
        sw_nat = sb("sw_nat", [128, 3, 128])
        bcol = sb("bcol", [128, 9])
        bo = sb("bo", [1, 3, 128])
        m3 = sb("m3", [128, B, 32])
        v3 = sb("v3", [32, B, 128])
        crow = sb("crow", [1, 128])
        kmod = sb("kmod", [128, B])
        ctx_mean = sb("ctx_mean", [128, B])
        w2conv = sb("w2conv", [128, 128])
        mask_i = sb("mask_i", [128, TB, KEYS], I32)
        mask_add = sb("mask_add", [128, TB, KEYS], BF16)
        anykeep = sb("anykeep", [128, TB])
        stats = sb("stats", [128, TB, 6])
        mv = sb("mv", [128, TB, 2])
        veps = sb("veps", [128, TB])
        rstd = sb("rstd", [128, TB])
        mx = sb("mx", [128, 16])
        zsum = sb("zsum", [128, 16])
        bq0s = sb("bq0s", [128, 1])
        sm = sb("sm", [128, 16])
        sm1 = sb("sm1", [128, 16])
        rt = sb("rt", [128, TB, 32])
        ch = sb("ch", [128, TB, 38])
        mr = sb("mr", [128, TB, 38])
        t8 = sb("t8", [128, TB, 8])
        chosen = sb("chosen", [128, 256])
        tour = chosen[:, :].rearrange("p (g j) -> p g j", g=16)
        gp = sb("gp", [128, TB, 10])
        gr = sb("gr", [128, TB, 10])
        gm = sb("gm", [128, TB, 4])
        selm = chosen[:, 0:128].rearrange("p (k e) -> p k e", k=TB)
        wsel = chosen[:, 128:256].rearrange("p (k e) -> p k e", k=TB)
        wsum = sb("wsum", [128, TB])
        wrec = sb("wrec", [128, TB])
        chl = sb("chl", [128, TB, 96], BF16)
        sel_bf = sb("sel_bf", [128, TB, 32], BF16)
        run_bf = sb("run_bf", [128, TB, 32], BF16)
        run = sb("run", [128, TB + 1, 32])

        d_const, d_dft, d_small, d_wnat, d_out = [sem(n) for n in ("d_const", "d_dft", "d_small", "d_wnat", "d_out")]
        d_x = [sem(f"d_x{b}") for b in range(B)]
        d_stage = [sem(f"d_stage{i}") for i in range(2)]
        names = """pool_set sel_set prep_ps prep_sb prep_act veps_set rstd_set ln_done xt_ps xhi_done xlo_done
            xf_done logits_ps score_done cum_need cum_ps comb_done combt_ps combt_done T_free g_done u_done sg_done
            h_done hhi_done hlo_done down_done outt_done outt_ps x_done dve act pool s_ps s_sub s_exp s_prob
            p_ps p_sb pv_ps l0w_ps l0w_hi l0w_lo stage_used mexp_max kbd_done m1_ps m1_sb fft_in fft_ps w_ps w_sb
            prod_done z_proj z_s z_max z_exp z_tr z_pt z_pp z_pv z_up inv_ps o_sb dw_done dwt_ps dwt_sb bf_done sw_done rsm_sub rsm_exp""".split()
        q = {n: sem(n) for n in names}

        wnat = wk[:, 0:3, :].rearrange("p a (m d) -> p (a m) d", m=4)
        wk_flat = wk[:, :, :].rearrange("p a c -> p (a c)")
        KEYS0 = KEYS + S
        p0 = [wk_flat[:, 0:544], wk_flat[:, 544:1088]]
        pt0 = [wk_flat[:, 1088:1600], wk_flat[:, 1600:2112]]
        ptc0 = [wk_flat[0:KEYS, 2112:2240], wk_flat[0:KEYS, 2240:2368]]
        w0t = xt[:, 0, :].rearrange("p (m d) -> p m d", m=4)
        w1t = xt[:, 1, :].rearrange("p (m d) -> p m d", m=4)
        w3t = wk[:, 5, 0:384].rearrange("p (m d) -> p m d", m=3)
        ctxt = hb[:, 0, 0:128]
        kv3 = hb[:, 1, 0:256].rearrange("p (m c) -> p m c", m=2)
        ctx_nat = hb[:, 2, 0:128]
        kpw_nat = hb[:, 3, 0:128]

        xn4 = xn[:, :, :].rearrange("p (m k) d -> p m (k d)", m=4)

        lora_a, lora_bt = xn[0:R, 0:4, :], xn[0:R, 4:8, :]
        lora_b = xn[:, 8, 0:4 * R].rearrange("p (m r) -> p m r", m=4)
        rw_nat, bfc_nat = xn[0:32, 9:12, :], xn[0:32, 12, :]
        brow = xn[0:9, 13, :]
        small_bf = xn[:, 14:16, :].rearrange("p a b -> p (a b)").bitcast(BF16)
        sw_bf = small_bf[:, 0:384].rearrange("p (m d) -> p m d", m=3)
        gw2_bf = small_bf[0:32, 384:512]
        bproj = wk[0:24, 5, 384:512]
        early = const[:, C_DFT:]
        v0c = early[0:KEYS, 0:512].rearrange("p (b d) -> p b d", b=B)
        w0 = early[:, 1792:2304].rearrange("p (m d) -> p m d", m=4)
        ctx0 = early[:, 512:640]
        v0row = early[0:1, 640:768]
        crow1 = early[0:1, 768:1280]
        wq1, wo1t = early[:, 1280:1408], early[:, 1408:1536]
        kt1 = early[:, 1536:1792].rearrange("p (m c) -> p m c", m=2)

        def cols4(t):
            return t[:, :].rearrange("p (k c) -> p k c", k=4)

        def quads_l0():
            r = []
            for base, w in ((0, a["L0_ffn_expert_gate"]), (16, a["L0_ffn_expert_up"])):
                v = w.rearrange("(c e) i d -> (e i) c d", e=2)
                r += [(v[:, 4 * k:4 * k + 4, :], base + 4 * k, 4) for k in range(4)]
            v = a["L0_ffn_expert_down"].rearrange("e d i -> d e i")
            r += [(v[:, 8 * k:8 * k + 8, :], 32 + 4 * k, 4) for k in range(4)]
            return r

        QL0 = quads_l0()
        NQ0 = len(QL0) + 1

        def quads_nat(layer):
            r = []
            if layer == 1:
                fc = a["L1_ffn_w_fc"]
                pr = a["L1_ffn_w_proj"].rearrange("e (c h) d -> e h c d", c=4)
                for e in range(8):
                    r += [(fc[e], 4 * e, 4), (pr[e], 32 + 4 * e, 4)]
            if layer == 3:
                for base, w in ((0, "routed_w1"), (20, "routed_w2"), (40, "routed_w3")):
                    v = a["L3_ffn_" + w].rearrange("e d h -> d e h")
                    r += [(v[:, 4 * k:4 * k + 4, :], base + 4 * k, 4) for k in range(4)]
                r += [(a["L3_ffn_shared_w1"][0], 16, 4), (a["L3_ffn_shared_w2"][0], 36, 4),
                      (a["L3_ffn_shared_w3"][0].rearrange("(c h) d -> h c d", c=4), 56, 4)]
            if layer == 2:
                for base, w in ((0, "W1"), (16, "W3")):
                    v = a["L2_ffn_" + w].rearrange("e d i -> d e i")
                    r += [(v[:, 8 * k:8 * k + 8, :], base + 4 * k, 4) for k in range(4)]
                v = a["L2_ffn_W2"].rearrange("(c e) i d -> (e i) c d", e=2)
                r += [(v[:, 4 * k:4 * k + 4, :], 32 + 4 * k, 4) for k in range(4)]
            return r

        QN = {l: quads_nat(l) for l in (1, 2, 3)}
        QBASE = {1: NQ0, 2: NQ0 + len(QN[1]), 3: NQ0 + len(QN[1]) + len(QN[2])}
        NQ = QBASE[3] + len(QN[3])

        def slots(layer, c):
            if layer == 0:
                return (c, 16 + c, 32 + c) if c < 16 else (48, 49, 50)
            if layer == 1:
                return c, None, 32 + c
            if layer == 2:
                return (c, 16 + c, 32 + c) if c < 16 else (48, 49, 50)
            return c, 20 + c, 40 + c

        block = ctx.enter_context(nc.Block())

        def loaded(r):
            return sum(48 if k == NQ0 - 1 else 16 for k in range(r % 2, r + 1, 2))

        def quad(r):
            if r < NQ0 - 1:
                return QL0[r][1], QL0[r][2], 0
            if r == NQ0 - 1:
                return 48, 3, 0
            layer = 1 if r < QBASE[2] else 2 if r < QBASE[3] else 3
            return QN[layer][r - QBASE[layer]][1:] + (layer,)

        @block.sync
        def _(sp):
            sp.dma_start(const[:, 0:C_DFT], a["consts"][:, 0:C_DFT]).then_inc(d_const, 16)
            sp.dma_start(ctx_nat, a["ctx_1024"].rearrange("b t d -> (b t) d")).then_inc(d_wnat, 16)
            for i, n in enumerate([f"L{l}_xattn_W{w}" for l in (0, 1, 3) for w in "qkvo"]):
                dst = wq1[:, :] if n == "L1_xattn_Wq" else w0t[:, 2, :] if n == "L0_xattn_Wv" else wnat[:, i, :]
                sp.dma_start(dst, a[n]).then_inc(d_wnat, 16)
            sp.dma_start(kpw_nat, a["L2_xattn_kp_w"]).then_inc(d_wnat, 16)
            for b in range(B):
                sp.dma_start(x[:, TB * b:TB * b + TB, :], a["x"][b].rearrange("(k p) d -> p k d", p=128)).then_inc(d_x[b], 16)
            for r in range(NQ):
                if r == QBASE[2]:
                    sp.wait_ge(q["x_done"], min(12, 4 * stages))
                    sp.dma_start(dft, a["consts"][:, C_DFT:].rearrange("p (m h) -> p m h", m=N_DFT)).then_inc(d_dft, 16)
                if r >= 2:
                    sp.wait_ge(q["stage_used"], r - 1)
                dst = stage[:, r % 2, :]
                if r == NQ0 - 1:
                    for i, w in enumerate(("gate", "up", "down")):
                        sp.dma_start(dst[:, 128 * i:128 * i + 128], a["L0_ffn_shared_" + w]).then_inc(d_stage[r % 2], 16)
                    continue
                layer = quad(r)[2]
                if layer == 2:
                    dst = dst.bitcast(BF16)[:, 0:512]
                src = QL0[r][0] if layer == 0 else QN[layer][r - QBASE[layer]][0]
                if len(src.shape) == 3:
                    dst = dst.rearrange("p (c i) -> p c i", c=src.shape[1])
                sp.dma_start(dst, src).then_inc(d_stage[r % 2], 16)
            for b in range(B):
                sp.wait_ge(q["x_done"], 20 if stages == 5 else 4 * (stages - 1) + b + 1)
                sp.dma_start(out[b].rearrange("(k p) d -> p k d", p=128), x[:, TB * b:TB * b + TB, :]).then_inc(d_out, 16)
            sp.wait_ge(d_out, 16 * B)

        SMALL = [(g_all[:, 0:4], a["g_xattn"].rearrange("(o n) -> o n", o=1).broadcast_to([128, 4])),
                 (g_all[:, 4:8], a["g_ffn"].rearrange("(o n) -> o n", o=1).broadcast_to([128, 4])),
                 (rb[:, 0:32], a["L0_ffn_gate_bias"].rearrange("(o n) -> o n", o=1).broadcast_to([128, 32])),
                 (rb[:, 32:64], a["L2_ffn_bias"].rearrange("(o n) -> o n", o=1).broadcast_to([128, 32])),
                 (rb[:, 64:80], a["L3_ffn_expert_bias"].rearrange("(o n) -> o n", o=1).broadcast_to([128, 16])),
                 (rw_nat[0:32, 0, :], a["L0_ffn_gate_w"]),
                 (rw_nat[0:8, 1, :], a["L1_ffn_router_w"]),
                 (gw2_bf[:, :], a["L2_ffn_gate_w"]),
                 (rw[:, 72:88], a["L3_ffn_router_w"]),
                 (bfc_nat, a["L1_ffn_b_fc"].rearrange("e (c h) -> (e c) h", c=4)),
                 (bproj[0:8, :], a["L1_ffn_b_proj"]),
                 (bproj[8:16, :], a["L1_ffn_b_proj"]),
                 (bproj[16:24, :], a["L1_ffn_b_proj"]),
                 (sw_bf[0:64, 0, :], a["L2_ffn_sw1"]),
                 (sw_bf[0:64, 1, :], a["L2_ffn_sw3"]),
                 (sw_bf[:, 2, 0:64], a["L2_ffn_sw2"]),
                 (w2conv[:, :], a["L2_xattn_weight"]),
                 (mask_i[:, :, :], a["mask_1x1xSxS2_ik0"].rearrange("u v (k p) t -> p (u v k) t", p=128))]
        for i, n in enumerate(("L0_xattn_bq", "L0_xattn_bk", "L0_xattn_bv", "L1_xattn_bq", "L1_xattn_bk", "L1_xattn_bv",
                               "L3_xattn_bq", "L3_xattn_bv", "L2_xattn_kp_b")):
            SMALL.append((brow[i:i + 1, :], a[n].rearrange("(o n) -> o n", o=1)))
        for i, l in enumerate((0, 1, 3)):
            SMALL.append((bo[0:1, i, :], a[f"L{l}_xattn_bo"].rearrange("(o n) -> o n", o=1)))
        for i, w in enumerate("qkvo"):
            SMALL.append((lora_a[:, i, :], a["L0_xattn_A" + w]))
            SMALL.append((lora_b[:, i, :], a["L0_xattn_B" + w]))
        N_SMALL = 16 * len(SMALL)

        @block.gpsimd
        def _(pool):
            pool.memset(neghalf[:, :], -0.5).then_inc(q["pool_set"], 1)
            pool.memset(ones_row[:, :], 1.0).then_inc(q["pool_set"], 1)
            pool.memset(ones_bf[:, :], 1.0).then_inc(q["pool_set"], 1)
            pool.memset(sw_nat[:, :, :], 0.0).then_inc(q["pool_set"], 1)
            pool.memset(gp[:, :, 4:10], LOW).then_inc(q["pool_set"], 1)
            pool.wait_ge(d_const, 16)
            pool.tensor_copy(ident_bf[:, :], ident).then_inc(q["pool_set"], 1)
            pool.tensor_copy(tri_bf[:, :], const[:, C_TRI:C_TRI + 128]).then_inc(q["pool_set"], 1)
            pool.tensor_copy(pair_sel[:, :, :], const[0:96, C_SEL:C_SEL + 32].unsqueeze(2).broadcast_to([96, 32, 64]),
                             saturate=False).then_inc(q["pool_set"], 1)
            pool.tensor_copy(sel16[:, :], const[0:48, C_SEL16:C_SEL16 + 16]).then_inc(q["pool_set"], 1)
            pool.tensor_copy(sel8[:, :], const[0:24, C_SEL8:C_SEL8 + 8]).then_inc(q["pool_set"], 1)
            pool.wait_ge(d_small, N_SMALL)
            pool.wait_ge(q["pool_set"], 4)
            pool.tensor_copy(sw_nat[0:64, 0:2, :], sw_bf[0:64, 0:2, :]).then_inc(q["pool_set"], 1)
            pool.tensor_copy(sw_nat[:, 2, 0:64], sw_bf[:, 2, 0:64]).then_inc(q["pool_set"], 1)
            pool.tensor_copy(rw_nat[:, 2, :], gw2_bf[:, :]).then_inc(q["pool_set"], 1)

            def rsqrt(n):
                pool.wait_ge(q["veps_set"], n + 1)
                pool.tensor_tensor(rstd[:, :], veps[:, :], neghalf[:, :], ALU.pow).then_inc(q["rstd_set"], 1)

            def split(r):
                slot, n, layer = quad(r)
                pool.wait_ge(d_stage[r % 2], loaded(r))
                if layer == 2:
                    src = stage[:, r % 2, :].bitcast(BF16)[:, 0:512].rearrange("p (c h) -> p c h", c=4)
                    pool.tensor_copy(wa_hi[:, slot:slot + 4, :], src).then_inc(q["stage_used"], 1)
                    return
                src = stage[:, r % 2, :].rearrange("p (c h) -> p c h", c=4)
                pool.tensor_copy(wb_hi[:, slot:slot + 4, :], src).then_inc(q["pool"], 1)
                split.n += 1
                pool.wait_ge(q["pool"], split.n)
                pool.tensor_tensor(wb_lo[:, slot:slot + 4, :], src, wb_hi[:, slot:slot + 4, :].bitcast(F32),
                                   ALU.subtract).then_inc(q["stage_used"], 1)
            split.n = 0

            def kbd(b):
                if b >= 1:
                    pool.wait_ge(q["m1_ps"], 3 * b)
                for j in range(2):
                    src = kt1[:, j, KEYS * b:KEYS * b + KEYS].unsqueeze(1).broadcast_to([128, HEADS, KEYS])
                    hm = headmask.unsqueeze(2).broadcast_to([128, HEADS, KEYS])
                    pool.tensor_tensor(hb[:, j, :].rearrange("p (h t) -> p h t", h=HEADS), src, hm,
                                       ALU.mult).then_inc(q["kbd_done"], 1)

            when = {1: 1, 2: 3, 3: 5}
            for s in range(stages):
                for b in range(B):
                    rsqrt(4 * s + b)
                    for layer, at in when.items():
                        if s == at:
                            n = -(-len(QN[layer]) // B)
                            if b == 0 and layer == 2:
                                pool.wait_ge(q["x_done"], 8)
                            if b == 0 and layer == 3:
                                pool.wait_ge(q["x_done"], 16)
                            if b == 0 and layer == 2:
                                pool.wait_ge(q["prep_sb"], 9)
                                pool.tensor_copy(wa_hi[:, 48:51, :], sw_nat[:, :, :])
                            for r in range(n * b, min(n * b + n, len(QN[layer]))):
                                split(QBASE[layer] + r)
                if s == 2:
                    for b in range(B):
                        kbd(b)
            for layer, at in when.items():
                if at >= stages:
                    for r in range(QBASE[layer], QBASE[layer] + len(QN[layer])):
                        split(r)

        def tnum(s, b):
            return 4 * TRANSPOSED[s] + b + 1

        def fnum(l, b):
            return 4 * l + b + 1

        def knum(l, b, c):
            return CB[l] + b * NC[l] + c

        def softmax_num(l, b):
            return b if l == 1 else 16 + b

        KW = {3: KEYS}

        @block.scalar
        def _(act):
            for dst, src in SMALL:
                act.dma_start(dst, src).then_inc(d_small, 16)
            act.wait_ge(d_small, N_SMALL)
            act.activation(tg[:, :], g_all[:, :], ACT.Tanh).then_inc(q["act"], 1)
            act.wait_ge(q["prep_sb"], 9)
            act.activation(rw_hi[:, :], rw[:, :], ACT.Copy).then_inc(q["prep_act"], 1)

            def weights0(r):
                act.wait_ge(q["l0w_ps"], r + 1)
                slot, n, _ = quad(r)
                act.activation(wa_hi[:, slot:slot + n, :], cols4(W[r % 2])[:, 0:n, :], ACT.Copy).then_inc(q["l0w_hi"], 1)

            def xf(s, b):
                act.wait_ge(q["xt_ps"], tnum(s, b))
                act.activation(xt[:, b % 2, :], T[:, :], ACT.Copy).then_inc(q["T_free"], 1)

            def softmax_exp(l, b):
                i = softmax_num(l, b)
                n = KW[l] * TB if l in KW else 512
                act.wait_ge(q["s_sub"], i + 1)
                act.activation(wk[:, 2 + b % 2, 0:n], wk[:, b % 2, 0:n], ACT.Exp).then_inc(q["s_exp"], 1)

            def prob_t(l, b):
                i = softmax_num(l, b)
                act.wait_ge(q["p_ps"], i + 1)
                if i >= 2:
                    act.wait_ge(q["pv_ps"], i - 1)
                rows = KW[l] if l in KW else 128
                src = U[b % 2] if l in KW else W[b % 2]
                act.activation(wk[0:rows, 4 + b % 2, :], src[0:rows, :], ACT.Copy).then_inc(q["p_sb"], 1)

            def m1(b):
                sc = DK ** -0.5
                act.wait_ge(q["m1_ps"], 3 * b + 1)
                if b >= 1:
                    act.wait_ge(q["s_ps"], 4 * b)
                act.activation(hb[:, 2, :], T[:, :], ACT.Copy, scale=sc).then_inc(q["m1_sb"], 1)
                act.wait_ge(q["m1_ps"], 3 * b + 2)
                act.activation(crow1[:, :], T[0:1, :], ACT.Copy, scale=sc).then_inc(q["m1_sb"], 1)

            def v1(b):
                act.wait_ge(q["m1_ps"], 3 * b + 3)
                if b >= 1:
                    act.wait_ge(q["pv_ps"], 4 * b)
                act.activation(hb[:, 3, :], T[:, :], ACT.Copy).then_inc(q["m1_sb"], 1)

            def pre_x(l, b):
                s = 2 * l + 1
                act.wait_ge(q["xt_ps"], tnum(s, b))
                act.activation(xt_hi[:, b % 2, :], T[:, :], ACT.Copy).then_inc(q["xhi_done"], 1)

            def pre_score(l, b):
                act.wait_ge(q["logits_ps"], fnum(l, b))
                E = N_EXP[l]
                src = T[:, 0:TB * E].rearrange("p (k e) -> p k e", k=TB)
                if l == 1:
                    act.wait_ge(q["rsm_sub"], b + 1)
                    act.activation(rt[:, :, 0:E], rt[:, :, 0:E], ACT.Exp).then_inc(q["score_done"], 1)
                else:
                    act.activation(rt[:, :, 0:E], src, ACT.Sigmoid).then_inc(q["score_done"], 1)

            def pre_comb(l, b):
                rows = 3 * N_EXP[l]
                act.wait_ge(q["combt_ps"], fnum(l, b))
                act.activation(comb_t[0:rows, b % 2, :], T[:, :].bitcast(BF16)[0:rows, 0:S], ACT.Copy).then_inc(q["combt_done"], 1)

            def unit(l, b, c):
                k = knum(l, b, c)
                act.wait_ge(q["g_done"], k + 1)
                if k >= 4:
                    act.wait_ge(q["hlo_done"], k - 3)
                if l == 1:
                    act.activation(hb[:, k % 4, :], bank[k % 4][:, :], ACT.Gelu_apprx_tanh,
                                   bias=bfc[:, c:c + 1]).then_inc(q["sg_done"], 1)
                else:
                    act.activation(hb[:, k % 4, :], G[k % 2][:, :], ACT.Silu).then_inc(q["sg_done"], 1)

            def high(l, b, c):
                k = knum(l, b, c)
                act.wait_ge(q["h_done"], k + 1)
                if k >= 2:
                    act.wait_ge(q["down_done"], k - 1)
                act.activation(h_hi[:, k % 2, :], hb[:, k % 4, :], ACT.Copy).then_inc(q["hhi_done"], 1)

            def out_t(l, b):
                act.wait_ge(q["down_done"], knum(l, b, NC[l] - 1) + 1)
                act.activation(xt[:, b % 2, :], ACC[:, :], ACT.Copy).then_inc(q["outt_done"], 1)

            act.wait_ge(q["act"], 1)
            for r in range(NQ0):
                weights0(r)

            def project_out(b, j):
                act.wait_ge(q["z_proj"], 3 * b + j + 1)
                if j == 0:
                    ins = act.activation(hb[:, 2 * (b % 2), :], T[:, :], ACT.Identity, bias=bq0s[:, 0:1], scale=D ** -0.5)
                elif j == 1:
                    ins = act.activation(hb[:, 2 * (b % 2) + 1, :], T[:, :], ACT.Identity, bias=bcol[:, 1:2])
                else:
                    ins = act.activation(xt[:, b % 2, :], T[:, :], ACT.Copy)
                ins.then_inc(q["T_free"], 1)

            def exp0(i):
                act.wait_ge(q["z_max"], i + 1)
                if i >= 2:
                    act.wait_ge(q["z_tr"], i - 1)
                act.activation(p0[i % 2].rearrange("p (a n) -> p a n", a=2), psum[:, 2 * (i % 2):2 * (i % 2) + 2, 0:KEYS0 // 2],
                               ACT.Exp, bias=mx[:, i:i + 1], accum_out=zsum[:, i:i + 1]).then_inc(q["z_exp"], 1)

            def context_out(i):
                act.wait_ge(q["z_tr"], i + 1)
                if i >= 2:
                    act.wait_ge(q["z_pv"], i - 1)
                act.activation(ptc0[i % 2], bank[2 * (i % 2)][0:KEYS, 384:512], ACT.Copy).then_inc(q["z_pp"], 1)

            for s in range(stages):
                l = s // 2
                if s == 0:
                    xf(0, 0)
                    for j in range(3):
                        project_out(0, j)
                    exp0(0)
                    for i in range(16):
                        if i < 15:
                            exp0(i + 1)
                        context_out(i)
                        if i < 12:
                            if i % 4 == 0:
                                xf(0, i // 4 + 1)
                            else:
                                project_out(i // 4 + 1, i % 4 - 1)
                elif s % 2 == 0 and l in KW:
                    xf(s, 0)
                    xf(s, 1)
                    for b in range(B + 1):
                        if b < B:
                            softmax_exp(l, b)
                        if b >= 1:
                            prob_t(l, b - 1)
                        if b + 2 < B and b + 2 >= 2:
                            act.wait_ge(q["s_ps"], softmax_num(l, b) + 1)
                            xf(s, b + 2)
                elif s == 2:
                    for i in range(4 * B + 2):
                        if i % 4 == 0 and i < 16:
                            m1(i // 4)
                            if i >= 8:
                                act.wait_ge(q["s_ps"], i - 4)
                            xf(s, i // 4)
                        if i < 16:
                            softmax_exp(1, i)
                        if 1 <= i <= 16:
                            prob_t(1, i - 1)
                        if i % 4 == 0 and i < 16:
                            v1(i // 4)
                elif s == 4:
                    act.wait_ge(q["dwt_ps"], 1)
                    act.activation(xt[:, 1, :], bank[0][:, :], ACT.Copy).then_inc(q["dwt_sb"], 1)
                    for i in range(5):
                        act.wait_ge(q["w_ps"], i + 1)
                        act.activation(wk[:, i, :], bank[1 + i][:, :], ACT.Copy).then_inc(q["w_sb"], 1)
                    for i in range(2):
                        act.wait_ge(q["inv_ps"], i + 1)
                        act.activation(xt[:, i, :], bank[6 + i][:, :], ACT.Copy, scale=tg[:, 2:3]).then_inc(q["o_sb"], 1)
                else:
                    pre_x(l, 0)
                    pre_score(l, 0)
                    pre_comb(l, 0)
                    for b in range(B):
                        for c in range(NC[l]):
                            unit(l, b, c)
                            k = b * NC[l] + c
                            if k >= 1:
                                pb, pc = divmod(k - 1, NC[l])
                                high(l, pb, pc)
                            if c == 1 and b >= 1:
                                out_t(l, b - 1)
                            if b + 1 < B:
                                if c == 5:
                                    pre_x(l, b + 1)
                                if c == 9:
                                    pre_score(l, b + 1)
                                if c == 14:
                                    pre_comb(l, b + 1)
                    high(l, B - 1, NC[l] - 1)
                    out_t(l, B - 1)

        @block.tensor
        def _(pe):
            t_uses = [0]

            def use_t():
                if t_uses[0]:
                    pe.wait_ge(q["T_free"], t_uses[0])
                t_uses[0] += 1

            def mm(o, l, r, start, stop):
                return pe.matmul(o, l, r, start=start, stop=stop, skip_group_check=True)

            pe.wait_ge(d_const, 16)
            pe.wait_ge(q["pool_set"], 13)
            pe.wait_ge(d_wnat, 16 * 14)
            pe.wait_ge(d_small, N_SMALL)
            b0, b1, b2, b3, b4, b5 = [bank[i] for i in range(6)]
            for j, src in enumerate((wnat[:, 0, :], wnat[:, 1, :], ctx_nat, wnat[:, 3, :])):
                last = pe.transpose(b0[:, 128 * j:128 * j + 128], src, ident)
            last.then_inc(q["prep_ps"], 1)
            for j, src in enumerate((wnat[:, 5, :], wnat[:, 6, :], wnat[:, 7, :], kpw_nat)):
                last = pe.transpose(b1[:, 128 * j:128 * j + 128], src, ident)
            last.then_inc(q["prep_ps"], 1)
            for j in range(3):
                last = pe.transpose(b2[:, 128 * j:128 * j + 128], wnat[:, 9 + j, :], ident)
            last.then_inc(q["prep_ps"], 1)
            for j in range(4):
                last = pe.transpose(b3[0:R, 128 * j:128 * j + 128], lora_b[:, j, :], ident)
            last.then_inc(q["prep_ps"], 1)
            pe.transpose(b4[:, 0:32], rw_nat[0:32, 0, :], ident[0:32, 0:32])
            pe.transpose(b4[:, 32:40], rw_nat[0:8, 1, :], ident[0:8, 0:8])
            pe.transpose(b4[:, 40:72], rw_nat[0:32, 2, :], ident[0:32, 0:32])
            pe.transpose(b4[:, 128:160], bfc_nat[:, :], ident[0:32, 0:32])
            pe.transpose(b4[:, 160:169], brow[:, :], ident[0:9, 0:9]).then_inc(q["prep_ps"], 1)
            for j in range(3):
                last = pe.transpose(b5[:, 128 * j:128 * j + 128], sw_nat[:, j, :], ident)
            last.then_inc(q["prep_ps"], 1)
            pe.wait_ge(q["prep_sb"], 4)
            for j in range(4):
                l, r = (lora_bt, lora_a) if j == 2 else (lora_a, lora_bt)
                last = mm(bank[6][:, 128 * j:128 * j + 128], l[:, j, :], r[:, j, :], True, True)
            last.then_inc(q["prep_ps"], 1)
            pe.wait_ge(q["prep_sb"], 10)
            mm(bank[7][:, 0:128], w0[:, 2, :], w0[:, 3, :], True, True)
            mm(bank[7][0:1, 128:256], bcol[:, 2:3], w0[:, 3, :], True, True)
            mm(bank[7][:, 256:384], w1t[:, 0, :], ctxt, True, True)
            mm(bank[7][:, 384:512], w1t[:, 1, :], ctxt, True, True).then_inc(q["prep_ps"], 1)
            mm(b0[:, 0:128], w3t[:, 0, :], ctxt, True, True)
            mm(b0[:, 128:256], w3t[:, 1, :], ctxt, True, True)
            mm(b0[:, 256:260], w1t[:, 3, :], ctx_mean[:, :], True, True).then_inc(q["prep_ps"], 1)
            pe.wait_ge(q["prep_sb"], 19)
            mm(b1[:, 256:384], wnat[:, 8, :], kv3[:, 0, :], True, True).then_inc(q["prep_ps"], 1)
            mm(b2[0:1, 256:384], bcol[:, 6:7], kv3[:, 0, :], True, True).then_inc(q["prep_ps"], 1)
            for b in range(B):
                mm(b3[0:KEYS, 128 * b:128 * b + 128], ctxt[:, KEYS * b:KEYS * b + KEYS], w0[:, 3, :], True, False)
                last = mm(b3[0:KEYS, 128 * b:128 * b + 128], ones_row[:, 0:KEYS], bo[:, 0, :], False, True)
            last.then_inc(q["prep_ps"], 1)
            for b in range(B):
                o = b4[0:KEYS, 128 * b:128 * b + 128]
                mm(o, kv3[:, 1, KEYS * b:KEYS * b + KEYS], w3t[:, 2, :], True, False)
                last = mm(o, ones_row[:, 0:KEYS], bo[:, 2, :], False, True)
            last.then_inc(q["prep_ps"], 1)
            pe.wait_ge(q["prep_sb"], 23)

            for r in range(NQ0):
                pe.wait_ge(d_stage[r % 2], loaded(r))
                if r >= 2:
                    pe.wait_ge(q["l0w_lo"], r - 1)
                for j in range(quad(r)[1]):
                    last = pe.transpose(W[r % 2][:, 128 * j:128 * j + 128], stage[:, r % 2, 128 * j:128 * j + 128], ident)
                last.then_inc(q["l0w_ps"], 1)
            pe.wait_ge(q["l0w_lo"], NQ0)

            def xt_in(s, b):
                pe.wait_ge(q["ln_done"], 4 * s + b + 1)
                use_t()
                for k in range(TB):
                    last = pe.transpose(T[:, 128 * k:128 * k + 128], xn[:, TB * b + k, :], ident)
                last.then_inc(q["xt_ps"], 1)

            xf_base = {}

            def scores(l, b):
                n = KW[l]
                mat = m3
                row = crow[:, 32 * b:32 + 32 * b]
                pe.wait_ge(q["T_free"], xf_base[(2 * l, b)])
                if b >= 2:
                    pe.wait_ge(q["s_sub"], softmax_num(l, b) - 1)
                mm(G[b % 2][:, 0:TB * n].rearrange("p (k n) -> p k n", k=TB), ones_row[:, :],
                   row.unsqueeze(1).broadcast_to([1, TB, n]), True, False)
                for k in range(TB):
                    last = mm(G[b % 2][:, n * k:n * k + n], xt[:, b % 2, 128 * k:128 * k + 128], mat[:, b, :], False, k == TB - 1)
                last.then_inc(q["s_ps"], 1)

            def probs_t(l, b):
                n = KW[l]
                pe.wait_ge(q["s_prob"], softmax_num(l, b) + 1)
                if b >= 2:
                    pe.wait_ge(q["p_sb"], softmax_num(l, b) - 1)
                for k in range(TB):
                    last = pe.transpose(U[b % 2][0:n, 128 * k:128 * k + 128], wk[:, 2 + b % 2, n * k:n * k + n], ident)
                last.then_inc(q["p_ps"], 1)

            def values(l, b):
                n = KW[l]
                i = softmax_num(l, b)
                pe.wait_ge(q["p_sb"], i + 1)
                if b >= 2:
                    pe.wait_ge(q["x_done"], 4 * (2 * l) + b - 1)
                v = v3
                for k in range(TB):
                    last = mm(W[b % 2][:, 128 * k:128 * k + 128], wk[0:n, 4 + b % 2, 128 * k:128 * k + 128], v[:, b, :], True, True)
                last.then_inc(q["pv_ps"], 1)

            def m1(b):
                pe.wait_ge(q["kbd_done"], 2 * b + 2)
                use_t()
                mm(T[:, :], wq1[:, :], hb[:, 0, :], True, True).then_inc(q["m1_ps"], 1)
                pe.wait_ge(q["m1_sb"], 3 * b + 1)
                mm(T[0:1, :], bcol[:, 3:4], hb[:, 0, :], True, True).then_inc(q["m1_ps"], 1)
                pe.wait_ge(q["m1_sb"], 3 * b + 2)
                t_uses[0] -= 1

            def v1(b):
                use_t()
                for j in range(4):
                    last = mm(T[:, 128 * j:128 * j + 128], hb[:, 1, 128 * j:128 * j + 128], wo1t[:, :], True, True)
                last.then_inc(q["m1_ps"], 1)
                pe.wait_ge(q["m1_sb"], 3 * b + 3)
                t_uses[0] -= 1

            def scores1(i):
                b, k = divmod(i, TB)
                if k == 0:
                    m1(b)
                    xt_in(2, b)
                    xf_base[(2, b)] = t_uses[0]
                    pe.wait_ge(q["T_free"], xf_base[(2, b)])
                o = bank[i % 4]
                if i >= 4:
                    pe.wait_ge(q["s_sub"], i - 3)
                mm(o[:, :], ones_row[:, :], crow1[:, :], True, False)
                mm(o[:, :].rearrange("p (h t) -> p h t", h=HEADS), ident_bf[:, :],
                   mask_add[:, k, :].unsqueeze(1).broadcast_to([128, HEADS, KEYS]), False, False)
                mm(o[:, :], xt[:, b % 2, 128 * k:128 * k + 128], hb[:, 2, :], False, True).then_inc(q["s_ps"], 1)

            def probs_t1(i):
                pe.wait_ge(q["s_prob"], i + 1)
                if i >= 2:
                    pe.wait_ge(q["p_sb"], i - 1)
                for j in range(4):
                    last = pe.transpose(W[i % 2][:, 128 * j:128 * j + 128], wk[:, 2 + i % 2, 128 * j:128 * j + 128], ident)
                last.then_inc(q["p_ps"], 1)

            def values1(i):
                b, k = divmod(i, TB)
                pe.wait_ge(q["p_sb"], i + 1)
                if k == 0 and b >= 1:
                    pe.wait_ge(q["x_done"], 8 + b)
                o = ACC[:, 128 * k:128 * k + 128]
                mm(o, ones_row[:, :], bo[:, 1, :], True, False)
                for j in range(4):
                    last = mm(o, wk[:, 4 + i % 2, 128 * j:128 * j + 128], hb[:, 3, 128 * j:128 * j + 128], False, j == 3)
                last.then_inc(q["pv_ps"], 1)

            def logits(l, b):
                pe.wait_ge(q["xlo_done"], fnum(l, b))
                use_t()
                E, off = N_EXP[l], (0, 32, 40, 72)[l]
                for k in range(TB):
                    o = T[:, E * k:E * k + E]
                    hi, lo = (t[:, b % 2, 128 * k:128 * k + 128] for t in (xt_hi, xt_lo))
                    rh, rl = rw_hi[:, off:off + E], rw_lo[:, off:off + E]
                    mm(o, lo, rl, True, False)
                    mm(o, lo, rh, False, False)
                    mm(o, hi, rl, False, False)
                    last = mm(o, hi, rh, False, True)
                last.then_inc(q["logits_ps"], 1)

            def running(b):
                pe.wait_ge(q["cum_need"], b + 1)
                use_t()
                o = T[:, 0:128].rearrange("p (k e) -> p k e", k=TB)
                mm(o, tri_bf[:, :], sel_bf[:, :, :], True, False)
                mm(o, ones_bf[:, :], run_bf[:, :, :], False, True).then_inc(q["cum_ps"], 1)

            def comb_in(l, b):
                rows = 3 * N_EXP[l]
                pe.wait_ge(q["comb_done"], fnum(l, b))
                use_t()
                for k in range(TB):
                    last = pe.transpose(T[:, :].bitcast(BF16)[0:rows, 128 * k:128 * k + 128], chl[:, k, 0:rows], ident_bf[:, :])
                last.then_inc(q["combt_ps"], 1)

            def gu(l, b, c):
                k = knum(l, b, c)
                gs, us, _ = slots(l, c)
                wh, wl = (wa_hi, wa_lo) if l in (0, 2) else (wb_hi, wb_lo)
                hi, lo = xt_hi[:, b % 2, :], xt_lo[:, b % 2, :]
                if c == 0:
                    pe.wait_ge(q["combt_done"], fnum(l, b))

                def product(o, s):
                    mm(o, wh[:, s, :], hi, True, False)
                    if l != 2:
                        mm(o, wl[:, s, :], hi, False, False)
                    return mm(o, wh[:, s, :], lo, False, True)

                if l == 1:
                    if k - CB[1] >= 4:
                        pe.wait_ge(q["sg_done"], k - 3)
                    product(bank[k % 4][:, :], gs).then_inc(q["g_done"], 1)
                    if c % 4 == 0:
                        e = k // 4
                        if k - CB[1] >= 8:
                            pe.wait_ge(q["h_done"], k - 4)
                        mm(W[e % 2][:, :], sel8[:, c // 4:c // 4 + 1].broadcast_to([24, 128]),
                           comb_t[0:24, b % 2, :], True, True).then_inc(q["u_done"], 1)
                    return
                if k - CB[l] >= 2:
                    pe.wait_ge(q["h_done"], k - 1)
                product(G[k % 2][:, :], gs).then_inc(q["g_done"], 1)
                last = product(U[k % 2][:, :], us)
                if c < ROUTED[l]:
                    if N_EXP[l] == 32:
                        pick = pair_sel[:, 2 * c:2 * c + 2, :].rearrange("p e i -> p (e i)")
                    else:
                        pick = sel16[:, c:c + 1].broadcast_to([48, 128])
                    last = mm(W[k % 2][:, :], pick, comb_t[0:3 * N_EXP[l], b % 2, :], True, True)
                last.then_inc(q["u_done"], 1)

            def down(l, b, c):
                k = knum(l, b, c)
                s = slots(l, c)[2]
                wh, wl = (wa_hi, wa_lo) if l in (0, 2) else (wb_hi, wb_lo)
                if c == 0:
                    if fnum(l, b) > 4 * l + 1:
                        pe.wait_ge(q["outt_done"], fnum(l, b) - 1)
                    if l == 1:
                        for j in range(3):
                            mm(ACC[:, :], bproj_bf[:, j, :], comb_t[0:24, b % 2, :], j == 0, False)
                pe.wait_ge(q["hlo_done"], k + 1)
                mm(ACC[:, :], wh[:, s, :], h_hi[:, k % 2, :], c == 0 and l != 1, False)
                if l != 2:
                    mm(ACC[:, :], wl[:, s, :], h_hi[:, k % 2, :], False, False)
                last = mm(ACC[:, :], wh[:, s, :], h_lo[:, k % 2, :], False, c == NC[l] - 1)
                last.then_inc(q["down_done"], 1)

            def out_back(l, b):
                pe.wait_ge(q["outt_done"], fnum(l, b))
                use_t()
                for k in range(TB):
                    last = pe.transpose(T[:, 128 * k:128 * k + 128], xt[:, b % 2, 128 * k:128 * k + 128], ident)
                last.then_inc(q["outt_ps"], 1)

            ready0 = {}

            def project(b, j):
                xb = xt[:, b % 2, :]
                use_t()
                if j < 2:
                    last = mm(T[:, :], w0[:, j, :], xb, True, True)
                else:
                    mm(cols4(T), ones_row[:, :], v0row.unsqueeze(1).broadcast_to([1, TB, 128]), True, False)
                    for k in range(TB):
                        last = mm(T[:, 128 * k:128 * k + 128], xb[:, 128 * k:128 * k + 128], w0[:, 2, :], False, k == TB - 1)
                last.then_inc(q["z_proj"], 1)
                ready0[(b, j)] = t_uses[0]

            def scores0(i):
                b, k = divmod(i, TB)
                pe.wait_ge(q["T_free"], ready0[(b, 1)])
                if i >= 2:
                    pe.wait_ge(q["z_pp"], i - 1)
                qt, kt = hb[:, 2 * (b % 2), 128 * k:128 * k + 128], hb[:, 2 * (b % 2) + 1, :]
                a0, a1 = bank[2 * (i % 2)], bank[2 * (i % 2) + 1]
                mm(a0[:, 0:272], qt, kt[:, 0:272], True, True)
                mm(a1[:, 0:240], qt, kt[:, 272:512], True, True)
                mm(a1[:, 240:272], qt, ctx0[:, KEYS * b:KEYS * b + KEYS], True, True).then_inc(q["z_s"], 1)

            def transpose0(i):
                pe.wait_ge(q["z_exp"], i + 1)
                if i >= 2:
                    pe.wait_ge(q["z_pt"], i - 1)
                for j in range(4):
                    pe.transpose(W[i % 2][:, 128 * j:128 * j + 128], p0[i % 2][:, 128 * j:128 * j + 128], ident)
                pe.transpose(bank[2 * (i % 2)][0:KEYS, 384:512], p0[i % 2][:, 512:544], ident).then_inc(q["z_tr"], 1)

            def values0(i):
                b, k = divmod(i, TB)
                pe.wait_ge(q["z_pt"], i + 1)
                pe.wait_ge(q["z_pp"], i + 1)
                pe.wait_ge(q["T_free"], ready0[(b, 2)])
                if i >= 1:
                    pe.wait_ge(q["z_up"], i)
                o = ACC[:, 0:128]
                for j in range(4):
                    mm(o, pt0[i % 2][:, 128 * j:128 * j + 128], xt[:, b % 2, 128 * j:128 * j + 128], j == 0, False)
                mm(o, ptc0[i % 2], v0c[:, b, :], False, True).then_inc(q["z_pv"], 1)

            for s in range(stages):
                l = s // 2
                if s == 0:
                    xt_in(0, 0)
                    for j in range(3):
                        project(0, j)
                    scores0(0)
                    for i in range(16):
                        if i < 15:
                            scores0(i + 1)
                        transpose0(i)
                        if i >= 1:
                            values0(i - 1)
                        if i < 12:
                            if i % 4 == 0:
                                xt_in(0, i // 4 + 1)
                            else:
                                project(i // 4 + 1, i % 4 - 1)
                    values0(15)
                elif s % 2 == 0 and l in KW:
                    for b in range(2):
                        xt_in(s, b)
                        xf_base[(s, b)] = t_uses[0]
                    scores(l, 0)
                    for b in range(B):
                        if b + 2 < B:
                            xt_in(s, b + 2)
                            xf_base[(s, b + 2)] = t_uses[0]
                        if b + 1 < B:
                            scores(l, b + 1)
                        probs_t(l, b)
                        if b >= 1:
                            values(l, b - 1)
                    values(l, B - 1)
                elif s == 2:
                    scores1(0)
                    for i in range(16):
                        if i + 1 < 16:
                            scores1(i + 1)
                        probs_t1(i)
                        if i >= 1:
                            values1(i - 1)
                        if i % 4 == 0:
                            v1(i // 4)
                    values1(15)
                elif s == 4:
                    pe.wait_ge(q["dw_done"], 1)
                    for b in range(B):
                        last = pe.transpose(bank[0][:, 128 * b:128 * b + 128], xt[:, 0, 128 * b:128 * b + 128], ident)
                    last.then_inc(q["dwt_ps"], 1)
                    pe.wait_ge(d_dft, 16)
                    pe.wait_ge(q["dwt_sb"], 1)
                    for i, m in enumerate((FWD_RE_E, W_IM_E, W_RE_E2, FWD_RE_O, FWD_IM_O)):
                        mm(bank[1 + i][:, :], dft[:, m, :], xt[:, 1, :], True, True).then_inc(q["w_ps"], 1)
                    pe.wait_ge(q["fft_in"], 1)
                    pe.wait_ge(q["w_sb"], 5)
                    for i, (m, lo) in enumerate(((FWD_RE_E, 0), (FWD_IM_E, 0), (FWD_RE_O, 2), (FWD_IM_O, 2))):
                        mm(bank[i][:, :], dft[:, m, :], hb[:, lo, :], True, False)
                        mm(bank[i][:, :], dft[:, m + 1, :], hb[:, lo + 1, :], False, True).then_inc(q["fft_ps"], 1)
                    pe.wait_ge(q["prod_done"], 2)
                    yo = [xn4[:, 0, :], xn4[:, 2, :], hb[:, 0, :], hb[:, 2, :]]
                    for i, (bk, mr_, mi_, re, im) in enumerate(((6, INV_RE_O, INV_IM_O, yo[2], yo[3]), (7, INV_RE_O + 1, INV_IM_O + 1, yo[2], yo[3]),
                                                               (4, INV_RE_E, INV_IM_E, yo[0], yo[1]), (5, INV_RE_E + 1, INV_IM_E + 1, yo[0], yo[1]))):
                        mm(bank[bk][:, :], dft[:, mr_, :], re, True, False)
                        mm(bank[bk][:, :], dft[:, mi_, :], im, False, True).then_inc(q["inv_ps"], 1)
                else:
                    def pre(b, part):
                        if part == 0:
                            xt_in(s, b)
                        elif part == 1:
                            logits(l, b)
                        elif part == 2 and l == 2:
                            running(b)
                        elif part == 3:
                            comb_in(l, b)
                    for p in range(4):
                        pre(0, p)
                    pe.wait_ge(q["stage_used"], NQ if l == 3 else QBASE[l + 1])
                    gu(l, 0, 0)
                    gu(l, 0, 1)
                    for b in range(B):
                        for c in range(NC[l]):
                            k = b * NC[l] + c + 2
                            if k < B * NC[l]:
                                gu(l, *divmod(k, NC[l]))
                            down(l, b, c)
                            if c == 3 and b >= 1:
                                out_back(l, b - 1)
                            if b + 1 < B:
                                for at, p in ((4, 0), (7, 1), (11, 2), (13, 3)):
                                    if c == at:
                                        pre(b + 1, p)
                    out_back(l, B - 1)

        @block.vector
        def _(dve):
            ch_ = Chain(dve, q["dve"])
            link = ch_.link
            ps = q["prep_sb"]

            dve.wait_ge(q["prep_ps"], 1)
            dve.tensor_copy(w0t[:, 0:4:3, :], cols4(bank[0])[:, 0:4:3, :])
            dve.tensor_copy(w0t[:, 1, :], bank[0][:, 128:256]).then_inc(ps, 1)
            dve.tensor_copy(ctxt, bank[0][:, 256:384]).then_inc(ps, 1)
            dve.wait_ge(q["prep_ps"], 4)
            dve.tensor_copy(w1t, cols4(bank[1])).then_inc(ps, 1)
            dve.tensor_copy(lora_bt[:, :, :], cols4(bank[3])[0:R]).then_inc(ps, 1)
            dve.tensor_copy(w3t, cols4(bank[2])[:, 0:3, :]).then_inc(ps, 1)
            dve.wait_ge(q["prep_ps"], 6)
            dve.tensor_copy(rw[:, 0:72], bank[4][:, 0:72]).then_inc(ps, 1)
            dve.tensor_copy(bfc[:, :], bank[4][:, 128:160]).then_inc(ps, 1)
            dve.tensor_copy(bcol[:, :], bank[4][:, 160:169]).then_inc(ps, 1)
            dve.tensor_copy(sw_nat[:, :, :], cols4(bank[5])[:, 0:3, :]).then_inc(ps, 1)
            dve.wait_ge(ps, 2)
            dve.tensor_reduce(ctx_mean[:, :], ctxt.rearrange("p (b t) -> p b t", b=B), AX, ALU.add).then_inc(q["dve"], 1)
            ch_.n += 1
            dve.wait_ge(q["prep_ps"], 7)
            dve.wait_ge(q["dve"], ch_.n)
            link(dve.tensor_scalar(ctx_mean[:, :], ctx_mean[:, :], 1.0 / KEYS, None, ALU.mult))
            dve.scalar_tensor_tensor(w0, cols4(bank[6]), 2.0, w0t, ALU.mult, ALU.add).then_inc(ps, 1)
            dve.wait_ge(ps, 10)
            dve.tensor_copy(wo1t[:, :], w1t[:, 2, :])
            dve.tensor_copy(ctx0, ctxt).then_inc(ps, 1)
            dve.tensor_scalar(bq0s[:, :], bcol[:, 0:1], D ** -0.5, None, ALU.mult).then_inc(ps, 1)
            dve.wait_ge(q["prep_ps"], 8)
            dve.tensor_copy(w0[:, 2, :], bank[7][:, 0:128]).then_inc(ps, 1)
            dve.tensor_tensor(v0row, bank[7][0:1, 128:256], bo[:, 0, :], ALU.add).then_inc(ps, 1)
            dve.tensor_scalar(kt1[:, 0, :], bank[7][:, 256:384], bcol[:, 4:5], None, ALU.add).then_inc(ps, 1)
            dve.tensor_scalar(kt1[:, 1, :], bank[7][:, 384:512], bcol[:, 5:6], None, ALU.add).then_inc(ps, 1)
            dve.wait_ge(q["prep_ps"], 9)
            dve.tensor_copy(kv3[:, 0, :], bank[0][:, 0:128]).then_inc(ps, 1)
            dve.tensor_scalar(kv3[:, 1, :], bank[0][:, 128:256], bcol[:, 7:8], None, ALU.add).then_inc(ps, 1)
            dve.tensor_scalar(kmod[:, :], bank[0][:, 256:260], bcol[:, 8:9], None, ALU.add).then_inc(ps, 1)
            dve.wait_ge(q["prep_ps"], 10)
            sc = D ** -0.5
            dve.tensor_scalar(m3[:, :, :], bank[1][:, 256:384].rearrange("p (b n) -> p b n", b=B), sc, None, ALU.mult).then_inc(ps, 1)
            dve.wait_ge(q["prep_ps"], 11)
            dve.tensor_scalar(crow[:, :], bank[2][0:1, 256:384], sc, None, ALU.mult).then_inc(ps, 1)
            dve.wait_ge(q["prep_ps"], 13)
            dve.tensor_copy(v0c, cols4(bank[3])[0:KEYS]).then_inc(ps, 1)
            dve.tensor_copy(v3[:, :, :], cols4(bank[4])[0:KEYS]).then_inc(ps, 1)
            for j in range(3):
                link(dve.tensor_copy(bproj_bf[:, j, :], bproj))
                if j < 2:
                    link(dve.tensor_tensor(bproj, bproj, bproj_bf[:, j, :], ALU.subtract))
            link(dve.tensor_scalar(mask_add[:, :, :], mask_i[:, :, :], 0.0, NO_KEY, ALU.is_equal, ALU.mult))
            link(dve.tensor_reduce(anykeep[:, :], mask_add[:, :, :], AX, ALU.max))
            link(dve.tensor_scalar(anykeep[:, :], anykeep[:, :], NO_KEY / 2, None, ALU.is_gt))
            dve.wait_ge(q["prep_act"], 1)
            dve.tensor_tensor(rw_lo[:, :], rw[:, :], rw_hi[:, :].bitcast(F32), ALU.subtract)
            link(dve.memset(run[:, :, :], 0.0))

            for r in range(NQ0):
                slot, n, _ = quad(r)
                dve.wait_ge(q["l0w_hi"], r + 1)
                dve.tensor_tensor(wa_lo[:, slot:slot + n, :], cols4(W[r % 2])[:, 0:n, :], wa_hi[:, slot:slot + n, :].bitcast(F32),
                                  ALU.subtract).then_inc(q["l0w_lo"], 1)
                dve.wait_ge(q["l0w_lo"], r + 1)
                dve.sem_inc(q["stage_used"], 1)

            def norm(s, b):
                if 4 * s + b:
                    dve.wait_ge(q["ln_done"], 4 * s + b)
                if s == 0:
                    dve.wait_ge(d_x[b], 16)
                else:
                    dve.wait_ge(q["x_done"], 4 * (s - 1) + b + 1)
                for k in range(TB):
                    last = dve.bn_stats(stats[:, k, :], x[:, TB * b + k, :])
                link(last)
                for k in range(TB):
                    last = dve.bn_aggr(mv[:, k, :], stats[:, k, :])
                link(last)
                dve.tensor_scalar(veps[:, :], mv[:, :, 1], EPS, None, ALU.add).then_inc(q["veps_set"], 1)
                dve.wait_ge(q["rstd_set"], 4 * s + b + 1)
                for k in range(TB):
                    last = dve.tensor_scalar(xn[:, TB * b + k, :], x[:, TB * b + k, :], mv[:, k, 0:1], rstd[:, k:k + 1],
                                             ALU.subtract, ALU.mult)
                last.then_inc(q["ln_done"], 1)

            def shift(l, b):
                i = softmax_num(l, b)
                if l in KW:
                    g, n, src = TB, KW[l], G[b % 2]
                else:
                    g, n, src = HEADS, KEYS, bank[b % 4]
                dve.wait_ge(q["s_ps"], i + 1)
                if i >= 1:
                    dve.wait_ge(q["s_sub"], i)
                if i >= 2:
                    dve.wait_ge(q["s_exp"], i - 1)
                src = src[:, 0:g * n].rearrange("p (g n) -> p g n", g=g)
                link(dve.tensor_reduce(mx[:, 0:g], src, AX, ALU.max))
                dve.tensor_tensor(wk[:, b % 2, 0:g * n].rearrange("p (g n) -> p g n", g=g), src,
                                  mx[:, 0:g].unsqueeze(2).broadcast_to([128, g, n]), ALU.subtract).then_inc(q["s_sub"], 1)

            def normalise(l, b):
                i = softmax_num(l, b)
                g, n = (TB, KW[l]) if l in KW else (HEADS, KEYS)
                p = wk[:, 2 + b % 2, 0:g * n].rearrange("p (g n) -> p g n", g=g)
                dve.wait_ge(q["s_exp"], i + 1)
                if i >= 1:
                    dve.wait_ge(q["s_prob"], i)
                link(dve.tensor_reduce(sm[:, 0:g], p, AX, ALU.add))
                link(dve.reciprocal(sm1[:, 0:g], sm[:, 0:g]))
                if l == 1:
                    link(dve.tensor_scalar(sm1[:, :], sm1[:, :], anykeep[:, b % TB:b % TB + 1], None, ALU.mult))
                dve.tensor_tensor(p, p, sm1[:, 0:g].unsqueeze(2).broadcast_to([128, g, n]), ALU.mult).then_inc(q["s_prob"], 1)

            def update(s, b, src, scale):
                dve.scalar_tensor_tensor(x[:, TB * b:TB * b + TB, :], cols4(src), scale, x[:, TB * b:TB * b + TB, :],
                                         ALU.mult, ALU.add).then_inc(q["x_done"], 1)

            def lo_x(l, b):
                dve.wait_ge(q["xhi_done"], fnum(l, b))
                dve.tensor_tensor(xt_lo[:, b % 2, :], T[:, :], xt_hi[:, b % 2, :].bitcast(F32), ALU.subtract).then_inc(q["xlo_done"], 1)
                dve.wait_ge(q["xlo_done"], fnum(l, b))
                dve.sem_inc(q["T_free"], 1)

            def top(vals, n, k, marked):
                w = n + 8 - k
                if k < 8:
                    dve.memset(vals[:, :, n:w], LOW)
                for t in range(TB):
                    last = dve.max(t8[:, t, :], vals[:, t, 0:w if k == 8 else n] if n >= 8 else vals[:, t, 0:w])
                link(last)
                if k < 8:
                    link(dve.memset(t8[:, :, k:8], LOW))
                for t in range(TB):
                    last = dve.match_replace(marked[:, t, 0:w], t8[:, t, :], vals[:, t, 0:w], TAKEN)
                link(last)

            def route_shift(l, b):
                if l == 1:
                    E = N_EXP[l]
                    s_ = rt[:, :, 0:E]
                    dve.wait_ge(q["logits_ps"], fnum(l, b))
                    src = T[:, 0:TB * E].rearrange("p (k e) -> p k e", k=TB)
                    link(dve.tensor_reduce(wsum[:, :], src, AX, ALU.max))
                    dve.tensor_tensor(s_, src, wsum[:, :].unsqueeze(2).broadcast_to([128, TB, E]), ALU.subtract).then_inc(q["rsm_sub"], 1)

            def route(l, b):
                E, K = N_EXP[l], TOP_K[l]
                s_ = rt[:, :, 0:E]
                c_ = ch[:, :, 0:E]
                if fnum(l, b) > 1:
                    dve.wait_ge(q["comb_done"], fnum(l, b) - 1)
                if l == 1:
                    dve.wait_ge(q["score_done"], fnum(l, b))
                    dve.sem_inc(q["T_free"], 1)
                    link(dve.tensor_reduce(wsum[:, :], s_, AX, ALU.add))
                    link(dve.reciprocal(wrec[:, :], wsum[:, :]))
                    link(dve.tensor_tensor(c_, s_, wrec[:, :].unsqueeze(2).broadcast_to([128, TB, E]), ALU.mult))
                    s_ = c_
                else:
                    dve.wait_ge(q["score_done"], fnum(l, b))
                    dve.sem_inc(q["T_free"], 1)
                    off = {0: 0, 2: 32, 3: 64}[l]
                    link(dve.tensor_tensor(c_, s_, rb[:, off:off + E].unsqueeze(1).broadcast_to([128, TB, E]), ALU.add))
                if l == 0:
                    v = ch[:, :, 0:32].rearrange("p k (g j) -> p k g j", g=4)
                    u = tour[:, :, :].rearrange("p (k g) j -> p k g j", k=TB)
                    dve.tensor_tensor(u[:, :, :, 0:4], v[:, :, :, 0:4], v[:, :, :, 4:8], ALU.max)
                    link(dve.tensor_tensor(u[:, :, :, 4:8], v[:, :, :, 0:4], v[:, :, :, 4:8], ALU.min))
                    for first, second, n, o in ((0, 4, 2, 8), (8, 10, 1, 12)):
                        f0, f1 = u[:, :, :, first:first + n], u[:, :, :, first + n:first + 2 * n]
                        s0, s1 = u[:, :, :, second:second + n], u[:, :, :, second + n:second + 2 * n]
                        dve.tensor_tensor(u[:, :, :, o:o + n], f0, f1, ALU.max)
                        dve.tensor_tensor(u[:, :, :, 14:14 + n], f0, f1, ALU.min)
                        link(dve.tensor_tensor(u[:, :, :, o + n:o + 2 * n], s0, s1, ALU.max))
                        link(dve.tensor_tensor(u[:, :, :, o + n:o + 2 * n], u[:, :, :, o + n:o + 2 * n], u[:, :, :, 14:14 + n], ALU.max))
                    link(dve.tensor_tensor(gp[:, :, 0:4], u[:, :, :, 12], u[:, :, :, 13], ALU.add))
                    for t in range(TB):
                        last = dve.max(t8[:, t, :], gp[:, t, :])
                    link(last)
                    link(dve.memset(t8[:, :, 2:8], LOW))
                    for t in range(TB):
                        last = dve.match_replace(gr[:, t, :], t8[:, t, :], gp[:, t, :], TAKEN)
                    link(last)
                    link(dve.tensor_scalar(gm[:, :, :], gr[:, :, 0:4], TAKEN / 2, None, ALU.is_gt))
                    link(dve.tensor_tensor(v, v, gm[:, :, :].unsqueeze(3).broadcast_to([128, TB, 4, 8]), ALU.mult))
                    link(dve.tensor_scalar(c_, c_, 0.0, None, ALU.add))
                top(ch, E, K, mr)
                m_ = selm[:, :, 0:E]
                link(dve.tensor_scalar(m_, mr[:, :, 0:E], TAKEN / 2, None, ALU.is_gt))
                w_ = wsel[:, :, 0:E]
                link(dve.tensor_tensor(w_, m_, s_, ALU.mult))
                if l != 3:
                    link(dve.tensor_reduce(wsum[:, :], w_, AX, ALU.add))
                    if l == 0:
                        link(dve.tensor_scalar(wsum[:, :], wsum[:, :], 1e-20, None, ALU.add))
                    if l == 2:
                        link(dve.tensor_scalar(wsum[:, :], wsum[:, :], 1e-12, None, ALU.max))
                    link(dve.reciprocal(wrec[:, :], wsum[:, :]))
                    if l == 0:
                        link(dve.tensor_scalar(wrec[:, :], wrec[:, :], 2.5, None, ALU.mult))
                    link(dve.tensor_tensor(w_, w_, wrec[:, :].unsqueeze(2).broadcast_to([128, TB, E]), ALU.mult))
                if l == 2:
                    if b >= 1:
                        link(dve.tensor_copy(run[:, 0, :], run[:, TB, :]))
                    for t in range(TB):
                        link(dve.tensor_tensor(run[:, t + 1, :], run[:, t, :], m_[:, t, :], ALU.add))
                    dve.tensor_copy(sel_bf[:, :, :], m_)
                    dve.tensor_copy(run_bf[:, :, :], run[:, 0:TB, :]).then_inc(q["cum_need"], 1)

            def route_end(l, b):
                E = N_EXP[l]
                m_, w_ = selm[:, :, 0:E], wsel[:, :, 0:E]
                if l == 2:
                    dve.wait_ge(q["cum_ps"], b + 1)
                    cum = T[:, 0:128].rearrange("p (k e) -> p k e", k=TB)
                    link(dve.tensor_scalar(m_, cum, CAPACITY + 0.5, None, ALU.is_lt))
                    dve.sem_inc(q["T_free"], 1)
                    link(dve.tensor_tensor(w_, w_, m_, ALU.mult))
                for j in range(2):
                    link(dve.tensor_copy(chl[:, :, E * j:E * j + E], w_))
                    rest = w_ if j == 0 else chl[:, :, 2 * E:3 * E]
                    last = dve.tensor_tensor(rest, w_, chl[:, :, E * j:E * j + E], ALU.subtract)
                    if j == 0:
                        link(last)
                last.then_inc(q["comb_done"], 1)

            def combt_free(l, b):
                dve.wait_ge(q["combt_done"], fnum(l, b))
                dve.sem_inc(q["T_free"], 1)

            def mult(l, b, c):
                k = knum(l, b, c)
                h = hb[:, k % 4, :]
                dve.wait_ge(q["sg_done"], k + 1)
                if l == 1:
                    dve.wait_ge(q["u_done"], UB[1] + (k - CB[1]) // 4 + 1)
                    dve.tensor_tensor(h, h, W[(k // 4) % 2][:, :], ALU.mult).then_inc(q["h_done"], 1)
                    return
                dve.wait_ge(q["u_done"], UB[l] + k - CB[l] + 1)
                if c < ROUTED[l]:
                    link(dve.tensor_tensor(h, h, U[k % 2][:, :], ALU.mult))
                    dve.tensor_tensor(h, h, W[k % 2][:, :], ALU.mult).then_inc(q["h_done"], 1)
                else:
                    dve.tensor_tensor(h, h, U[k % 2][:, :], ALU.mult).then_inc(q["h_done"], 1)

            def low(l, b, c):
                k = knum(l, b, c)
                dve.wait_ge(q["hhi_done"], k + 1)
                dve.tensor_tensor(h_lo[:, k % 2, :], hb[:, k % 4, :], h_hi[:, k % 2, :].bitcast(F32),
                                  ALU.subtract).then_inc(q["hlo_done"], 1)

            def max0(i):
                dve.wait_ge(q["z_s"], i + 1)
                dve.tensor_reduce(mx[:, i:i + 1], psum[:, 2 * (i % 2):2 * (i % 2) + 2, 0:KEYS0 // 2], mybir.AxisListType.XY,
                                  ALU.max, negate=True).then_inc(q["z_max"], 1)

            def probs0_out(i):
                dve.wait_ge(q["z_tr"], i + 1)
                if i >= 2:
                    dve.wait_ge(q["z_pv"], i - 1)
                dve.tensor_copy(pt0[i % 2], W[i % 2][:, :]).then_inc(q["z_pt"], 1)

            def update0(i):
                dve.wait_ge(q["z_pv"], i + 1)
                if i:
                    dve.wait_ge(q["z_up"], i)
                link(dve.reciprocal(sm1[:, 0:1], zsum[:, i:i + 1]))
                link(dve.tensor_scalar(sm[:, 0:1], sm1[:, 0:1], tg[:, 0:1], None, ALU.mult))
                dve.scalar_tensor_tensor(x[:, i, :], ACC[:, 0:128], sm[:, 0:1], x[:, i, :],
                                         ALU.mult, ALU.add).then_inc(q["z_up"], 1)
                if i % TB == TB - 1:
                    dve.wait_ge(q["z_up"], i + 1)
                    dve.sem_inc(q["x_done"], 1)

            dve.wait_ge(q["act"], 1)
            for s in range(stages):
                l = s // 2
                if s == 0:
                    norm(0, 0)
                    norm(0, 1)
                    max0(0)
                    for i in range(16):
                        if i < 15:
                            max0(i + 1)
                        probs0_out(i)
                        if i >= 1:
                            update0(i - 1)
                        if i % 4 == 2 and i < 8:
                            norm(0, i // 4 + 2)
                    update0(15)
                elif s % 2 == 0 and l in KW:
                    norm(s, 0)
                    norm(s, 1)
                    shift(l, 0)
                    for b in range(B):
                        if b + 2 < B:
                            norm(s, b + 2)
                        if b + 1 < B:
                            shift(l, b + 1)
                        normalise(l, b)
                        if b >= 1:
                            dve.wait_ge(q["pv_ps"], softmax_num(l, b))
                            update(s, b - 1, W[(b - 1) % 2], tg[:, l:l + 1])
                    dve.wait_ge(q["pv_ps"], softmax_num(l, B - 1) + 1)
                    update(s, B - 1, W[(B - 1) % 2], tg[:, l:l + 1])
                elif s == 2:
                    for b in range(B):
                        norm(s, b)
                    shift(1, 0)
                    for i in range(16):
                        if i + 1 < 16:
                            shift(1, i + 1)
                        normalise(1, i)
                        if i % 4 == 1 and i > 4:
                            dve.wait_ge(q["pv_ps"], i - 1)
                            update(s, i // 4 - 1, ACC, tg[:, 1:2])
                    dve.wait_ge(q["pv_ps"], 16)
                    update(s, 3, ACC, tg[:, 1:2])
                elif s == 4:
                    for b in range(B):
                        dve.tensor_scalar(xt[:, 0, 128 * b:128 * b + 128], w2conv[:, :], kmod[:, b:b + 1], None, ALU.mult) if b < B - 1 else \
                            dve.tensor_scalar(xt[:, 0, 128 * b:128 * b + 128], w2conv[:, :], kmod[:, b:b + 1], None, ALU.mult).then_inc(q["dw_done"], 1)
                    for b in range(B):
                        norm(s, b)
                    dve.wait_ge(q["ln_done"], 4 * s + B)
                    blk = xn[:, :, :].rearrange("p (b k) d -> p b k d", b=B)
                    hv = hb[:, :, :].rearrange("p m (b d) -> p m b d", b=B)
                    dve.tensor_tensor(hv[:, 0], blk[:, :, 0, :], blk[:, :, 2, :], ALU.add)
                    dve.tensor_tensor(hv[:, 1], blk[:, :, 1, :], blk[:, :, 3, :], ALU.add)
                    dve.tensor_tensor(hv[:, 2], blk[:, :, 0, :], blk[:, :, 2, :], ALU.subtract)
                    dve.tensor_tensor(hv[:, 3], blk[:, :, 1, :], blk[:, :, 3, :], ALU.subtract).then_inc(q["fft_in"], 1)
                    dve.wait_ge(q["w_sb"], 5)
                    dve.wait_ge(q["fft_in"], 1)
                    for par in range(2):
                        y = xn4 if par == 0 else hb
                        xr, xi = bank[2 * par], bank[2 * par + 1]
                        wr, wi, wr2 = (wk[:, 0, :], wk[:, 1, :], wk[:, 2, :]) if par == 0 else (wk[:, 3, :], wk[:, 4, :], wk[:, 3, :])
                        dve.wait_ge(q["fft_ps"], 4 if par == 1 else 2)
                        dve.tensor_tensor(y[:, 0, :], wr, xr[:, :], ALU.mult)
                        dve.tensor_tensor(y[:, 1, :], wi, xi[:, :], ALU.mult)
                        dve.tensor_tensor(y[:, 2, :], wi, xr[:, :], ALU.mult)
                        link(dve.tensor_tensor(y[:, 3, :], wr2, xi[:, :], ALU.mult))
                        dve.tensor_tensor(y[:, 0, :], y[:, 0, :], y[:, 1, :], ALU.subtract)
                        dve.tensor_tensor(y[:, 2, :], y[:, 2, :], y[:, 3, :], ALU.add).then_inc(q["prod_done"], 1)
                    xv = x[:, :, :].rearrange("p (b k) d -> p b k d", b=B)
                    g2 = tg[:, 2:3]
                    dve.wait_ge(q["inv_ps"], 4)
                    for k in range(4):
                        e = bank[4 + k % 2][:, :].rearrange("p (b d) -> p b d", b=B)
                        last = dve.scalar_tensor_tensor(xv[:, :, k, :], e, g2, xv[:, :, k, :], ALU.mult, ALU.add)
                    link(last)
                    dve.wait_ge(q["o_sb"], 2)
                    for k in range(4):
                        o = xt[:, k % 2, :].rearrange("p (b d) -> p b d", b=B)
                        dve.tensor_tensor(xv[:, :, k, :], xv[:, :, k, :], o, ALU.add if k < 2 else ALU.subtract).then_inc(q["x_done"], 1)
                    dve.wait_ge(q["x_done"], 20)
                else:
                    norm(s, 0)
                    lo_x(l, 0)
                    route_shift(l, 0)
                    route(l, 0)
                    route_end(l, 0)
                    combt_free(l, 0)
                    for b in range(B):
                        for c in range(NC[l]):
                            mult(l, b, c)
                            k = b * NC[l] + c
                            if k >= 1:
                                low(l, *divmod(k - 1, NC[l]))
                            if c == 4 and b >= 1:
                                dve.wait_ge(q["outt_ps"], fnum(l, b - 1))
                                update(s, b - 1, T, tg[:, 4 + l:5 + l])
                                dve.wait_ge(q["x_done"], 4 * s + b)
                                dve.sem_inc(q["T_free"], 1)
                            if b + 1 < B:
                                if c == 2:
                                    norm(s, b + 1)
                                if c == 6:
                                    lo_x(l, b + 1)
                                if c == 8:
                                    route_shift(l, b + 1)
                                if c == 10:
                                    route(l, b + 1)
                                if c == 12:
                                    route_end(l, b + 1)
                                if c == 15:
                                    combt_free(l, b + 1)
                    low(l, B - 1, NC[l] - 1)
                    dve.wait_ge(q["outt_ps"], fnum(l, B - 1))
                    update(s, B - 1, T, tg[:, 4 + l:5 + l])
                    dve.wait_ge(q["x_done"], 4 * s + B)
                    dve.sem_inc(q["T_free"], 1)
    return nc


def _inputs():
    return ["x", "ctx_1024", "mask_1x1xSxS2_ik0", "g_xattn", "g_ffn"] + [
        f"L0_xattn_{k}{w}" for w in "qkvo" for k in "WbAB"] + [
        "L0_ffn_" + n for n in ("gate_w", "gate_bias", "expert_gate", "expert_up", "expert_down", "shared_gate", "shared_up", "shared_down")] + [
        f"L1_xattn_{k}{w}" for w in "qkvo" for k in "Wb"] + [
        "L1_ffn_" + n for n in ("router_w", "w_fc", "b_fc", "w_proj", "b_proj")] + [
        "L2_xattn_" + n for n in ("weight", "kp_w", "kp_b")] + [
        "L2_ffn_" + n for n in ("gate_w", "bias", "W1", "W3", "W2", "sw1", "sw3", "sw2")] + [
        "L3_xattn_" + n for n in ("Wk", "Wv", "bv", "Wq", "bq", "Wo", "bo")] + [
        "L3_ffn_" + n for n in ("router_w", "expert_bias", "shared_w1", "shared_w2", "shared_w3", "routed_w1", "routed_w2", "routed_w3")]


STAGES = 8


def kernel(**inputs):
    import concourse.bacc as bacc
    from concourse.bass_utils import run_bass_kernel_spmd

    nc = bacc.Bacc("TRN2", target_bir_lowering=False, num_devices=1)
    arrays, a = {}, {}
    for name in _inputs():
        arrays["in_" + name] = np.ascontiguousarray(inputs[name])
    arrays["in_consts"] = constants()
    for name, v in arrays.items():
        a[name[3:]] = nc.dram_tensor(name, v.shape, mybir.dt.from_np(v.dtype), kind="ExternalInput").ap()
    out = nc.dram_tensor("out", (B, S, D), F32, kind="ExternalOutput").ap()
    build(nc, a, out, STAGES)
    r = run_bass_kernel_spmd(nc, [arrays], core_ids=[0])
    return r.results[0]["out"]
```

```python
from contextlib import ExitStack

import concourse.bass as bass
import numpy as np
from concourse import mybir

F32 = mybir.dt.float32
F32R = mybir.dt.float32r
BF16 = mybir.dt.bfloat16
I32 = mybir.dt.int32
ALU = mybir.AluOpType
ACT = mybir.ActivationFunctionType
AX = mybir.AxisListType.X

B, S, D = 4, 512, 128
TB = S // 128
KEYS = 32
HEADS, DK = 16, 8
R = 8
NO_KEY = -1.0e30
LOW, TAKEN = -3.0e38, 3.0e38
EPS = 1e-5
N_EXP = [32, 8, 32, 16]
TOP_K = [8, 2, 4, 2]
ROUTED = [16, 32, 16, 16]
SHARED = [1, 0, 1, 4]
NC = [r + s for r, s in zip(ROUTED, SHARED)]
CB = [B * sum(NC[:l]) for l in range(5)]
CAPACITY = 2 * 512 * 4 // 32
UB = [0, CB[1], CB[1] + B * 8, CB[1] + B * 8 + B * NC[2]]
TRANSPOSED = {0: 0, 1: 1, 2: 2, 3: 3, 5: 4, 6: 5, 7: 6}

C_ID, C_HEAD, C_TRI, C_SEL, C_SEL16, C_SEL8, C_DFT = 0, 128, 144, 272, 304, 320, 328
FWD_RE_E, FWD_IM_E, FWD_RE_O, FWD_IM_O, W_IM_E, W_RE_E2, INV_RE_E, INV_IM_E, INV_RE_O, INV_IM_O = 0, 2, 4, 6, 8, 9, 10, 12, 14, 16
N_DFT = 18
C_ALL = C_DFT + N_DFT * 128


def constants():
    c = np.zeros((128, C_ALL), np.float64)
    i = np.arange(128)
    c[:, C_ID:C_ID + 128] = np.eye(128)
    c[:, C_HEAD:C_HEAD + HEADS] = (i[:, None] // DK) == np.arange(HEADS)[None]
    c[:, C_TRI:C_TRI + 128] = i[:, None] <= i[None]
    c[0:96, C_SEL:C_SEL + 32] = (i[:96, None] % 32) == np.arange(32)[None]
    c[0:48, C_SEL16:C_SEL16 + 16] = (i[:48, None] % 16) == np.arange(16)[None]
    c[0:24, C_SEL8:C_SEL8 + 8] = (i[:24, None] % 8) == np.arange(8)[None]
    m = c[:, C_DFT:].reshape(128, N_DFT, 128)
    h = i[None]
    for blk in range(2):
        n = (i + 128 * blk)[:, None]
        even, odd = 2 * np.pi * n * (2 * h) / 512, 2 * np.pi * n * (2 * h + 1) / 512
        m[:, FWD_RE_E + blk], m[:, FWD_RE_O + blk], m[:, FWD_IM_O + blk] = np.cos(even), np.cos(odd), -np.sin(odd)
        m[:, FWD_IM_E + blk] = -np.sin(even)
        m[:, FWD_IM_E + blk, 0] = (-1.0) ** n[:, 0]
        m[:, INV_RE_E + blk], m[:, INV_IM_E + blk] = 2 / 512 * np.cos(even).T, -2 / 512 * np.sin(even).T
        m[0, INV_RE_E + blk] = 1 / 512
        m[0, INV_IM_E + blk] = (-1.0) ** n[:, 0] / 512
        m[:, INV_RE_O + blk], m[:, INV_IM_O + blk] = 2 / 512 * np.cos(odd).T, -2 / 512 * np.sin(odd).T
    m[:, W_IM_E] = m[:, FWD_IM_E]
    m[:, W_IM_E, 0] = 0
    m[:, W_RE_E2] = m[:, FWD_RE_E]
    m[:, W_RE_E2, 0] = (-1.0) ** i
    return c.astype(np.float32)


class Chain:

    def __init__(self, eng, sem):
        self.eng, self.sem, self.n = eng, sem, 0

    def link(self, ins):
        self.n += 1
        ins.then_inc(self.sem, 1)
        self.eng.wait_ge(self.sem, self.n)


def build(nc, a, out, stages=8):
    with ExitStack() as ctx:
        def sb(name, shape, dt=F32):
            return ctx.enter_context(nc.sbuf_tensor(name, shape, dt))

        def sem(name):
            return ctx.enter_context(nc.semaphore(name))

        psum = ctx.enter_context(nc.psum_tensor("psum", [128, 8, 512], F32))
        bank = [psum[:, i, :] for i in range(8)]
        G, U, W, ACC, T = bank[0:2], bank[2:4], bank[4:6], bank[6], bank[7]

        const = sb("const", [128, C_ALL])
        ident = const[:, C_ID:C_ID + 128]
        headmask = const[:, C_HEAD:C_HEAD + HEADS]
        dft = const[:, C_DFT:].rearrange("p (m h) -> p m h", m=N_DFT)
        ident_bf = sb("ident_bf", [128, 128], BF16)
        tri_bf = sb("tri_bf", [128, 128], BF16)
        ones_bf = sb("ones_bf", [128, 128], BF16)
        ones_row = sb("ones_row", [1, 128])
        pair_sel = sb("pair_sel", [96, 32, 64], mybir.dt.float8e4)
        sel16 = sb("sel16", [48, 16], BF16)
        sel8 = sb("sel8", [24, 8], BF16)
        neghalf = sb("neghalf", [128, TB])
        e_base = sb("e_base", [128, 8])
        x = sb("x", [128, B * TB, D])
        xn = sb("xn", [128, B * TB, D])
        xt = sb("xt", [128, 2, S])
        xt_hi = sb("xt_hi", [128, 2, S], F32R)
        xt_lo = sb("xt_lo", [128, 2, S], F32R)
        wa_hi = sb("wa_hi", [128, 51, 128], F32R)
        wa_lo = sb("wa_lo", [128, 51, 128], F32R)
        wb_hi = sb("wb_hi", [128, 64, 128], F32R)
        wb_lo = sb("wb_lo", [128, 64, 128], F32R)
        stage = sb("stage", [128, 2, 512])
        hb = sb("hb", [128, 4, 512])
        h_hi = sb("h_hi", [128, 3, 512], F32R)
        h_lo = sb("h_lo", [128, 3, 512], F32R)
        comb_t = sb("comb_t", [96, 2, S], BF16)
        wk = sb("wk", [128, 6, 512])
        g_all = sb("g_all", [128, 8])
        tg = sb("tg", [128, 8])
        rb = sb("rb", [128, 80])
        rw_hi = sb("rw_hi", [128, 88], F32R)
        rw_lo = sb("rw_lo", [128, 88], F32R)
        bfc = sb("bfc", [128, 32])
        bproj_bf = sb("bproj_bf", [24, 3, 128], BF16)
        sw_t = sb("sw_t", [128, 3, 128], BF16)
        bcol = sb("bcol", [128, 9])
        bo = sb("bo", [1, 3, 128])
        m3 = const[:, C_TRI:C_TRI + 128].rearrange("p (b n) -> p b n", b=B)
        v3 = sb("v3", [32, B, 128])
        crow = sb("crow", [1, 128])
        kmod = sb("kmod", [128, B])
        ctx_mean = sb("ctx_mean", [128, B])
        w2conv = sb("w2conv", [128, 128])
        mask_add = sb("mask_add", [128, TB, KEYS], BF16)
        anykeep = sb("anykeep", [128, TB])
        stats = sb("stats", [128, TB, 6])
        mv = sb("mv", [128, TB, 2])
        veps = sb("veps", [128, TB])
        rstd = sb("rstd", [128, TB])
        mx = const[:, C_SEL16:C_SEL16 + 16]
        zsum = sb("zsum", [128, 16])
        bq0s = sb("bq0s", [128, 1])
        bq1s = sb("bq1s", [128, 1])
        sm = sb("sm", [128, 16])
        sm1 = const[:, C_SEL:C_SEL + 32].rearrange("p (i h) -> p i h", i=2)
        rt = sb("rt", [128, TB, 32])
        ch = sb("ch", [128, TB, 38])
        mr = sb("mr", [128, TB, 38])
        t8 = sb("t8", [128, TB, 8])
        chosen = sb("chosen", [128, 256])
        mask_i = chosen[:, 0:128].bitcast(I32).rearrange("p (k t) -> p k t", k=TB)
        tour = chosen[:, :].rearrange("p (g j) -> p g j", g=16)
        gp = sb("gp", [128, TB, 10])
        gr = sb("gr", [128, TB, 10])
        gm = sb("gm", [128, TB, 4])
        selm = chosen[:, 0:128].rearrange("p (k e) -> p k e", k=TB)
        wsel = chosen[:, 128:256].rearrange("p (k e) -> p k e", k=TB)
        wsum = sb("wsum", [128, TB])
        wrec = sb("wrec", [128, TB])
        chl = sb("chl", [128, TB, 96], BF16)
        sel_bf = sb("sel_bf", [128, TB, 32], BF16)
        run_bf = sb("run_bf", [128, TB, 32], BF16)
        run = sb("run", [128, TB + 1, 32])

        d_const, d_dft, d_small, d_l0, d_wnat, d_out = [sem(n) for n in ("d_const", "d_dft", "d_small", "d_l0", "d_wnat", "d_out")]
        d_x = [sem(f"d_x{b}") for b in range(B)]
        d_stage = [sem(f"d_stage{i}") for i in range(2)]
        names = """pool_set sel_set prep_ps prep_sb prep_act veps_set rstd_set ln_done xt_ps xhi_done xlo_done
            xf_done logits_ps score_done cum_need cum_ps comb_done combt_ps combt_done T_free g_done u_done sg_done
            h_done hhi_done hlo_done down_done outt_done outt_ps x_done dve act pool s_ps s_sub s_exp s_prob s_rec
            p_ps p_sb pv_ps l0w_ps l0w_hi l0w_lo stage_used mexp_max kbd_done q1_need vbd_done v1_ps q1_ps fft_in fft_ps w_ps w_sb
            prod_done whi_done shared2 z_proj z_s z_max z_exp z_tr z_pt z_pp z_pv z_up inv_ps o_sb dw_done dwt_ps dwt_sb bf_done sw_done rsm_sub m_done""".split()
        q = {n: sem(n) for n in names}

        wnat = wk[:, 0:3, :].rearrange("p a (m d) -> p (a m) d", m=4)
        wk_flat = wk[:, :, :].rearrange("p a c -> p (a c)")
        KEYS0 = KEYS + S
        p0 = [wk_flat[:, 0:544], wk_flat[:, 544:1088]]
        pt0 = [wk_flat[:, 1088:1600], wk_flat[:, 1600:2112]]
        ptc0 = [wk_flat[0:KEYS, 2112:2240], wk_flat[0:KEYS, 2240:2368]]
        w0t = xt[:, 0, :].rearrange("p (m d) -> p m d", m=4)
        w1t = xt[:, 1, :].rearrange("p (m d) -> p m d", m=4)
        kbd1, vbd1, q1t = hb[:, 0:2, :], xt[:, 1, :], hb[:, 2:4, :]
        v1 = xn[:, 2 * TB:, :].rearrange("p (a k) d -> p a (k d)", a=2)
        w3t = wk[:, 5, 0:384].rearrange("p (m d) -> p m d", m=3)
        ctxt = hb[:, 0, 0:128]
        kv3 = hb[:, 1, 0:256].rearrange("p (m c) -> p m c", m=2)
        ctx_nat = hb[:, 2, 0:128]
        kpw_nat = hb[:, 3, 0:128]
        sw_nat = hb[:, 2, 128:512].rearrange("p (m d) -> p m d", m=3)
        rw = hb[:, 3, 128:216]

        xn4 = xn[:, :, :].rearrange("p (m k) d -> p m (k d)", m=4)

        lora_a, lora_bt = [wk[0:R, i, :].rearrange("p (m d) -> p m d", m=4) for i in (3, 4)]
        lora_b = xn[:, 8, 0:4 * R].rearrange("p (m r) -> p m r", m=4)
        rw_nat, bfc_nat = xn[0:32, 9:12, :], xn[0:32, 12, :]
        brow = xn[0:9, 13, :]
        small_bf = xn[:, 14:16, :].rearrange("p a b -> p (a b)").bitcast(BF16)
        sw_bf = small_bf[:, 0:384].rearrange("p (m d) -> p m d", m=3)
        gw2_bf = small_bf[0:32, 384:512]
        bproj = wk[0:24, 5, 384:512]
        early = const[:, C_DFT:]
        v0c = early[0:KEYS, 0:512].rearrange("p (b d) -> p b d", b=B)
        w0 = early[:, 1792:2304].rearrange("p (m d) -> p m d", m=4)
        ctx0 = early[:, 512:640]
        v0row = early[0:1, 640:768]
        wq1, wo1t = early[:, 1280:1408], early[:, 1408:1536]
        kt1 = early[:, 1536:1792].rearrange("p (m c) -> p m c", m=2)

        def cols4(t):
            return t[:, :].rearrange("p (k c) -> p k c", k=4)

        def quads_l0():
            r = []
            for base, w in ((0, a["L0_ffn_expert_gate"]), (16, a["L0_ffn_expert_up"])):
                v = w.rearrange("(c e) i d -> (e i) c d", e=2)
                r += [(v[:, 4 * k:4 * k + 4, :], base + 4 * k, 4) for k in range(4)]
            v = a["L0_ffn_expert_down"].rearrange("e d i -> d e i")
            r += [(v[:, 8 * k:8 * k + 8, :], 32 + 4 * k, 4) for k in range(4)]
            return r

        QL0 = quads_l0()
        NQ0 = len(QL0) + 1

        def quads_nat(layer):
            r = []
            if layer == 1:
                fc = a["L1_ffn_w_fc"]
                pr = a["L1_ffn_w_proj"].rearrange("e (c h) d -> e h c d", c=4)
                for e in range(8):
                    r += [(fc[e], 4 * e, 4), (pr[e], 32 + 4 * e, 4)]
            if layer == 3:
                for base, w in ((0, "routed_w1"), (20, "routed_w2"), (40, "routed_w3")):
                    v = a["L3_ffn_" + w].rearrange("e d h -> d e h")
                    r += [(v[:, 4 * k:4 * k + 4, :], base + 4 * k, 4) for k in range(4)]
                r += [(a["L3_ffn_shared_w1"][0], 16, 4), (a["L3_ffn_shared_w2"][0], 36, 4),
                      (a["L3_ffn_shared_w3"][0].rearrange("(c h) d -> h c d", c=4), 56, 4)]
            if layer == 2:
                for base, w in ((0, "W1"), (16, "W3")):
                    v = a["L2_ffn_" + w].rearrange("e d i -> d e i")
                    r += [(v[:, 8 * k:8 * k + 8, :], base + 4 * k, 4) for k in range(4)]
                v = a["L2_ffn_W2"].rearrange("(c e) i d -> (e i) c d", e=2)
                r += [(v[:, 4 * k:4 * k + 4, :], 32 + 4 * k, 4) for k in range(4)]
            return r

        QN = {l: quads_nat(l) for l in (1, 2, 3)}
        QBASE = {1: NQ0, 2: NQ0 + len(QN[1]), 3: NQ0 + len(QN[1]) + len(QN[2])}
        NQ = QBASE[3] + len(QN[3])

        def slots(layer, c):
            if layer == 0:
                return (c, 16 + c, 32 + c) if c < 16 else (48, 49, 50)
            if layer == 1:
                return c, None, 32 + c
            if layer == 2:
                return (c, 16 + c, 32 + c) if c < 16 else (48, 49, 50)
            return c, 20 + c, 40 + c

        block = ctx.enter_context(nc.Block())

        def loaded(r):
            return sum(48 if k == NQ0 - 1 else 16 for k in range(r % 2, r + 1, 2))

        def quad(r):
            if r < NQ0 - 1:
                return QL0[r][1], QL0[r][2], 0
            if r == NQ0 - 1:
                return 48, 3, 0
            layer = 1 if r < QBASE[2] else 2 if r < QBASE[3] else 3
            return QN[layer][r - QBASE[layer]][1:] + (layer,)

        def tnum(s, b):
            return 4 * TRANSPOSED[s] + b + 1

        def xn_rows(s, b):
            return TB * (b if s == 4 else b % 2)

        def fnum(l, b):
            return 4 * l + b + 1

        def knum(l, b, c):
            return CB[l] + b * NC[l] + c

        def softmax_num(l, b):
            return b if l == 1 else 16 + b

        KW = {3: KEYS}

        NORM_AT, OUT_AT, BACK_AT, ADD_AT, XN_AT, XHI_AT, XLO_AT, LOGITS_AT, SCORE_AT = 0, 1, 0, 2, 2, 4, 5, 4, 6
        RUN_AT = 10
        ROUTE_AT, WEIGH_AT, COMB_AT, COMBT_AT = [{l: at + 7 * (l == 1) for l in range(4)} for at in (7, 12, 11, 13)]
        NORM2_AT, XN2_AT, NORM3_AT, XN3_AT = 4, 6, 9, 11
        AHEAD = 3

        def split_round(l, b, c):
            if l == 3 or c % 4 != 2 or c > 14:
                return None
            n = -(-len(QN[l + 1]) // B)
            j, r = c // 4, n * b + c // 4
            return QBASE[l + 1] + r if j < n and r < len(QN[l + 1]) else None

        @block.sync
        def _(sp):
            sp.dma_start(const[:, 0:C_DFT], a["consts"][:, 0:C_DFT]).then_inc(d_const, 16)
            sp.dma_start(x[:, 0:TB, :], a["x"][0].rearrange("(k p) d -> p k d", p=128)).then_inc(d_x[0], 16)
            sp.dma_start(ctx_nat, a["ctx_1024"].rearrange("b t d -> (b t) d")).then_inc(d_l0, 16)
            for i, n in enumerate([f"L{l}_xattn_W{w}" for l in (0, 1, 3) for w in "qkvo"]):
                dst = w0t[:, 2, :] if n == "L0_xattn_Wv" else wnat[:, i, :]
                sp.dma_start(dst, a[n]).then_inc(d_l0 if i < 4 else d_wnat, 16)
                if i == 3:
                    sp.dma_start(x[:, TB:2 * TB, :], a["x"][1].rearrange("(k p) d -> p k d", p=128)).then_inc(d_x[1], 16)
            sp.dma_start(kpw_nat, a["L2_xattn_kp_w"]).then_inc(d_wnat, 16)
            for b in range(2, B):
                sp.dma_start(x[:, TB * b:TB * b + TB, :], a["x"][b].rearrange("(k p) d -> p k d", p=128)).then_inc(d_x[b], 16)
            for r in range(NQ):
                if r == QBASE[2]:
                    sp.wait_ge(q["x_done"], min(12, 4 * stages))
                    sp.dma_start(dft, a["consts"][:, C_DFT:].rearrange("p (m h) -> p m h", m=N_DFT)).then_inc(d_dft, 16)
                if r >= 2:
                    sp.wait_ge(q["stage_used"], r - 1)
                dst = stage[:, r % 2, :]
                if r == NQ0 - 1:
                    for i, w in enumerate(("gate", "up", "down")):
                        sp.dma_start(dst[:, 128 * i:128 * i + 128], a["L0_ffn_shared_" + w]).then_inc(d_stage[r % 2], 16)
                    continue
                layer = quad(r)[2]
                if layer == 2:
                    dst = dst.bitcast(BF16)[:, 0:512]
                src = QL0[r][0] if layer == 0 else QN[layer][r - QBASE[layer]][0]
                if len(src.shape) == 3:
                    dst = dst.rearrange("p (c i) -> p c i", c=src.shape[1])
                sp.dma_start(dst, src).then_inc(d_stage[r % 2], 16)
            for b in range(B):
                sp.wait_ge(q["x_done"], 20 if stages == 5 else 4 * (stages - 1) + b + 1)
                sp.dma_start(out[b].rearrange("(k p) d -> p k d", p=128), x[:, TB * b:TB * b + TB, :]).then_inc(d_out, 16)
            sp.wait_ge(d_out, 16 * B)

        SMALL = [(g_all[:, 0:4], a["g_xattn"].rearrange("(o n) -> o n", o=1).broadcast_to([128, 4])),
                 (g_all[:, 4:8], a["g_ffn"].rearrange("(o n) -> o n", o=1).broadcast_to([128, 4])),
                 (rb[:, 0:32], a["L0_ffn_gate_bias"].rearrange("(o n) -> o n", o=1).broadcast_to([128, 32])),
                 (rb[:, 32:64], a["L2_ffn_bias"].rearrange("(o n) -> o n", o=1).broadcast_to([128, 32])),
                 (rb[:, 64:80], a["L3_ffn_expert_bias"].rearrange("(o n) -> o n", o=1).broadcast_to([128, 16])),
                 (rw_nat[0:32, 0, :], a["L0_ffn_gate_w"]),
                 (rw_nat[0:8, 1, :], a["L1_ffn_router_w"]),
                 (gw2_bf[:, :], a["L2_ffn_gate_w"]),
                 (rw[:, 72:88], a["L3_ffn_router_w"]),
                 (bfc_nat, a["L1_ffn_b_fc"].rearrange("e (c h) -> (e c) h", c=4)),
                 (bproj[0:8, :], a["L1_ffn_b_proj"]),
                 (bproj[8:16, :], a["L1_ffn_b_proj"]),
                 (bproj[16:24, :], a["L1_ffn_b_proj"]),
                 (sw_bf[0:64, 0, :], a["L2_ffn_sw1"]),
                 (sw_bf[0:64, 1, :], a["L2_ffn_sw3"]),
                 (sw_bf[:, 2, 0:64], a["L2_ffn_sw2"]),
                 (w2conv[:, :], a["L2_xattn_weight"]),
                 (mask_i[:, :, :], a["mask_1x1xSxS2_ik0"].rearrange("u v (k p) t -> p (u v k) t", p=128))]
        for i, n in enumerate(("L0_xattn_bq", "L0_xattn_bk", "L0_xattn_bv", "L1_xattn_bq", "L1_xattn_bk", "L1_xattn_bv",
                               "L3_xattn_bq", "L3_xattn_bv", "L2_xattn_kp_b")):
            SMALL.append((brow[i:i + 1, :], a[n].rearrange("(o n) -> o n", o=1)))
        for i, l in enumerate((0, 1, 3)):
            SMALL.append((bo[0:1, i, :], a[f"L{l}_xattn_bo"].rearrange("(o n) -> o n", o=1)))
        SMALL = SMALL[:2] + SMALL[9:] + SMALL[2:9]
        LORA = []
        for i, w in enumerate("qkvo"):
            LORA.append((lora_a[:, i, :], a["L0_xattn_A" + w]))
            LORA.append((lora_b[:, i, :], a["L0_xattn_B" + w]))
        N_L0 = 16 * (len(LORA) + 5)
        N_SMALL = 16 * len(SMALL)

        @block.gpsimd
        def _(pool):
            pool.memset(neghalf[:, :], -0.5).then_inc(q["pool_set"], 1)
            pool.memset(e_base[:, :], float(np.e))
            pool.memset(ones_row[:, :], 1.0).then_inc(q["pool_set"], 1)
            pool.memset(ones_bf[:, :], 1.0).then_inc(q["pool_set"], 1)
            pool.memset(sw_nat[:, :, :], 0.0).then_inc(q["pool_set"], 1)
            pool.memset(gp[:, :, 4:10], LOW).then_inc(q["pool_set"], 1)
            pool.wait_ge(d_const, 16)
            pool.tensor_copy(ident_bf[:, :], ident).then_inc(q["pool_set"], 1)
            pool.tensor_copy(tri_bf[:, :], const[:, C_TRI:C_TRI + 128]).then_inc(q["pool_set"], 1)
            pool.tensor_copy(pair_sel[:, :, :], const[0:96, C_SEL:C_SEL + 32].unsqueeze(2).broadcast_to([96, 32, 64]),
                             saturate=False).then_inc(q["pool_set"], 1)
            pool.tensor_copy(sel16[:, :], const[0:48, C_SEL16:C_SEL16 + 16]).then_inc(q["pool_set"], 1)
            pool.tensor_copy(sel8[:, :], const[0:24, C_SEL8:C_SEL8 + 8]).then_inc(q["pool_set"], 1)
            def rsqrt(n):
                pool.wait_ge(q["veps_set"], n + 1)
                pool.tensor_tensor(rstd[:, :], veps[:, :], neghalf[:, :], ALU.pow).then_inc(q["rstd_set"], 1)

            pool.wait_ge(q["pool_set"], 1)
            rsqrt(0)
            rsqrt(1)
            pool.wait_ge(d_small, N_SMALL)
            pool.wait_ge(q["pool_set"], 4)
            pool.tensor_copy(sw_nat[0:64, 0:2, :], sw_bf[0:64, 0:2, :]).then_inc(q["pool_set"], 1)
            pool.tensor_copy(sw_nat[:, 2, 0:64], sw_bf[:, 2, 0:64]).then_inc(q["pool_set"], 1)
            pool.tensor_copy(rw_nat[:, 2, :], gw2_bf[:, :]).then_inc(q["pool_set"], 1)

            def split_low(r):
                slot, n, layer = quad(r)
                pool.wait_ge(q["whi_done"], r - NQ0 + 1)
                if layer == 2:
                    pool.sem_inc(q["stage_used"], 1)
                    return
                src = stage[:, r % 2, :].rearrange("p (c h) -> p c h", c=4)
                pool.tensor_tensor(wb_lo[:, slot:slot + 4, :], src, wb_hi[:, slot:slot + 4, :].bitcast(F32),
                                   ALU.subtract).then_inc(q["stage_used"], 1)

            def low(l, b, c):
                k = knum(l, b, c)
                pool.wait_ge(q["hhi_done"], k + 1)
                pool.tensor_tensor(h_lo[:, k % 3, :], hb[:, k % 4, :], h_hi[:, k % 3, :].bitcast(F32),
                                   ALU.subtract).then_inc(q["hlo_done"], 1)

            def by_heads(dst, j, b):
                src = kt1[:, j, KEYS * b:KEYS * b + KEYS].unsqueeze(1).broadcast_to([128, HEADS, KEYS])
                hm = headmask.unsqueeze(2).broadcast_to([128, HEADS, KEYS])
                return pool.tensor_tensor(dst.rearrange("p (h t) -> p h t", h=HEADS), src, hm, ALU.mult)

            def kbd(b):
                if b >= 2:
                    pool.wait_ge(q["s_ps"], 4 * (b - 1))
                by_heads(kbd1[:, b % 2, :], 0, b).then_inc(q["kbd_done"], 1)

            def vbd(b):
                if b >= 1:
                    pool.wait_ge(q["v1_ps"], b)
                by_heads(vbd1, 1, b).then_inc(q["vbd_done"], 1)

            def router_exp(b, k):
                pool.wait_ge(q["rsm_sub"], b + 1)
                ins = pool.tensor_tensor(rt[:, k, 0:8], e_base[:, :], rt[:, k, 0:8], ALU.pow)
                if k == TB - 1:
                    ins.then_inc(q["score_done"], 1)

            def count2(b):
                pool.wait_ge(q["m_done"], b + 1)
                m_ = selm[:, :, 0:32]
                if b >= 1:
                    pool.tensor_copy(run[:, 0, :], run[:, TB, :]).then_inc(q["pool"], 1)
                for t in range(TB):
                    if b or t:
                        pool.wait_ge(q["pool"], 5 * b + t)
                    pool.tensor_tensor(run[:, t + 1, :], run[:, t, :], m_[:, t, :], ALU.add).then_inc(q["pool"], 1)
                pool.tensor_copy(sel_bf[:, :, :], m_)
                pool.wait_ge(q["pool"], 5 * b + TB)
                pool.tensor_copy(run_bf[:, :, :], run[:, 0:TB, :]).then_inc(q["cum_need"], 1)

            def prob1(i):
                pool.wait_ge(q["s_rec"], i + 1)
                p = wk[:, i % 4, :].rearrange("p (h t) -> p h t", h=HEADS)
                pool.tensor_tensor(p, p, sm1[:, i % 2, :].unsqueeze(2).broadcast_to([128, HEADS, KEYS]),
                                   ALU.mult).then_inc(q["s_prob"], 1)

            for s in range(stages):
                l = s // 2
                if s == 2:
                    pool.wait_ge(q["x_done"], 8)
                    kbd(0)
                    vbd(0)
                    for i in range(16):
                        b, k = divmod(i, TB)
                        if k == 1 and b + 2 < B:
                            rsqrt(4 * s + b + 2)
                        prob1(i)
                        if k == 0 and b + 1 < B:
                            kbd(b + 1)
                        if k == 2 and b + 1 < B:
                            vbd(b + 1)
                        if i == 11:
                            rsqrt(4 * s + 4)
                    continue
                if s % 2 == 0:
                    for b in range(3 if s == 4 else 2, B):
                        rsqrt(4 * s + b)
                    if s == 0 and stages > 1:
                        rsqrt(4)
                    continue
                if l >= 2:
                    rsqrt(4 * s)
                if l == 2:
                    count2(0)
                if s == 3:
                    pool.wait_ge(q["x_done"], 8)
                    pool.wait_ge(q["prep_sb"], 10)
                    pool.tensor_copy(wa_hi[:, 48:51, :], sw_t[:, :, :]).then_inc(q["shared2"], 1)
                for b in range(B):
                    for c in range(NC[l]):
                        low(l, b, c)
                        if b + 1 < B and c == NORM_AT:
                            rsqrt(4 * s + b + 1)
                        if l == 1 and b + 1 < B and c in (6, 8, 10, 12):
                            router_exp(b + 1, (c - 6) // 2)
                        if l == 2 and b + 1 < B and c == RUN_AT:
                            count2(b + 1)
                        if b + 1 == B and s + 1 < stages:
                            for j, at in enumerate((NORM_AT, NORM2_AT, NORM3_AT)):
                                if c == at and (j < 2 or s == 3):
                                    rsqrt(4 * s + 4 + j)
                        r = split_round(l, b, c)
                        if r is not None:
                            split_low(r)

        @block.scalar
        def _(act):
            for dst, src in LORA:
                act.dma_start(dst, src).then_inc(d_l0, 16)
            for dst, src in SMALL:
                act.dma_start(dst, src).then_inc(d_small, 16)
            act.wait_ge(d_small, N_SMALL)
            act.activation(tg[:, :], g_all[:, :], ACT.Tanh).then_inc(q["act"], 1)
            act.wait_ge(q["prep_sb"], 9)
            act.activation(rw_hi[:, :], rw[:, :], ACT.Copy).then_inc(q["prep_act"], 1)

            def weights0(r):
                act.wait_ge(q["l0w_ps"], r + 1)
                slot, n, _ = quad(r)
                act.activation(wa_hi[:, slot:slot + n, :], cols4(T)[:, 0:n, :], ACT.Copy).then_inc(q["l0w_hi"], 1)

            def xf(s, b):
                act.wait_ge(q["xt_ps"], tnum(s, b))
                act.activation(xt[:, 0 if s == 2 else b % 2, :], T[:, :], ACT.Copy).then_inc(q["T_free"], 1)

            def softmax_exp(l, b):
                i = softmax_num(l, b)
                n = KW[l] * TB
                act.wait_ge(q["s_sub"], i + 1)
                act.activation(wk[:, 2 + b % 2, 0:n], wk[:, b % 2, 0:n], ACT.Exp).then_inc(q["s_exp"], 1)

            def prob_t(l, b):
                i = softmax_num(l, b)
                act.wait_ge(q["p_ps"], i + 1)
                if i >= 2:
                    act.wait_ge(q["pv_ps"], i - 1)
                act.activation(wk[0:KEYS, 4 + b % 2, :], U[b % 2][0:KEYS, :], ACT.Copy).then_inc(q["p_sb"], 1)

            def exp1(i):
                act.wait_ge(q["s_sub"], i + 1)
                act.activation(wk[:, i % 4, :], wk[:, i % 4, :], ACT.Exp).then_inc(q["s_exp"], 1)

            def prob_t1(i):
                act.wait_ge(q["p_ps"], i + 1)
                if i >= 2:
                    act.wait_ge(q["pv_ps"], i - 1)
                act.activation(wk[:, 4 + i % 2, :], W[i % 2][:, :], ACT.Copy).then_inc(q["p_sb"], 1)

            def query1(b):
                act.wait_ge(q["q1_ps"], b + 1)
                if b >= 2:
                    act.wait_ge(q["s_ps"], 4 * (b - 1))
                act.activation(q1t[:, b % 2, :], T[:, :], ACT.Identity, bias=bq1s[:, 0:1], scale=DK ** -0.5).then_inc(q["T_free"], 1)

            def value1(b):
                act.wait_ge(q["v1_ps"], b + 1)
                if b >= 2:
                    act.wait_ge(q["pv_ps"], 4 * (b - 1))
                act.activation(v1[:, b % 2, :], T[:, :], ACT.Copy).then_inc(q["T_free"], 1)

            def pre_x(l, b):
                s = 2 * l + 1
                act.wait_ge(q["xt_ps"], tnum(s, b))
                act.activation(xt_hi[:, b % 2, :], T[:, :], ACT.Copy).then_inc(q["xhi_done"], 1)

            def pre_score(l, b):
                act.wait_ge(q["logits_ps"], fnum(l, b))
                E = N_EXP[l]
                src = T[:, 0:TB * E].rearrange("p (k e) -> p k e", k=TB)
                if l == 1:
                    act.wait_ge(q["rsm_sub"], b + 1)
                    act.activation(rt[:, :, 0:E], rt[:, :, 0:E], ACT.Exp).then_inc(q["score_done"], 1)
                    return
                act.activation(rt[:, :, 0:E], src, ACT.Tanh, scale=0.5).then_inc(q["score_done"], 1)

            def pre_comb(l, b):
                rows = 3 * N_EXP[l]
                act.wait_ge(q["combt_ps"], fnum(l, b))
                act.activation(comb_t[0:rows, b % 2, :], T[:, :].bitcast(BF16)[0:rows, 0:S], ACT.Copy).then_inc(q["combt_done"], 1)

            def unit(l, b, c):
                k = knum(l, b, c)
                act.wait_ge(q["g_done"], k + 1)
                if k >= 4:
                    act.wait_ge(q["hlo_done"], k - 3)
                if l == 1:
                    act.activation(hb[:, k % 4, :], bank[k % 4][:, :], ACT.Gelu_apprx_tanh,
                                   bias=bfc[:, c:c + 1]).then_inc(q["sg_done"], 1)
                else:
                    act.activation(hb[:, k % 4, :], G[k % 2][:, :], ACT.Silu).then_inc(q["sg_done"], 1)

            def high(l, b, c):
                k = knum(l, b, c)
                act.wait_ge(q["h_done"], k + 1)
                if k >= 3:
                    act.wait_ge(q["down_done"], k - 2)
                act.activation(h_hi[:, k % 3, :], hb[:, k % 4, :], ACT.Copy).then_inc(q["hhi_done"], 1)

            def out_t(l, b):
                act.wait_ge(q["down_done"], knum(l, b, NC[l] - 1) + 1)
                act.activation(xt[:, b % 2, :], ACC[:, :], ACT.Copy).then_inc(q["outt_done"], 1)

            def split_high(r):
                slot, n, layer = quad(r)
                act.wait_ge(d_stage[r % 2], loaded(r))
                src = stage[:, r % 2, :]
                if layer == 2:
                    src = src.bitcast(BF16)[:, 0:512]
                dst = (wa_hi if layer == 2 else wb_hi)[:, slot:slot + 4, :]
                act.activation(dst, src.rearrange("p (c h) -> p c h", c=4), ACT.Copy).then_inc(q["whi_done"], 1)

            act.wait_ge(q["act"], 1)

            def project_out(b, j):
                act.wait_ge(q["z_proj"], 3 * b + j + 1)
                if j == 0:
                    ins = act.activation(hb[:, 2 * (b % 2), :], T[:, :], ACT.Identity, bias=bq0s[:, 0:1], scale=D ** -0.5)
                elif j == 1:
                    ins = act.activation(hb[:, 2 * (b % 2) + 1, :], T[:, :], ACT.Identity, bias=bcol[:, 1:2])
                else:
                    ins = act.activation(xt[:, b % 2, :], T[:, :], ACT.Copy)
                ins.then_inc(q["T_free"], 1)

            def exp0(i):
                act.wait_ge(q["z_max"], i + 1)
                if i >= 2:
                    act.wait_ge(q["z_tr"], i - 1)
                act.activation(p0[i % 2].rearrange("p (a n) -> p a n", a=2), psum[:, 2 * (i % 2):2 * (i % 2) + 2, 0:KEYS0 // 2],
                               ACT.Exp, bias=mx[:, i:i + 1], accum_out=zsum[:, i:i + 1]).then_inc(q["z_exp"], 1)

            def context_out(i):
                act.wait_ge(q["z_tr"], i + 1)
                if i >= 2:
                    act.wait_ge(q["z_pv"], i - 1)
                act.activation(ptc0[i % 2], bank[2 * (i % 2)][0:KEYS, 384:512], ACT.Copy).then_inc(q["z_pp"], 1)

            for s in range(stages):
                l = s // 2
                if s == 0:
                    xf(0, 0)
                    for j in range(3):
                        project_out(0, j)
                    exp0(0)
                    for i in range(16):
                        if i < NQ0:
                            weights0(i)
                        if i < 15:
                            exp0(i + 1)
                        context_out(i)
                        if i < 12:
                            if i % 4 == 0:
                                xf(0, i // 4 + 1)
                            else:
                                project_out(i // 4 + 1, i % 4 - 1)
                        if stages > 1:
                            if i == 13:
                                pre_x(0, 0)
                            if i == 15:
                                pre_score(0, 0)
                elif s % 2 == 0 and l in KW:
                    xf(s, 1)
                    for b in range(B + 1):
                        if b < B:
                            softmax_exp(l, b)
                        if b >= 1:
                            prob_t(l, b - 1)
                        if b + 2 < B and b + 2 >= 2:
                            act.wait_ge(q["s_ps"], softmax_num(l, b) + 1)
                            xf(s, b + 2)
                elif s == 2:
                    query1(0)
                    value1(0)
                    exp1(0)
                    for i in range(16):
                        b, k = divmod(i, TB)
                        if i + 1 < 16:
                            exp1(i + 1)
                        prob_t1(i)
                        if b + 1 < B:
                            if k == 0:
                                xf(s, b + 1)
                            if k == 1:
                                query1(b + 1)
                            if k == 3:
                                value1(b + 1)
                        if stages > 3:
                            if i == 12:
                                pre_x(1, 0)
                            if i == 15:
                                pre_score(1, 0)
                elif s == 4:
                    act.wait_ge(q["dwt_ps"], 1)
                    act.activation(xt[:, 1, :], bank[0][:, :], ACT.Copy).then_inc(q["dwt_sb"], 1)
                    for i in range(5):
                        act.wait_ge(q["w_ps"], i + 1)
                        act.activation(wk[:, i, :], bank[1 + i][:, :], ACT.Copy).then_inc(q["w_sb"], 1)
                    for i in range(2):
                        act.wait_ge(q["inv_ps"], i + 1)
                        act.activation(xt[:, i, :], bank[6 + i][:, :], ACT.Copy, scale=tg[:, 2:3]).then_inc(q["o_sb"], 1)
                else:
                    if l >= 2:
                        pre_x(l, 0)
                        pre_score(l, 0)
                    pre_comb(l, 0)
                    for b in range(B):
                        for c in range(NC[l]):
                            unit(l, b, c)
                            k = b * NC[l] + c
                            if k >= 1:
                                pb, pc = divmod(k - 1, NC[l])
                                high(l, pb, pc)
                            if c == OUT_AT and b >= 1:
                                out_t(l, b - 1)
                            if b + 1 < B:
                                if c == XHI_AT:
                                    pre_x(l, b + 1)
                                if c == SCORE_AT and l != 1:
                                    pre_score(l, b + 1)
                                if c == COMBT_AT[l]:
                                    pre_comb(l, b + 1)
                            elif s in (1, 5) and s + 1 < stages and c == XHI_AT:
                                xf(s + 1, 0)
                            r = split_round(l, b, c)
                            if r is not None:
                                split_high(r)
                    high(l, B - 1, NC[l] - 1)
                    out_t(l, B - 1)

        @block.tensor
        def _(pe):
            t_uses = [0]

            def use_t():
                if t_uses[0]:
                    pe.wait_ge(q["T_free"], t_uses[0])
                t_uses[0] += 1

            def mm(o, l, r, start, stop):
                return pe.matmul(o, l, r, start=start, stop=stop, skip_group_check=True)

            pe.wait_ge(d_const, 16)
            pe.wait_ge(d_l0, N_L0)
            b0, b1, b2, b3, b4, b5 = [bank[i] for i in range(6)]
            for j, src in enumerate((wnat[:, 0, :], wnat[:, 1, :], ctx_nat, wnat[:, 3, :])):
                last = pe.transpose(b0[:, 128 * j:128 * j + 128], src, ident)
            last.then_inc(q["prep_ps"], 1)
            for j in range(4):
                last = pe.transpose(b3[0:R, 128 * j:128 * j + 128], lora_b[:, j, :], ident)
            last.then_inc(q["prep_ps"], 1)
            pe.wait_ge(q["prep_sb"], 3)
            for j in range(4):
                l, r = (lora_bt, lora_a) if j == 2 else (lora_a, lora_bt)
                last = mm(bank[6][:, 128 * j:128 * j + 128], l[:, j, :], r[:, j, :], True, True)
            last.then_inc(q["prep_ps"], 1)
            pe.wait_ge(q["pool_set"], 13)
            pe.wait_ge(d_wnat, 16 * 9)
            pe.wait_ge(d_small, N_SMALL)
            for j, src in enumerate((wnat[:, 5, :], wnat[:, 6, :], wnat[:, 7, :], kpw_nat)):
                last = pe.transpose(b1[:, 128 * j:128 * j + 128], src, ident)
            last.then_inc(q["prep_ps"], 1)
            for j, m in enumerate((9, 10, 11, 4)):
                last = pe.transpose(b2[:, 128 * j:128 * j + 128], wnat[:, m, :], ident)
            last.then_inc(q["prep_ps"], 1)
            pe.transpose(b4[:, 0:32], rw_nat[0:32, 0, :], ident[0:32, 0:32])
            pe.transpose(b4[:, 32:40], rw_nat[0:8, 1, :], ident[0:8, 0:8])
            pe.transpose(b4[:, 40:72], rw_nat[0:32, 2, :], ident[0:32, 0:32])
            pe.transpose(b4[:, 128:160], bfc_nat[:, :], ident[0:32, 0:32])
            pe.transpose(b4[:, 160:169], brow[:, :], ident[0:9, 0:9]).then_inc(q["prep_ps"], 1)
            for j in range(3):
                last = pe.transpose(b5[:, 128 * j:128 * j + 128], sw_nat[:, j, :], ident)
            last.then_inc(q["prep_ps"], 1)
            pe.wait_ge(q["prep_sb"], 12)
            mm(bank[7][:, 0:128], w0[:, 2, :], w0[:, 3, :], True, True)
            mm(bank[7][0:1, 128:256], bcol[:, 2:3], w0[:, 3, :], True, True)
            mm(bank[7][:, 256:384], w1t[:, 0, :], ctxt, True, True)
            mm(bank[7][:, 384:512], w1t[:, 1, :], ctxt, True, True).then_inc(q["prep_ps"], 1)
            mm(b0[:, 0:128], w3t[:, 0, :], ctxt, True, True)
            mm(b0[:, 128:256], w3t[:, 1, :], ctxt, True, True)
            mm(b0[:, 256:260], w1t[:, 3, :], ctx_mean[:, :], True, True).then_inc(q["prep_ps"], 1)
            pe.wait_ge(q["prep_sb"], 19)
            mm(b1[:, 256:384], wnat[:, 8, :], kv3[:, 0, :], True, True).then_inc(q["prep_ps"], 1)
            mm(b2[0:1, 256:384], bcol[:, 6:7], kv3[:, 0, :], True, True).then_inc(q["prep_ps"], 1)
            for b in range(B):
                mm(b3[0:KEYS, 128 * b:128 * b + 128], ctxt[:, KEYS * b:KEYS * b + KEYS], w0[:, 3, :], True, False)
                last = mm(b3[0:KEYS, 128 * b:128 * b + 128], ones_row[:, 0:KEYS], bo[:, 0, :], False, True)
            last.then_inc(q["prep_ps"], 1)
            for b in range(B):
                o = b4[0:KEYS, 128 * b:128 * b + 128]
                mm(o, kv3[:, 1, KEYS * b:KEYS * b + KEYS], w3t[:, 2, :], True, False)
                last = mm(o, ones_row[:, 0:KEYS], bo[:, 2, :], False, True)
            last.then_inc(q["prep_ps"], 1)
            pe.wait_ge(q["prep_sb"], 23)

            def weights0(r):
                pe.wait_ge(d_stage[r % 2], loaded(r))
                use_t()
                for j in range(quad(r)[1]):
                    last = pe.transpose(T[:, 128 * j:128 * j + 128], stage[:, r % 2, 128 * j:128 * j + 128], ident)
                last.then_inc(q["l0w_ps"], 1)

            def xt_in(s, b):
                pe.wait_ge(q["ln_done"], 4 * s + b + 1)
                use_t()
                for k in range(TB):
                    last = pe.transpose(T[:, 128 * k:128 * k + 128], xn[:, xn_rows(s, b) + k, :], ident)
                last.then_inc(q["xt_ps"], 1)

            xf_base = {}

            def scores(l, b):
                n = KW[l]
                mat = m3
                row = crow[:, 32 * b:32 + 32 * b]
                pe.wait_ge(q["T_free"], xf_base[(2 * l, b)])
                if b >= 2:
                    pe.wait_ge(q["s_sub"], softmax_num(l, b) - 1)
                mm(G[b % 2][:, 0:TB * n].rearrange("p (k n) -> p k n", k=TB), ones_row[:, :],
                   row.unsqueeze(1).broadcast_to([1, TB, n]), True, False)
                for k in range(TB):
                    last = mm(G[b % 2][:, n * k:n * k + n], xt[:, b % 2, 128 * k:128 * k + 128], mat[:, b, :], False, k == TB - 1)
                last.then_inc(q["s_ps"], 1)

            def probs_t(l, b):
                n = KW[l]
                pe.wait_ge(q["s_prob"], softmax_num(l, b) + 1)
                if b >= 2:
                    pe.wait_ge(q["p_sb"], softmax_num(l, b) - 1)
                for k in range(TB):
                    last = pe.transpose(U[b % 2][0:n, 128 * k:128 * k + 128], wk[:, 2 + b % 2, n * k:n * k + n], ident)
                last.then_inc(q["p_ps"], 1)

            def values(l, b):
                n = KW[l]
                i = softmax_num(l, b)
                pe.wait_ge(q["p_sb"], i + 1)
                if b >= 2:
                    pe.wait_ge(q["x_done"], 4 * (2 * l) + b - 1)
                v = v3
                for k in range(TB):
                    last = mm(W[b % 2][:, 128 * k:128 * k + 128], wk[0:n, 4 + b % 2, 128 * k:128 * k + 128], v[:, b, :], True, True)
                last.then_inc(q["pv_ps"], 1)

            def query1(b):
                use_t()
                mm(T[:, :], wq1[:, :], xt[:, 0, :], True, True).then_inc(q["q1_ps"], 1)
                q1_base[b] = t_uses[0]

            def value1(b):
                pe.wait_ge(q["vbd_done"], b + 1)
                use_t()
                for j in range(4):
                    last = mm(T[:, 128 * j:128 * j + 128], vbd1[:, 128 * j:128 * j + 128], wo1t[:, :], True, True)
                last.then_inc(q["v1_ps"], 1)
                v1_base[b] = t_uses[0]

            q1_base, v1_base = {}, {}

            def scores1(i):
                b, k = divmod(i, TB)
                if k == 0:
                    pe.wait_ge(q["T_free"], q1_base[b])
                    pe.wait_ge(q["kbd_done"], b + 1)
                o = bank[i % 4]
                if i >= 4:
                    pe.wait_ge(q["s_sub"], i - 3)
                mm(o[:, :].rearrange("p (h t) -> p h t", h=HEADS), ident_bf[:, :],
                   mask_add[:, k, :].unsqueeze(1).broadcast_to([128, HEADS, KEYS]), True, False)
                mm(o[:, :], q1t[:, b % 2, 128 * k:128 * k + 128], kbd1[:, b % 2, :], False, True).then_inc(q["s_ps"], 1)

            def probs_t1(i):
                pe.wait_ge(q["s_prob"], i + 1)
                if i >= 2:
                    pe.wait_ge(q["p_sb"], i - 1)
                for j in range(4):
                    last = pe.transpose(W[i % 2][:, 128 * j:128 * j + 128], wk[:, i % 4, 128 * j:128 * j + 128], ident)
                last.then_inc(q["p_ps"], 1)

            def values1(i):
                b, k = divmod(i, TB)
                pe.wait_ge(q["p_sb"], i + 1)
                if k == 0:
                    pe.wait_ge(q["T_free"], v1_base[b])
                if k == 0 and b >= 1:
                    pe.wait_ge(q["x_done"], 8 + b)
                o = ACC[:, 128 * k:128 * k + 128]
                mm(o, ones_row[:, :], bo[:, 1, :], True, False)
                for j in range(4):
                    last = mm(o, wk[:, 4 + i % 2, 128 * j:128 * j + 128], v1[:, b % 2, 128 * j:128 * j + 128], False, j == 3)
                last.then_inc(q["pv_ps"], 1)

            def logits(l, b):
                pe.wait_ge(q["xlo_done"], fnum(l, b))
                use_t()
                E, off = N_EXP[l], (0, 32, 40, 72)[l]
                for k in range(TB):
                    o = T[:, E * k:E * k + E]
                    hi, lo = (t[:, b % 2, 128 * k:128 * k + 128] for t in (xt_hi, xt_lo))
                    rh, rl = rw_hi[:, off:off + E], rw_lo[:, off:off + E]
                    mm(o, lo, rl, True, False)
                    mm(o, lo, rh, False, False)
                    mm(o, hi, rl, False, False)
                    last = mm(o, hi, rh, False, True)
                last.then_inc(q["logits_ps"], 1)

            def running(b):
                pe.wait_ge(q["cum_need"], b + 1)
                use_t()
                o = T[:, 0:128].rearrange("p (k e) -> p k e", k=TB)
                mm(o, tri_bf[:, :], sel_bf[:, :, :], True, False)
                mm(o, ones_bf[:, :], run_bf[:, :, :], False, True).then_inc(q["cum_ps"], 1)

            def comb_in(l, b):
                rows = 3 * N_EXP[l]
                pe.wait_ge(q["comb_done"], fnum(l, b))
                use_t()
                for k in range(TB):
                    last = pe.transpose(T[:, :].bitcast(BF16)[0:rows, 128 * k:128 * k + 128], chl[:, k, 0:rows], ident_bf[:, :])
                last.then_inc(q["combt_ps"], 1)

            def gu(l, b, c):
                k = knum(l, b, c)
                gs, us, _ = slots(l, c)
                wh, wl = (wa_hi, wa_lo) if l in (0, 2) else (wb_hi, wb_lo)
                hi, lo = xt_hi[:, b % 2, :], xt_lo[:, b % 2, :]
                def product(o, s):
                    mm(o, wh[:, s, :], hi, True, False)
                    if l != 2:
                        mm(o, wl[:, s, :], hi, False, False)
                    return mm(o, wh[:, s, :], lo, False, True)

                if l == 1:
                    if k - CB[1] >= 4:
                        pe.wait_ge(q["sg_done"], k - 3)
                    product(bank[k % 4][:, :], gs).then_inc(q["g_done"], 1)
                    if c % 4 == 0:
                        e = k // 4
                        if k - CB[1] >= 8:
                            pe.wait_ge(q["h_done"], k - 4)
                        if c == 0:
                            pe.wait_ge(q["combt_done"], fnum(l, b))
                        mm(W[e % 2][:, :], sel8[:, c // 4:c // 4 + 1].broadcast_to([24, 128]),
                           comb_t[0:24, b % 2, :], True, True).then_inc(q["u_done"], 1)
                    return
                if k - CB[l] >= 2:
                    pe.wait_ge(q["sg_done"], k - 1)
                product(G[k % 2][:, :], gs).then_inc(q["g_done"], 1)
                if k - CB[l] >= 2:
                    pe.wait_ge(q["h_done"], k - 1)
                last = product(U[k % 2][:, :], us)
                if c == 0:
                    pe.wait_ge(q["combt_done"], fnum(l, b))
                if c < ROUTED[l]:
                    if N_EXP[l] == 32:
                        pick = pair_sel[:, 2 * c:2 * c + 2, :].rearrange("p e i -> p (e i)")
                    else:
                        pick = sel16[:, c:c + 1].broadcast_to([48, 128])
                    last = mm(W[k % 2][:, :], pick, comb_t[0:3 * N_EXP[l], b % 2, :], True, True)
                last.then_inc(q["u_done"], 1)

            def down(l, b, c):
                k = knum(l, b, c)
                s = slots(l, c)[2]
                wh, wl = (wa_hi, wa_lo) if l in (0, 2) else (wb_hi, wb_lo)
                if c == 0:
                    if fnum(l, b) > 4 * l + 1:
                        pe.wait_ge(q["outt_done"], fnum(l, b) - 1)
                    else:
                        pe.wait_ge(q["x_done"], 8 * l + 4)
                    if l == 1:
                        for j in range(3):
                            mm(ACC[:, :], bproj_bf[:, j, :], comb_t[0:24, b % 2, :], j == 0, False)
                pe.wait_ge(q["hlo_done"], k + 1)
                mm(ACC[:, :], wh[:, s, :], h_hi[:, k % 3, :], c == 0 and l != 1, False)
                if l != 2:
                    mm(ACC[:, :], wl[:, s, :], h_hi[:, k % 3, :], False, False)
                last = mm(ACC[:, :], wh[:, s, :], h_lo[:, k % 3, :], False, c == NC[l] - 1)
                last.then_inc(q["down_done"], 1)

            def out_back(l, b):
                pe.wait_ge(q["outt_done"], fnum(l, b))
                use_t()
                for k in range(TB):
                    last = pe.transpose(T[:, 128 * k:128 * k + 128], xt[:, b % 2, 128 * k:128 * k + 128], ident)
                last.then_inc(q["outt_ps"], 1)

            ready0 = {}

            def project(b, j):
                xb = xt[:, b % 2, :]
                use_t()
                if j < 2:
                    last = mm(T[:, :], w0[:, j, :], xb, True, True)
                else:
                    mm(cols4(T), ones_row[:, :], v0row.unsqueeze(1).broadcast_to([1, TB, 128]), True, False)
                    for k in range(TB):
                        last = mm(T[:, 128 * k:128 * k + 128], xb[:, 128 * k:128 * k + 128], w0[:, 2, :], False, k == TB - 1)
                last.then_inc(q["z_proj"], 1)
                ready0[(b, j)] = t_uses[0]

            def scores0(i):
                b, k = divmod(i, TB)
                pe.wait_ge(q["T_free"], ready0[(b, 1)])
                if i >= 2:
                    pe.wait_ge(q["z_pp"], i - 1)
                qt, kt = hb[:, 2 * (b % 2), 128 * k:128 * k + 128], hb[:, 2 * (b % 2) + 1, :]
                a0, a1 = bank[2 * (i % 2)], bank[2 * (i % 2) + 1]
                mm(a0[:, 0:272], qt, kt[:, 0:272], True, True)
                mm(a1[:, 0:240], qt, kt[:, 272:512], True, True)
                mm(a1[:, 240:272], qt, ctx0[:, KEYS * b:KEYS * b + KEYS], True, True).then_inc(q["z_s"], 1)

            def transpose0(i):
                pe.wait_ge(q["z_exp"], i + 1)
                if i >= 2:
                    pe.wait_ge(q["z_pt"], i - 1)
                for j in range(4):
                    pe.transpose(W[i % 2][:, 128 * j:128 * j + 128], p0[i % 2][:, 128 * j:128 * j + 128], ident)
                pe.transpose(bank[2 * (i % 2)][0:KEYS, 384:512], p0[i % 2][:, 512:544], ident).then_inc(q["z_tr"], 1)

            def values0(i):
                b, k = divmod(i, TB)
                pe.wait_ge(q["z_pt"], i + 1)
                pe.wait_ge(q["z_pp"], i + 1)
                pe.wait_ge(q["T_free"], ready0[(b, 2)])
                if i >= 1:
                    pe.wait_ge(q["z_up"], i)
                o = ACC[:, 0:128]
                for j in range(4):
                    mm(o, pt0[i % 2][:, 128 * j:128 * j + 128], xt[:, b % 2, 128 * j:128 * j + 128], j == 0, False)
                mm(o, ptc0[i % 2], v0c[:, b, :], False, True).then_inc(q["z_pv"], 1)

            for s in range(stages):
                l = s // 2
                if s == 0:
                    xt_in(0, 0)
                    for j in range(3):
                        project(0, j)
                    scores0(0)
                    for i in range(16):
                        if i < 15:
                            scores0(i + 1)
                        if i < NQ0:
                            weights0(i)
                        transpose0(i)
                        if i >= 1:
                            values0(i - 1)
                        if i < 12:
                            if i % 4 == 0:
                                xt_in(0, i // 4 + 1)
                            else:
                                project(i // 4 + 1, i % 4 - 1)
                        if stages > 1:
                            if i == 13:
                                xt_in(1, 0)
                            if i == 14:
                                logits(0, 0)
                    values0(15)
                elif s % 2 == 0 and l in KW:
                    xt_in(s, 1)
                    xf_base[(s, 1)] = t_uses[0]
                    scores(l, 0)
                    for b in range(B):
                        if b + 2 < B:
                            xt_in(s, b + 2)
                            xf_base[(s, b + 2)] = t_uses[0]
                        if b + 1 < B:
                            scores(l, b + 1)
                        probs_t(l, b)
                        if b >= 1:
                            values(l, b - 1)
                    values(l, B - 1)
                elif s == 2:
                    query1(0)
                    value1(0)
                    scores1(0)
                    scores1(1)
                    for i in range(16):
                        b, k = divmod(i, TB)
                        if i + 2 < 16:
                            scores1(i + 2)
                        probs_t1(i)
                        if i >= 1:
                            values1(i - 1)
                        if b + 1 < B:
                            if k == 0:
                                xt_in(2, b + 1)
                            if k == 1:
                                query1(b + 1)
                            if k == 3:
                                value1(b + 1)
                        if stages > 3:
                            if i == 12:
                                xt_in(3, 0)
                            if i == 13:
                                logits(1, 0)
                    values1(15)
                elif s == 4:
                    pe.wait_ge(q["dw_done"], 1)
                    for b in range(B):
                        last = pe.transpose(bank[0][:, 128 * b:128 * b + 128], xt[:, 0, 128 * b:128 * b + 128], ident)
                    last.then_inc(q["dwt_ps"], 1)
                    pe.wait_ge(d_dft, 16)
                    pe.wait_ge(q["dwt_sb"], 1)
                    for i, m in enumerate((FWD_RE_E, W_IM_E, W_RE_E2, FWD_RE_O, FWD_IM_O)):
                        mm(bank[1 + i][:, :], dft[:, m, :], xt[:, 1, :], True, True).then_inc(q["w_ps"], 1)
                    pe.wait_ge(q["fft_in"], 1)
                    pe.wait_ge(q["w_sb"], 5)
                    for i, (m, lo) in enumerate(((FWD_RE_E, 0), (FWD_IM_E, 0), (FWD_RE_O, 2), (FWD_IM_O, 2))):
                        mm(bank[i][:, :], dft[:, m, :], hb[:, lo, :], True, False)
                        mm(bank[i][:, :], dft[:, m + 1, :], hb[:, lo + 1, :], False, True).then_inc(q["fft_ps"], 1)
                    pe.wait_ge(q["prod_done"], 2)
                    yo = [xn4[:, 0, :], xn4[:, 2, :], hb[:, 0, :], hb[:, 2, :]]
                    for i, (bk, mr_, mi_, re, im) in enumerate(((6, INV_RE_O, INV_IM_O, yo[2], yo[3]), (7, INV_RE_O + 1, INV_IM_O + 1, yo[2], yo[3]),
                                                               (4, INV_RE_E, INV_IM_E, yo[0], yo[1]), (5, INV_RE_E + 1, INV_IM_E + 1, yo[0], yo[1]))):
                        mm(bank[bk][:, :], dft[:, mr_, :], re, True, False)
                        mm(bank[bk][:, :], dft[:, mi_, :], im, False, True).then_inc(q["inv_ps"], 1)
                else:
                    def pre(b, part):
                        if part == 0:
                            xt_in(s, b)
                        elif part == 1:
                            logits(l, b)
                        elif part == 2 and l == 2:
                            running(b)
                        elif part == 3:
                            comb_in(l, b)
                    for p in range(3 if l <= 1 else 0, 4):
                        pre(0, p)
                    pe.wait_ge(q["stage_used"], NQ if l == 3 else QBASE[l + 1])
                    if l == 2:
                        pe.wait_ge(q["shared2"], 1)
                    for c in range(AHEAD):
                        gu(l, 0, c)
                    for b in range(B):
                        for c in range(NC[l]):
                            k = b * NC[l] + c + AHEAD
                            if k < B * NC[l]:
                                gu(l, *divmod(k, NC[l]))
                            down(l, b, c)
                            if c == BACK_AT and b >= 1:
                                out_back(l, b - 1)
                            if b + 1 < B:
                                for at, p in ((XN_AT, 0), (LOGITS_AT, 1), (RUN_AT, 2), (COMB_AT[l], 3)):
                                    if c == at:
                                        pre(b + 1, p)
                            elif s in (1, 5) and s + 1 < stages and c == XN_AT:
                                xt_in(s + 1, 0)
                                xf_base[(s + 1, 0)] = t_uses[0]
                    out_back(l, B - 1)

        @block.vector
        def _(dve):
            ch_ = Chain(dve, q["dve"])
            link = ch_.link
            ps = q["prep_sb"]

            def norm(s, b):
                moments(s, b)
                scale_rows(s, b)

            def moments(s, b):
                if 4 * s + b:
                    dve.wait_ge(q["ln_done"], 4 * s + b)
                if s == 0:
                    dve.wait_ge(d_x[b], 16)
                else:
                    dve.wait_ge(q["x_done"], 4 * (s - 1) + b + 1)
                for k in range(TB):
                    last = dve.bn_stats(stats[:, k, :], x[:, TB * b + k, :])
                link(last)
                for k in range(TB):
                    last = dve.bn_aggr(mv[:, k, :], stats[:, k, :])
                link(last)
                dve.tensor_scalar(veps[:, :], mv[:, :, 1], EPS, None, ALU.add).then_inc(q["veps_set"], 1)

            def scale_rows(s, b):
                dve.wait_ge(q["rstd_set"], 4 * s + b + 1)
                before = (s, b - 2) if s != 4 and b >= 2 else (s - 1, b + 2) if b < 2 else None
                if before and before[0] >= 0 and before[0] != 4:
                    dve.wait_ge(q["xt_ps"], tnum(*before))
                for k in range(TB):
                    last = dve.tensor_scalar(xn[:, xn_rows(s, b) + k, :], x[:, TB * b + k, :], mv[:, k, 0:1], rstd[:, k:k + 1],
                                             ALU.subtract, ALU.mult)
                last.then_inc(q["ln_done"], 1)

            def shift(l, b):
                i = softmax_num(l, b)
                dve.wait_ge(q["s_ps"], i + 1)
                dve.wait_ge(q["s_sub"], i)
                if b >= 2:
                    dve.wait_ge(q["s_exp"], i - 1)
                src = G[b % 2][:, 0:TB * KEYS].rearrange("p (g n) -> p g n", g=TB)
                link(dve.tensor_reduce(mx[:, 0:TB], src, AX, ALU.max))
                dve.tensor_tensor(wk[:, b % 2, 0:TB * KEYS].rearrange("p (g n) -> p g n", g=TB), src,
                                  mx[:, 0:TB].unsqueeze(2).broadcast_to([128, TB, KEYS]), ALU.subtract).then_inc(q["s_sub"], 1)

            def normalise(l, b):
                i = softmax_num(l, b)
                p = wk[:, 2 + b % 2, 0:TB * KEYS].rearrange("p (g n) -> p g n", g=TB)
                dve.wait_ge(q["s_exp"], i + 1)
                dve.wait_ge(q["s_prob"], i)
                link(dve.tensor_reduce(sm[:, 0:TB], p, AX, ALU.add))
                link(dve.reciprocal(sm1[:, 0, 0:TB], sm[:, 0:TB]))
                dve.tensor_tensor(p, p, sm1[:, 0, 0:TB].unsqueeze(2).broadcast_to([128, TB, KEYS]), ALU.mult).then_inc(q["s_prob"], 1)

            def shift1(i):
                dve.wait_ge(q["s_ps"], i + 1)
                if i >= 1:
                    dve.wait_ge(q["s_sub"], i)
                if i >= 4:
                    dve.wait_ge(q["p_ps"], i - 3)
                src = bank[i % 4][:, :].rearrange("p (h t) -> p h t", h=HEADS)
                link(dve.tensor_reduce(mx[:, :], src, AX, ALU.max))
                dve.tensor_tensor(wk[:, i % 4, :].rearrange("p (h t) -> p h t", h=HEADS), src,
                                  mx[:, :].unsqueeze(2).broadcast_to([128, HEADS, KEYS]), ALU.subtract).then_inc(q["s_sub"], 1)

            def sums1(i):
                dve.wait_ge(q["s_exp"], i + 1)
                link(dve.tensor_reduce(sm[:, :], wk[:, i % 4, :].rearrange("p (h t) -> p h t", h=HEADS), AX, ALU.add))
                link(dve.reciprocal(sm[:, :], sm[:, :]))
                if i >= 2:
                    dve.wait_ge(q["s_prob"], i - 1)
                dve.tensor_scalar(sm1[:, i % 2, :], sm[:, :], anykeep[:, i % TB:i % TB + 1], None, ALU.mult).then_inc(q["s_rec"], 1)
                dve.wait_ge(q["s_rec"], i + 1)

            def update(s, b, src, scale):
                dve.scalar_tensor_tensor(x[:, TB * b:TB * b + TB, :], cols4(src), scale, x[:, TB * b:TB * b + TB, :],
                                         ALU.mult, ALU.add).then_inc(q["x_done"], 1)

            def lo_x(l, b):
                dve.wait_ge(q["xhi_done"], fnum(l, b))
                dve.tensor_tensor(xt_lo[:, b % 2, :], T[:, :], xt_hi[:, b % 2, :].bitcast(F32), ALU.subtract).then_inc(q["xlo_done"], 1)
                dve.wait_ge(q["xlo_done"], fnum(l, b))
                dve.sem_inc(q["T_free"], 1)

            def top(vals, n, k, marked):
                w = n + 8 - k
                if k < 8:
                    dve.memset(vals[:, :, n:w], LOW)
                for t in range(TB):
                    last = dve.max(t8[:, t, :], vals[:, t, 0:w if k == 8 else n] if n >= 8 else vals[:, t, 0:w])
                link(last)
                if k < 8:
                    link(dve.memset(t8[:, :, k:8], LOW))
                for t in range(TB):
                    last = dve.match_replace(marked[:, t, 0:w], t8[:, t, :], vals[:, t, 0:w], TAKEN)
                link(last)

            def route_shift(l, b):
                if l == 1:
                    E = N_EXP[l]
                    s_ = rt[:, :, 0:E]
                    dve.wait_ge(q["logits_ps"], fnum(l, b))
                    src = T[:, 0:TB * E].rearrange("p (k e) -> p k e", k=TB)
                    link(dve.tensor_reduce(wsum[:, :], src, AX, ALU.max))
                    dve.tensor_tensor(s_, src, wsum[:, :].unsqueeze(2).broadcast_to([128, TB, E]), ALU.subtract).then_inc(q["rsm_sub"], 1)

            def route(l, b):
                for part in (route_scores, route_groups, route_top, route_weigh):
                    part(l, b)

            def route_scores(l, b):
                E = N_EXP[l]
                s_ = rt[:, :, 0:E]
                c_ = ch[:, :, 0:E]
                if fnum(l, b) > 1:
                    dve.wait_ge(q["comb_done"], fnum(l, b) - 1)
                if l == 1:
                    dve.wait_ge(q["score_done"], fnum(l, b))
                    dve.sem_inc(q["T_free"], 1)
                    link(dve.tensor_reduce(wsum[:, :], s_, AX, ALU.add))
                    link(dve.reciprocal(wrec[:, :], wsum[:, :]))
                    link(dve.tensor_tensor(c_, s_, wrec[:, :].unsqueeze(2).broadcast_to([128, TB, E]), ALU.mult))
                    s_ = c_
                else:
                    dve.wait_ge(q["score_done"], fnum(l, b))
                    dve.sem_inc(q["T_free"], 1)
                    off = {0: 0, 2: 32, 3: 64}[l]
                    link(dve.tensor_scalar(s_, s_, 0.5, 0.5, ALU.mult, ALU.add))
                    link(dve.tensor_tensor(c_, s_, rb[:, off:off + E].unsqueeze(1).broadcast_to([128, TB, E]), ALU.add))

            def route_groups(l, b):
                c_ = ch[:, :, 0:N_EXP[l]]
                if l == 0:
                    v = ch[:, :, 0:32].rearrange("p k (g j) -> p k g j", g=4)
                    u = tour[:, :, :].rearrange("p (k g) j -> p k g j", k=TB)
                    dve.tensor_tensor(u[:, :, :, 0:4], v[:, :, :, 0:4], v[:, :, :, 4:8], ALU.max)
                    link(dve.tensor_tensor(u[:, :, :, 4:8], v[:, :, :, 0:4], v[:, :, :, 4:8], ALU.min))
                    for first, second, n, o in ((0, 4, 2, 8), (8, 10, 1, 12)):
                        f0, f1 = u[:, :, :, first:first + n], u[:, :, :, first + n:first + 2 * n]
                        s0, s1 = u[:, :, :, second:second + n], u[:, :, :, second + n:second + 2 * n]
                        dve.tensor_tensor(u[:, :, :, o:o + n], f0, f1, ALU.max)
                        dve.tensor_tensor(u[:, :, :, 14:14 + n], f0, f1, ALU.min)
                        link(dve.tensor_tensor(u[:, :, :, o + n:o + 2 * n], s0, s1, ALU.max))
                        link(dve.tensor_tensor(u[:, :, :, o + n:o + 2 * n], u[:, :, :, o + n:o + 2 * n], u[:, :, :, 14:14 + n], ALU.max))
                    link(dve.tensor_tensor(gp[:, :, 0:4], u[:, :, :, 12], u[:, :, :, 13], ALU.add))
                    for t in range(TB):
                        last = dve.max(t8[:, t, :], gp[:, t, :])
                    link(last)
                    link(dve.memset(t8[:, :, 2:8], LOW))
                    for t in range(TB):
                        last = dve.match_replace(gr[:, t, :], t8[:, t, :], gp[:, t, :], TAKEN)
                    link(last)
                    link(dve.tensor_scalar(gm[:, :, :], gr[:, :, 0:4], TAKEN / 2, None, ALU.is_gt))
                    link(dve.tensor_tensor(v, v, gm[:, :, :].unsqueeze(3).broadcast_to([128, TB, 4, 8]), ALU.mult))
                    link(dve.tensor_scalar(c_, c_, 0.0, None, ALU.add))

            def route_top(l, b):
                top(ch, N_EXP[l], TOP_K[l], mr)

            def route_weigh(l, b):
                E = N_EXP[l]
                s_ = (ch if l == 1 else rt)[:, :, 0:E]
                m_ = selm[:, :, 0:E]
                last = dve.tensor_scalar(m_, mr[:, :, 0:E], TAKEN / 2, None, ALU.is_gt)
                link(last)
                if l == 2:
                    dve.sem_inc(q["m_done"], 1)
                w_ = wsel[:, :, 0:E]
                link(dve.tensor_tensor(w_, m_, s_, ALU.mult))
                if l != 3:
                    link(dve.tensor_reduce(wsum[:, :], w_, AX, ALU.add))
                    if l == 0:
                        link(dve.tensor_scalar(wsum[:, :], wsum[:, :], 1e-20, None, ALU.add))
                    if l == 2:
                        link(dve.tensor_scalar(wsum[:, :], wsum[:, :], 1e-12, None, ALU.max))
                    link(dve.reciprocal(wrec[:, :], wsum[:, :]))
                    if l == 0:
                        link(dve.tensor_scalar(wrec[:, :], wrec[:, :], 2.5, None, ALU.mult))
                    link(dve.tensor_tensor(w_, w_, wrec[:, :].unsqueeze(2).broadcast_to([128, TB, E]), ALU.mult))

            def route_end(l, b):
                E = N_EXP[l]
                m_, w_ = selm[:, :, 0:E], wsel[:, :, 0:E]
                if l == 2:
                    dve.wait_ge(q["cum_ps"], b + 1)
                    cum = T[:, 0:128].rearrange("p (k e) -> p k e", k=TB)
                    link(dve.tensor_scalar(m_, cum, CAPACITY + 0.5, None, ALU.is_lt))
                    dve.sem_inc(q["T_free"], 1)
                    link(dve.tensor_tensor(w_, w_, m_, ALU.mult))
                for j in range(2):
                    link(dve.tensor_copy(chl[:, :, E * j:E * j + E], w_))
                    rest = w_ if j == 0 else chl[:, :, 2 * E:3 * E]
                    last = dve.tensor_tensor(rest, w_, chl[:, :, E * j:E * j + E], ALU.subtract)
                    if j == 0:
                        link(last)
                last.then_inc(q["comb_done"], 1)

            def combt_free(l, b):
                dve.wait_ge(q["combt_done"], fnum(l, b))
                dve.sem_inc(q["T_free"], 1)

            def mult(l, b, c):
                k = knum(l, b, c)
                h = hb[:, k % 4, :]
                dve.wait_ge(q["sg_done"], k + 1)
                if l == 1:
                    dve.wait_ge(q["u_done"], UB[1] + (k - CB[1]) // 4 + 1)
                    dve.tensor_tensor(h, h, W[(k // 4) % 2][:, :], ALU.mult).then_inc(q["h_done"], 1)
                    return
                dve.wait_ge(q["u_done"], UB[l] + k - CB[l] + 1)
                if c < ROUTED[l]:
                    link(dve.tensor_tensor(h, h, U[k % 2][:, :], ALU.mult))
                    dve.tensor_tensor(h, h, W[k % 2][:, :], ALU.mult).then_inc(q["h_done"], 1)
                else:
                    dve.tensor_tensor(h, h, U[k % 2][:, :], ALU.mult).then_inc(q["h_done"], 1)

            def weights0(r):
                slot, n, _ = quad(r)
                dve.wait_ge(q["l0w_hi"], r + 1)
                dve.tensor_tensor(wa_lo[:, slot:slot + n, :], cols4(T)[:, 0:n, :], wa_hi[:, slot:slot + n, :].bitcast(F32),
                                  ALU.subtract).then_inc(q["l0w_lo"], 1)
                dve.wait_ge(q["l0w_lo"], r + 1)
                dve.sem_inc(q["T_free"], 1)
                dve.sem_inc(q["stage_used"], 1)

            def max0(i):
                dve.wait_ge(q["z_s"], i + 1)
                dve.tensor_reduce(mx[:, i:i + 1], psum[:, 2 * (i % 2):2 * (i % 2) + 2, 0:KEYS0 // 2], mybir.AxisListType.XY,
                                  ALU.max, negate=True).then_inc(q["z_max"], 1)

            def probs0_out(i):
                dve.wait_ge(q["z_tr"], i + 1)
                if i >= 2:
                    dve.wait_ge(q["z_pv"], i - 1)
                dve.tensor_copy(pt0[i % 2], W[i % 2][:, :]).then_inc(q["z_pt"], 1)

            def update0(i):
                dve.wait_ge(q["z_pv"], i + 1)
                if i:
                    dve.wait_ge(q["z_up"], i)
                link(dve.reciprocal(sm1[:, 0, 0:1], zsum[:, i:i + 1]))
                link(dve.tensor_scalar(sm[:, 0:1], sm1[:, 0, 0:1], tg[:, 0:1], None, ALU.mult))
                dve.scalar_tensor_tensor(x[:, i, :], ACC[:, 0:128], sm[:, 0:1], x[:, i, :],
                                         ALU.mult, ALU.add).then_inc(q["z_up"], 1)
                if i % TB == TB - 1:
                    dve.wait_ge(q["z_up"], i + 1)
                    dve.sem_inc(q["x_done"], 1)

            dve.wait_ge(q["prep_ps"], 1)
            dve.tensor_copy(w0t[:, 0:4:3, :], cols4(bank[0])[:, 0:4:3, :])
            dve.tensor_copy(w0t[:, 1, :], bank[0][:, 128:256]).then_inc(ps, 1)
            dve.tensor_copy(ctxt, bank[0][:, 256:384]).then_inc(ps, 1)
            dve.wait_ge(q["prep_ps"], 2)
            dve.tensor_copy(lora_bt[:, :, :], cols4(bank[3])[0:R]).then_inc(ps, 1)
            norm(0, 0)
            dve.wait_ge(q["prep_ps"], 3)
            dve.scalar_tensor_tensor(w0, cols4(bank[6]), 2.0, w0t, ALU.mult, ALU.add).then_inc(ps, 1)
            norm(0, 1)
            dve.wait_ge(q["prep_ps"], 5)
            dve.tensor_copy(w1t, cols4(bank[1])).then_inc(ps, 1)
            dve.tensor_copy(wq1[:, :], bank[2][:, 384:512])
            dve.tensor_copy(w3t, cols4(bank[2])[:, 0:3, :]).then_inc(ps, 1)
            dve.wait_ge(q["prep_ps"], 7)
            dve.tensor_copy(rw[:, 0:72], bank[4][:, 0:72]).then_inc(ps, 1)
            dve.tensor_copy(bfc[:, :], bank[4][:, 128:160]).then_inc(ps, 1)
            dve.tensor_copy(bcol[:, :], bank[4][:, 160:169]).then_inc(ps, 1)
            dve.tensor_copy(sw_t[:, :, :], cols4(bank[5])[:, 0:3, :]).then_inc(ps, 1)
            dve.wait_ge(ps, 2)
            dve.tensor_reduce(ctx_mean[:, :], ctxt.rearrange("p (b t) -> p b t", b=B), AX, ALU.add).then_inc(q["dve"], 1)
            ch_.n += 1
            dve.wait_ge(q["dve"], ch_.n)
            link(dve.tensor_scalar(ctx_mean[:, :], ctx_mean[:, :], 1.0 / KEYS, None, ALU.mult))
            dve.wait_ge(ps, 10)
            dve.tensor_copy(wo1t[:, :], w1t[:, 2, :])
            dve.tensor_copy(ctx0, ctxt).then_inc(ps, 1)
            dve.tensor_scalar(bq1s[:, :], bcol[:, 3:4], DK ** -0.5, None, ALU.mult)
            dve.tensor_scalar(bq0s[:, :], bcol[:, 0:1], D ** -0.5, None, ALU.mult).then_inc(ps, 1)
            dve.wait_ge(q["prep_ps"], 8)
            dve.tensor_copy(w0[:, 2, :], bank[7][:, 0:128]).then_inc(ps, 1)
            dve.tensor_tensor(v0row, bank[7][0:1, 128:256], bo[:, 0, :], ALU.add).then_inc(ps, 1)
            dve.tensor_scalar(kt1[:, 0, :], bank[7][:, 256:384], bcol[:, 4:5], None, ALU.add).then_inc(ps, 1)
            dve.tensor_scalar(kt1[:, 1, :], bank[7][:, 384:512], bcol[:, 5:6], None, ALU.add).then_inc(ps, 1)
            dve.wait_ge(q["prep_ps"], 9)
            dve.tensor_copy(kv3[:, 0, :], bank[0][:, 0:128]).then_inc(ps, 1)
            dve.tensor_scalar(kv3[:, 1, :], bank[0][:, 128:256], bcol[:, 7:8], None, ALU.add).then_inc(ps, 1)
            dve.tensor_scalar(kmod[:, :], bank[0][:, 256:260], bcol[:, 8:9], None, ALU.add).then_inc(ps, 1)
            dve.wait_ge(q["prep_ps"], 10)
            sc = D ** -0.5
            dve.tensor_scalar(m3[:, :, :], bank[1][:, 256:384].rearrange("p (b n) -> p b n", b=B), sc, None, ALU.mult).then_inc(ps, 1)
            dve.wait_ge(q["prep_ps"], 11)
            dve.tensor_scalar(crow[:, :], bank[2][0:1, 256:384], sc, None, ALU.mult).then_inc(ps, 1)
            dve.wait_ge(q["prep_ps"], 13)
            dve.tensor_copy(v0c, cols4(bank[3])[0:KEYS]).then_inc(ps, 1)
            dve.tensor_copy(v3[:, :, :], cols4(bank[4])[0:KEYS]).then_inc(ps, 1)
            for j in range(3):
                link(dve.tensor_copy(bproj_bf[:, j, :], bproj))
                if j < 2:
                    link(dve.tensor_tensor(bproj, bproj, bproj_bf[:, j, :], ALU.subtract))
            link(dve.tensor_scalar(mask_add[:, :, :], mask_i[:, :, :], 0.0, NO_KEY, ALU.is_equal, ALU.mult))
            link(dve.tensor_reduce(anykeep[:, :], mask_add[:, :, :], AX, ALU.max))
            link(dve.tensor_scalar(anykeep[:, :], anykeep[:, :], NO_KEY / 2, None, ALU.is_gt))
            dve.wait_ge(q["prep_act"], 1)
            dve.tensor_tensor(rw_lo[:, :], rw[:, :], rw_hi[:, :].bitcast(F32), ALU.subtract)
            link(dve.memset(run[:, :, :], 0.0))

            dve.wait_ge(q["act"], 1)
            for s in range(stages):
                l = s // 2
                if s == 0:
                    max0(0)
                    for i in range(16):
                        if i < 15:
                            max0(i + 1)
                        if i < NQ0:
                            weights0(i)
                        if stages > 1 and i == 14:
                            lo_x(0, 0)
                        probs0_out(i)
                        if i >= 1:
                            update0(i - 1)
                        if i % 4 == 2 and i < 8:
                            norm(0, i // 4 + 2)
                        if stages > 1:
                            if i == 9:
                                moments(1, 0)
                            if i == 10:
                                scale_rows(1, 0)
                            if i == 15:
                                route_scores(0, 0)
                    update0(15)
                    if stages > 1:
                        route_groups(0, 0)
                        route_top(0, 0)
                        route_weigh(0, 0)
                        route_end(0, 0)
                elif s % 2 == 0 and l in KW:
                    shift(l, 0)
                    for b in range(B):
                        if b + 2 < B:
                            norm(s, b + 2)
                        if b + 1 < B:
                            shift(l, b + 1)
                        normalise(l, b)
                        if b >= 1:
                            dve.wait_ge(q["pv_ps"], softmax_num(l, b))
                            update(s, b - 1, W[(b - 1) % 2], tg[:, l:l + 1])
                    dve.wait_ge(q["pv_ps"], softmax_num(l, B - 1) + 1)
                    update(s, B - 1, W[(B - 1) % 2], tg[:, l:l + 1])
                elif s == 2:
                    shift1(0)
                    for i in range(16):
                        b, k = divmod(i, TB)
                        if i + 1 < 16:
                            shift1(i + 1)
                        if k == 1 and b >= 1:
                            dve.wait_ge(q["pv_ps"], 4 * b)
                            update(s, b - 1, ACC, tg[:, 1:2])
                        if k == 1 and b + 2 < B:
                            moments(s, b + 2)
                        if k == 2 and b + 2 < B:
                            scale_rows(s, b + 2)
                        if stages > 3 and i == 13:
                            lo_x(1, 0)
                        sums1(i)
                        if stages > 3:
                            if i == 10:
                                moments(3, 0)
                            if i == 11:
                                scale_rows(3, 0)
                            if i == 14:
                                route_shift(1, 0)
                            if i == 15:
                                route_scores(1, 0)
                                route_top(1, 0)
                                route_weigh(1, 0)
                                route_end(1, 0)
                    dve.wait_ge(q["pv_ps"], 16)
                    update(s, 3, ACC, tg[:, 1:2])
                elif s == 4:
                    for b in range(B):
                        dve.tensor_scalar(xt[:, 0, 128 * b:128 * b + 128], w2conv[:, :], kmod[:, b:b + 1], None, ALU.mult) if b < B - 1 else \
                            dve.tensor_scalar(xt[:, 0, 128 * b:128 * b + 128], w2conv[:, :], kmod[:, b:b + 1], None, ALU.mult).then_inc(q["dw_done"], 1)
                    norm(s, 3)
                    dve.wait_ge(q["ln_done"], 4 * s + B)
                    blk = xn[:, :, :].rearrange("p (b k) d -> p b k d", b=B)
                    hv = hb[:, :, :].rearrange("p m (b d) -> p m b d", b=B)
                    dve.tensor_tensor(hv[:, 0], blk[:, :, 0, :], blk[:, :, 2, :], ALU.add)
                    dve.tensor_tensor(hv[:, 1], blk[:, :, 1, :], blk[:, :, 3, :], ALU.add)
                    dve.tensor_tensor(hv[:, 2], blk[:, :, 0, :], blk[:, :, 2, :], ALU.subtract)
                    dve.tensor_tensor(hv[:, 3], blk[:, :, 1, :], blk[:, :, 3, :], ALU.subtract).then_inc(q["fft_in"], 1)
                    dve.wait_ge(q["w_sb"], 5)
                    dve.wait_ge(q["fft_in"], 1)
                    for par in range(2):
                        y = xn4 if par == 0 else hb
                        xr, xi = bank[2 * par], bank[2 * par + 1]
                        wr, wi, wr2 = (wk[:, 0, :], wk[:, 1, :], wk[:, 2, :]) if par == 0 else (wk[:, 3, :], wk[:, 4, :], wk[:, 3, :])
                        dve.wait_ge(q["fft_ps"], 4 if par == 1 else 2)
                        dve.tensor_tensor(y[:, 0, :], wr, xr[:, :], ALU.mult)
                        dve.tensor_tensor(y[:, 1, :], wi, xi[:, :], ALU.mult)
                        dve.tensor_tensor(y[:, 2, :], wi, xr[:, :], ALU.mult)
                        link(dve.tensor_tensor(y[:, 3, :], wr2, xi[:, :], ALU.mult))
                        dve.tensor_tensor(y[:, 0, :], y[:, 0, :], y[:, 1, :], ALU.subtract)
                        dve.tensor_tensor(y[:, 2, :], y[:, 2, :], y[:, 3, :], ALU.add).then_inc(q["prod_done"], 1)
                    xv = x[:, :, :].rearrange("p (b k) d -> p b k d", b=B)
                    g2 = tg[:, 2:3]
                    dve.wait_ge(q["inv_ps"], 4)
                    for k in range(4):
                        e = bank[4 + k % 2][:, :].rearrange("p (b d) -> p b d", b=B)
                        last = dve.scalar_tensor_tensor(xv[:, :, k, :], e, g2, xv[:, :, k, :], ALU.mult, ALU.add)
                    link(last)
                    dve.wait_ge(q["o_sb"], 2)
                    for k in range(4):
                        o = xt[:, k % 2, :].rearrange("p (b d) -> p b d", b=B)
                        dve.tensor_tensor(xv[:, :, k, :], xv[:, :, k, :], o, ALU.add if k < 2 else ALU.subtract).then_inc(q["x_done"], 1)
                    dve.wait_ge(q["x_done"], 20)
                else:
                    if l >= 2:
                        norm(s, 0)
                        lo_x(l, 0)
                        route(l, 0)
                        route_end(l, 0)
                    combt_free(l, 0)
                    for b in range(B):
                        for c in range(NC[l]):
                            mult(l, b, c)
                            if c == ADD_AT and b >= 1:
                                dve.wait_ge(q["outt_ps"], fnum(l, b - 1))
                                update(s, b - 1, T, tg[:, 4 + l:5 + l])
                                dve.wait_ge(q["x_done"], 4 * s + b)
                                dve.sem_inc(q["T_free"], 1)
                            if b + 1 < B:
                                if c == NORM_AT:
                                    moments(s, b + 1)
                                if c == XN_AT:
                                    scale_rows(s, b + 1)
                                if c == XLO_AT:
                                    lo_x(l, b + 1)
                                if c == SCORE_AT:
                                    route_shift(l, b + 1)
                                if c == ROUTE_AT[l]:
                                    route_scores(l, b + 1)
                                if c == ROUTE_AT[l] + 1:
                                    route_groups(l, b + 1)
                                if c == ROUTE_AT[l] + 2:
                                    route_top(l, b + 1)
                                if c == ROUTE_AT[l] + 3:
                                    route_weigh(l, b + 1)
                                if c == WEIGH_AT[l]:
                                    route_end(l, b + 1)
                                if c == COMBT_AT[l]:
                                    combt_free(l, b + 1)
                            elif s + 1 < stages:
                                for j, (at, xn_at) in enumerate(((NORM_AT, XN_AT), (NORM2_AT, XN2_AT), (NORM3_AT, XN3_AT))):
                                    if j < 2 or s == 3:
                                        if c == at:
                                            moments(s + 1, j)
                                        if c == xn_at:
                                            scale_rows(s + 1, j)
                    dve.wait_ge(q["outt_ps"], fnum(l, B - 1))
                    update(s, B - 1, T, tg[:, 4 + l:5 + l])
                    dve.wait_ge(q["x_done"], 4 * s + B)
                    dve.sem_inc(q["T_free"], 1)
    return nc


def _inputs():
    return ["x", "ctx_1024", "mask_1x1xSxS2_ik0", "g_xattn", "g_ffn"] + [
        f"L0_xattn_{k}{w}" for w in "qkvo" for k in "WbAB"] + [
        "L0_ffn_" + n for n in ("gate_w", "gate_bias", "expert_gate", "expert_up", "expert_down", "shared_gate", "shared_up", "shared_down")] + [
        f"L1_xattn_{k}{w}" for w in "qkvo" for k in "Wb"] + [
        "L1_ffn_" + n for n in ("router_w", "w_fc", "b_fc", "w_proj", "b_proj")] + [
        "L2_xattn_" + n for n in ("weight", "kp_w", "kp_b")] + [
        "L2_ffn_" + n for n in ("gate_w", "bias", "W1", "W3", "W2", "sw1", "sw3", "sw2")] + [
        "L3_xattn_" + n for n in ("Wk", "Wv", "bv", "Wq", "bq", "Wo", "bo")] + [
        "L3_ffn_" + n for n in ("router_w", "expert_bias", "shared_w1", "shared_w2", "shared_w3", "routed_w1", "routed_w2", "routed_w3")]


STAGES = 8


def kernel(**inputs):
    import concourse.bacc as bacc
    from concourse.bass_utils import run_bass_kernel_spmd

    nc = bacc.Bacc("TRN2", target_bir_lowering=False, num_devices=1)
    arrays, a = {}, {}
    for name in _inputs():
        arrays["in_" + name] = np.ascontiguousarray(inputs[name])
    arrays["in_consts"] = constants()
    for name, v in arrays.items():
        a[name[3:]] = nc.dram_tensor(name, v.shape, mybir.dt.from_np(v.dtype), kind="ExternalInput").ap()
    out = nc.dram_tensor("out", (B, S, D), F32, kind="ExternalOutput").ap()
    build(nc, a, out, STAGES)
    r = run_bass_kernel_spmd(nc, [arrays], core_ids=[0])
    return r.results[0]["out"]
```

```python
from contextlib import ExitStack

import concourse.bass as bass
import numpy as np
from concourse import mybir

F32 = mybir.dt.float32
F32R = mybir.dt.float32r
BF16 = mybir.dt.bfloat16
I32 = mybir.dt.int32
ALU = mybir.AluOpType
ACT = mybir.ActivationFunctionType
AX = mybir.AxisListType.X

B, S, D = 4, 512, 128
TB = S // 128
KEYS = 32
HEADS, DK = 16, 8
R = 8
NO_KEY = -1.0e30
LOW, TAKEN = -3.0e38, 3.0e38
EPS = 1e-5
STAGES = 8
N_EXP = [32, 8, 32, 16]
TOP_K = [8, 2, 4, 2]
ROUTED = [16, 32, 16, 16]
SHARED = [1, 0, 1, 4]
NC = [r + s for r, s in zip(ROUTED, SHARED)]
CB = [B * sum(NC[:l]) for l in range(5)]
CAPACITY = 2 * 512 * 4 // 32
UB = [0, CB[1], CB[1] + B * 8, CB[1] + B * 8 + B * NC[2]]

C_ID, C_HEAD, C_TRI, C_SEL, C_SEL16, C_SEL8, C_DFT = 0, 128, 144, 272, 304, 320, 328
FWD_RE_E, FWD_IM_E, FWD_RE_O, FWD_IM_O, W_IM_E, W_RE_E2, INV_RE_E, INV_IM_E, INV_RE_O, INV_IM_O = 0, 2, 4, 6, 8, 9, 10, 12, 14, 16
N_DFT = 18
C_ALL = C_DFT + N_DFT * 128


def constants():
    c = np.zeros((128, C_ALL), np.float64)
    i = np.arange(128)
    c[:, C_ID:C_ID + 128] = np.eye(128)
    c[:, C_HEAD:C_HEAD + HEADS] = (i[:, None] // DK) == np.arange(HEADS)[None]
    c[:, C_TRI:C_TRI + 128] = i[:, None] <= i[None]
    c[0:96, C_SEL:C_SEL + 32] = (i[:96, None] % 32) == np.arange(32)[None]
    c[0:48, C_SEL16:C_SEL16 + 16] = (i[:48, None] % 16) == np.arange(16)[None]
    c[0:24, C_SEL8:C_SEL8 + 8] = (i[:24, None] % 8) == np.arange(8)[None]
    m = c[:, C_DFT:].reshape(128, N_DFT, 128)
    h = i[None]
    for blk in range(2):
        n = (i + 128 * blk)[:, None]
        even, odd = 2 * np.pi * n * (2 * h) / 512, 2 * np.pi * n * (2 * h + 1) / 512
        m[:, FWD_RE_E + blk], m[:, FWD_RE_O + blk], m[:, FWD_IM_O + blk] = np.cos(even), np.cos(odd), -np.sin(odd)
        m[:, FWD_IM_E + blk] = -np.sin(even)
        m[:, FWD_IM_E + blk, 0] = (-1.0) ** n[:, 0]
        m[:, INV_RE_E + blk], m[:, INV_IM_E + blk] = 2 / 512 * np.cos(even).T, -2 / 512 * np.sin(even).T
        m[0, INV_RE_E + blk] = 1 / 512
        m[0, INV_IM_E + blk] = (-1.0) ** n[:, 0] / 512
        m[:, INV_RE_O + blk], m[:, INV_IM_O + blk] = 2 / 512 * np.cos(odd).T, -2 / 512 * np.sin(odd).T
    m[:, W_IM_E] = m[:, FWD_IM_E]
    m[:, W_IM_E, 0] = 0
    m[:, W_RE_E2] = m[:, FWD_RE_E]
    m[:, W_RE_E2, 0] = (-1.0) ** i
    return c.astype(np.float32)


class Chain:

    def __init__(self, eng, sem):
        self.eng, self.sem, self.n = eng, sem, 0

    def link(self, ins):
        self.n += 1
        ins.then_inc(self.sem, 1)
        self.eng.wait_ge(self.sem, self.n)


def build(nc, a, out):
    with ExitStack() as ctx:
        def sb(name, shape, dt=F32):
            return ctx.enter_context(nc.sbuf_tensor(name, shape, dt))

        def sem(name):
            return ctx.enter_context(nc.semaphore(name))

        psum = ctx.enter_context(nc.psum_tensor("psum", [128, 8, 512], F32))
        bank = [psum[:, i, :] for i in range(8)]
        G, U, W, ACC, T = bank[0:2], bank[2:4], bank[4:6], bank[6], bank[7]

        const = sb("const", [128, C_ALL])
        ident = const[:, C_ID:C_ID + 128]
        headmask = const[:, C_HEAD:C_HEAD + HEADS]
        dft = const[:, C_DFT:].rearrange("p (m h) -> p m h", m=N_DFT)
        ident_bf = sb("ident_bf", [128, 128], BF16)
        tri_bf = sb("tri_bf", [128, 128], BF16)
        ones_bf = sb("ones_bf", [128, 128], BF16)
        ones_row = sb("ones_row", [1, 128])
        pair_sel = sb("pair_sel", [96, 32, 64], mybir.dt.float8e4)
        sel16 = sb("sel16", [48, 16], BF16)
        sel8 = sb("sel8", [24, 8], BF16)
        neghalf = sb("neghalf", [128, TB])
        e_base = sb("e_base", [128, 8])
        x = sb("x", [128, B * TB, D])
        xn = sb("xn", [128, B * TB, D])
        xt = sb("xt", [128, 2, S])
        xt_hi = sb("xt_hi", [128, 2, S], F32R)
        xt_lo = sb("xt_lo", [128, 2, S], F32R)
        wa_hi = sb("wa_hi", [128, 51, 128], F32R)
        wa_lo = sb("wa_lo", [128, 51, 128], F32R)
        wb_hi = sb("wb_hi", [128, 64, 128], F32R)
        wb_lo = sb("wb_lo", [128, 64, 128], F32R)
        stage = sb("stage", [128, 2, 512])
        hb = sb("hb", [128, 4, 512])
        h_hi = sb("h_hi", [128, 3, 512], F32R)
        h_lo = sb("h_lo", [128, 3, 512], F32R)
        comb_t = sb("comb_t", [96, 2, S], BF16)
        wk = sb("wk", [128, 6, 512])
        g_all = sb("g_all", [128, 8])
        tg = sb("tg", [128, 8])
        rb = sb("rb", [128, 80])
        rw_hi = sb("rw_hi", [128, 88], F32R)
        rw_lo = sb("rw_lo", [128, 88], F32R)
        bfc = sb("bfc", [128, 32])
        bproj_bf = sb("bproj_bf", [24, 3, 128], BF16)
        sw_t = sb("sw_t", [128, 3, 128], BF16)
        bcol = sb("bcol", [128, 9])
        bo = sb("bo", [1, 3, 128])
        m3 = const[:, C_TRI:C_TRI + 128].rearrange("p (b n) -> p b n", b=B)
        v3 = sb("v3", [32, B, 128])
        crow = sb("crow", [1, 128])
        kmod = sb("kmod", [128, B])
        ctx_mean = sb("ctx_mean", [128, B])
        w2conv = sb("w2conv", [128, 128])
        mask_add = sb("mask_add", [128, TB, KEYS], BF16)
        anykeep = sb("anykeep", [128, TB])
        stats = sb("stats", [128, TB, 6])
        mv = sb("mv", [128, TB, 2])
        veps = sb("veps", [128, TB])
        rstd = sb("rstd", [128, TB])
        mx = const[:, C_SEL16:C_SEL16 + 16]
        zsum = sb("zsum", [128, 16])
        bq0s = sb("bq0s", [128, 1])
        bq1s = sb("bq1s", [128, 1])
        tgn = sb("tgn", [128, 1])
        sm = sb("sm", [128, 16])
        sm1 = const[:, C_SEL:C_SEL + 32].rearrange("p (i h) -> p i h", i=2)
        rt = sb("rt", [128, TB, 32])
        ch = sb("ch", [128, TB, 38])
        mr = sb("mr", [128, TB, 38])
        t8 = sb("t8", [128, TB, 8])
        chosen = sb("chosen", [128, 256])
        mask_i = chosen[:, 0:128].bitcast(I32).rearrange("p (k t) -> p k t", k=TB)
        tour = chosen[:, :].rearrange("p (g j) -> p g j", g=16)
        gp = sb("gp", [128, TB, 10])
        gr = sb("gr", [128, TB, 10])
        gm = sb("gm", [128, TB, 4])
        selm = chosen[:, 0:128].rearrange("p (k e) -> p k e", k=TB)
        wsel = chosen[:, 128:256].rearrange("p (k e) -> p k e", k=TB)
        wsum = sb("wsum", [128, TB])
        wrec = sb("wrec", [128, TB])
        chl = sb("chl", [128, TB, 96], BF16)
        sel_bf = sb("sel_bf", [128, TB, 32], BF16)
        run_bf = sb("run_bf", [128, TB, 32], BF16)
        run = sb("run", [128, TB + 1, 32])

        d_const, d_dft, d_small, d_l0, d_wnat, d_out = [sem(n) for n in ("d_const", "d_dft", "d_small", "d_l0", "d_wnat", "d_out")]
        d_x = [sem(f"d_x{b}") for b in range(B)]
        d_stage = [sem(f"d_stage{i}") for i in range(2)]
        names = """pool_set prep_ps prep_sb prep_act veps_set rstd_set ln_done xt_ps xhi_done xlo_done logits_ps score_done
            cum_need cum_ps comb_done combt_ps combt_done T_free g_done u_done sg_done h_done hhi_done
            hlo_pool hlo_dve down_done outt_done outt_ps x_done dve act pool s_ps s_sub s_exp s_prob s_rec
            p_ps p_sb pv_ps l0w_ps l0w_hi l0w_lo stage_used kbd_done vbd_done v1_ps q1_ps fft_in fft_ps w_ps
            w_sb prod_done whi_done shared2 z_proj z_s z_max z_exp z_tr z_pt z_pp z_pv z_up inv_ps dw_done
            dwt_ps rsm_sub m_done""".split()
        q = {n: sem(n) for n in names}

        wnat = wk[:, 0:3, :].rearrange("p a (m d) -> p (a m) d", m=4)
        wk_flat = wk[:, :, :].rearrange("p a c -> p (a c)")
        KEYS0 = KEYS + S
        p0 = [wk_flat[:, 0:544], wk_flat[:, 544:1088]]
        pt0 = [wk_flat[:, 1088:1600], wk_flat[:, 1600:2112]]
        ptc0 = [wk_flat[0:KEYS, 2112:2240], wk_flat[0:KEYS, 2240:2368]]
        w0t = xt[:, 0, :].rearrange("p (m d) -> p m d", m=4)
        w1t = xt[:, 1, :].rearrange("p (m d) -> p m d", m=4)
        kbd1, vbd1, q1t = hb[:, 0:2, :], xt[:, 1, :], hb[:, 2:4, :]
        v1 = xn[:, 2 * TB:, :].rearrange("p (a k) d -> p a (k d)", a=2)
        w3t = wk[:, 5, 0:384].rearrange("p (m d) -> p m d", m=3)
        ctxt = hb[:, 0, 0:128]
        kv3 = hb[:, 1, 0:256].rearrange("p (m c) -> p m c", m=2)
        ctx_nat = hb[:, 2, 0:128]
        kpw_nat = hb[:, 3, 0:128]
        sw_nat = hb[:, 2, 128:512].rearrange("p (m d) -> p m d", m=3)
        rw = hb[:, 3, 128:216]

        freq, halves = xn[:, 2 * TB:3 * TB, :], xn[:, 3 * TB:4 * TB, :]
        prod2 = wk[:, 5, :].rearrange("p (m d) -> p m d", m=4)

        lora_a, lora_bt = [wk[0:R, i, :].rearrange("p (m d) -> p m d", m=4) for i in (3, 4)]
        lora_b = xn[:, 8, 0:4 * R].rearrange("p (m r) -> p m r", m=4)
        rw_nat, bfc_nat = xn[0:32, 9:12, :], xn[0:32, 12, :]
        brow = xn[0:9, 13, :]
        small_bf = xn[:, 14:16, :].rearrange("p a b -> p (a b)").bitcast(BF16)
        sw_bf = small_bf[:, 0:384].rearrange("p (m d) -> p m d", m=3)
        gw2_bf = small_bf[0:32, 384:512]
        bproj = wk[0:24, 5, 384:512]
        early = const[:, C_DFT:]
        v0c = early[0:KEYS, 0:512].rearrange("p (b d) -> p b d", b=B)
        w0 = early[:, 1792:2304].rearrange("p (m d) -> p m d", m=4)
        ctx0 = early[:, 512:640]
        v0row = early[0:1, 640:768]
        wq1, wo1t = early[:, 1280:1408], early[:, 1408:1536]
        kt1 = early[:, 1536:1792].rearrange("p (m c) -> p m c", m=2)

        def cols4(t):
            return t[:, :].rearrange("p (k c) -> p k c", k=4)

        def quads_l0():
            r = []
            for base, w in ((0, a["L0_ffn_expert_gate"]), (16, a["L0_ffn_expert_up"])):
                v = w.rearrange("(c e) i d -> (e i) c d", e=2)
                r += [(v[:, 4 * k:4 * k + 4, :], base + 4 * k, 4) for k in range(4)]
            v = a["L0_ffn_expert_down"].rearrange("e d i -> d e i")
            r += [(v[:, 8 * k:8 * k + 8, :], 32 + 4 * k, 4) for k in range(4)]
            return r

        QL0 = quads_l0()
        NQ0 = len(QL0) + 1

        def quads_nat(layer):
            r = []
            if layer == 1:
                fc = a["L1_ffn_w_fc"]
                pr = a["L1_ffn_w_proj"].rearrange("e (c h) d -> e h c d", c=4)
                for e in range(8):
                    r += [(fc[e], 4 * e, 4), (pr[e], 32 + 4 * e, 4)]
            if layer == 3:
                for base, w in ((0, "routed_w1"), (20, "routed_w2"), (40, "routed_w3")):
                    v = a["L3_ffn_" + w].rearrange("e d h -> d e h")
                    r += [(v[:, 4 * k:4 * k + 4, :], base + 4 * k, 4) for k in range(4)]
                r += [(a["L3_ffn_shared_w1"][0], 16, 4), (a["L3_ffn_shared_w2"][0], 36, 4),
                      (a["L3_ffn_shared_w3"][0].rearrange("(c h) d -> h c d", c=4), 56, 4)]
            if layer == 2:
                for base, w in ((0, "W1"), (16, "W3")):
                    v = a["L2_ffn_" + w].rearrange("e d i -> d e i")
                    r += [(v[:, 8 * k:8 * k + 8, :], base + 4 * k, 4) for k in range(4)]
                v = a["L2_ffn_W2"].rearrange("(c e) i d -> (e i) c d", e=2)
                r += [(v[:, 4 * k:4 * k + 4, :], 32 + 4 * k, 4) for k in range(4)]
            return r

        QN = {l: quads_nat(l) for l in (1, 2, 3)}
        QBASE = {1: NQ0, 2: NQ0 + len(QN[1]), 3: NQ0 + len(QN[1]) + len(QN[2])}
        NQ = QBASE[3] + len(QN[3])

        def slots(layer, c):
            if layer == 0:
                return (c, 16 + c, 32 + c) if c < 16 else (48, 49, 50)
            if layer == 1:
                return c, None, 32 + c
            if layer == 2:
                return (c, 16 + c, 32 + c) if c < 16 else (48, 49, 50)
            return c, 20 + c, 40 + c

        block = ctx.enter_context(nc.Block())

        def loaded(r):
            return sum(48 if k == NQ0 - 1 else 16 for k in range(r % 2, r + 1, 2))

        def quad(r):
            if r < NQ0 - 1:
                return QL0[r][1], QL0[r][2], 0
            if r == NQ0 - 1:
                return 48, 3, 0
            layer = 1 if r < QBASE[2] else 2 if r < QBASE[3] else 3
            return QN[layer][r - QBASE[layer]][1:] + (layer,)

        NORMS = [(s, b) for s in range(3) for b in range(B)] + [(3, 0), (3, 1), (3, 2), (4, 0), (3, 3), (4, 1), (4, 2),
                 (5, 0), (5, 1), (4, 3), (5, 2), (5, 3)] + [(s, b) for b in range(B) for s in (6, 7)]
        UPDATES = [(s, b) for s in range(3) for b in range(B)] + [(3, 0), (4, 0), (3, 1), (4, 1), (3, 2), (4, 2), (3, 3),
                   (4, 3), (5, 0), (5, 1), (5, 2), (6, 0), (5, 3), (6, 1), (7, 0), (6, 2), (7, 1), (6, 3), (7, 2), (7, 3)]
        X_ORDER = [n for n in NORMS if n[0] != 4]

        def norm_num(s, b):
            return NORMS.index((s, b)) + 1

        def x_num(s, b):
            return UPDATES.index((s, b)) + 1

        def tnum(s, b):
            return X_ORDER.index((s, b)) + 1

        def xn_rows(s, b):
            return TB * (2 if s == 4 else b % 2)

        def low_on(l, c):
            return "dve" if l == 1 and c % 4 == 3 else "pool"

        def wait_low(eng, k):
            l = max(n for n in range(4) if CB[n] <= k)
            on_dve = min(max(k + 1 - CB[1], 0), B * NC[1]) // 4
            if low_on(l, (k - CB[l]) % NC[l]) == "dve":
                eng.wait_ge(q["hlo_dve"], on_dve)
            else:
                eng.wait_ge(q["hlo_pool"], k + 1 - on_dve)

        def fnum(l, b):
            return 4 * l + b + 1

        def knum(l, b, c):
            return CB[l] + b * NC[l] + c

        def softmax_num(l, b):
            return b if l == 1 else 16 + b

        NORM_AT, OUT_AT, XN_AT, ADD_AT, XHI_AT, XLO_AT, SCORE_AT = 0, 2, 3, 3, 5, 6, 8
        ROUTE_AT = [(8, 9, 10, 11, 12, 13, 13), (16, 16, 16, 17, 18, 19, 20), (8, 8, 8, 9, 10, 11, 12), (8, 8, 8, 9, 10, 11, 12)]
        COUNT_AT = 10
        WEIGH_AT = [14, 21, 14, 13]
        COMBT_AT = [16, 24, 16, 15]
        PE_BACK, PE_XN, PE_LOGITS, PE_RUN = 0, 2, 5, 11
        PE_COMB = [13, 21, 13, 12]
        NORM2_AT, XN2_AT = 4, 7
        AHEAD = 3

        TAP_AT, PE_TAP, TAPW_AT, PE_SPEC = 7, 7, 11, 8

        ADD3_AT = 9

        def next3(l, b):
            return b + 1 if l == 3 and b + 1 < B else 0 if l == 2 and b + 1 == B else None

        def fft_steps(l, b):
            if l == 1 and b >= 1:
                return b - 1, (9, 11, 11, 14, 14, 18)
            if l == 2 and b == 0:
                return 3, (4, 7, 8, 11, 10, 13)
            return None, (None,) * 6

        PRE5 = (17, 19, 18, 21, 22, 21, 24, 25, 26, 26, 29, 28, 31)

        def spectrum_at(c, lag):
            i, odd = divmod(c - lag - PE_SPEC, 2)
            return i if 0 <= i < 5 and not odd else None

        def split_round(l, b, c):
            if l == 3 or c % 4 != 1 or c > 14:
                return None
            n = -(-len(QN[l + 1]) // B)
            j, r = c // 4, n * b + c // 4
            return QBASE[l + 1] + r if j < n and r < len(QN[l + 1]) else None

        @block.sync
        def _(sp):
            sp.dma_start(const[:, 0:C_DFT], a["consts"][:, 0:C_DFT]).then_inc(d_const, 16)
            sp.dma_start(x[:, 0:TB, :], a["x"][0].rearrange("(k p) d -> p k d", p=128)).then_inc(d_x[0], 16)
            sp.dma_start(ctx_nat, a["ctx_1024"].rearrange("b t d -> (b t) d")).then_inc(d_l0, 16)
            for i, n in enumerate([f"L{l}_xattn_W{w}" for l in (0, 1, 3) for w in "qkvo"]):
                dst = w0t[:, 2, :] if n == "L0_xattn_Wv" else wnat[:, i, :]
                sp.dma_start(dst, a[n]).then_inc(d_l0 if i < 4 else d_wnat, 16)
                if i == 3:
                    sp.dma_start(x[:, TB:2 * TB, :], a["x"][1].rearrange("(k p) d -> p k d", p=128)).then_inc(d_x[1], 16)
            sp.dma_start(kpw_nat, a["L2_xattn_kp_w"]).then_inc(d_wnat, 16)
            for b in range(2, B):
                sp.dma_start(x[:, TB * b:TB * b + TB, :], a["x"][b].rearrange("(k p) d -> p k d", p=128)).then_inc(d_x[b], 16)
            for r in range(NQ):
                if r == QBASE[2]:
                    sp.wait_ge(q["x_done"], x_num(2, 3))
                    sp.dma_start(dft, a["consts"][:, C_DFT:].rearrange("p (m h) -> p m h", m=N_DFT)).then_inc(d_dft, 16)
                if r >= 2:
                    sp.wait_ge(q["stage_used"], r - 1)
                dst = stage[:, r % 2, :]
                if r == NQ0 - 1:
                    for i, w in enumerate(("gate", "up", "down")):
                        sp.dma_start(dst[:, 128 * i:128 * i + 128], a["L0_ffn_shared_" + w]).then_inc(d_stage[r % 2], 16)
                    continue
                layer = quad(r)[2]
                if layer == 2:
                    dst = dst.bitcast(BF16)[:, 0:512]
                src = QL0[r][0] if layer == 0 else QN[layer][r - QBASE[layer]][0]
                if len(src.shape) == 3:
                    dst = dst.rearrange("p (c i) -> p c i", c=src.shape[1])
                sp.dma_start(dst, src).then_inc(d_stage[r % 2], 16)
            for b in range(B):
                sp.wait_ge(q["x_done"], x_num(7, b))
                sp.dma_start(out[b].rearrange("(k p) d -> p k d", p=128), x[:, TB * b:TB * b + TB, :]).then_inc(d_out, 16)
            sp.wait_ge(d_out, 16 * B)

        SMALL = [(g_all[:, 0:4], a["g_xattn"].rearrange("(o n) -> o n", o=1).broadcast_to([128, 4])),
                 (g_all[:, 4:8], a["g_ffn"].rearrange("(o n) -> o n", o=1).broadcast_to([128, 4])),
                 (rb[:, 0:32], a["L0_ffn_gate_bias"].rearrange("(o n) -> o n", o=1).broadcast_to([128, 32])),
                 (rb[:, 32:64], a["L2_ffn_bias"].rearrange("(o n) -> o n", o=1).broadcast_to([128, 32])),
                 (rb[:, 64:80], a["L3_ffn_expert_bias"].rearrange("(o n) -> o n", o=1).broadcast_to([128, 16])),
                 (rw_nat[0:32, 0, :], a["L0_ffn_gate_w"]),
                 (rw_nat[0:8, 1, :], a["L1_ffn_router_w"]),
                 (gw2_bf[:, :], a["L2_ffn_gate_w"]),
                 (rw[:, 72:88], a["L3_ffn_router_w"]),
                 (bfc_nat, a["L1_ffn_b_fc"].rearrange("e (c h) -> (e c) h", c=4)),
                 (bproj[0:8, :], a["L1_ffn_b_proj"]),
                 (bproj[8:16, :], a["L1_ffn_b_proj"]),
                 (bproj[16:24, :], a["L1_ffn_b_proj"]),
                 (sw_bf[0:64, 0, :], a["L2_ffn_sw1"]),
                 (sw_bf[0:64, 1, :], a["L2_ffn_sw3"]),
                 (sw_bf[:, 2, 0:64], a["L2_ffn_sw2"]),
                 (w2conv[:, :], a["L2_xattn_weight"]),
                 (mask_i[:, :, :], a["mask_1x1xSxS2_ik0"].rearrange("u v (k p) t -> p (u v k) t", p=128))]
        for i, n in enumerate(("L0_xattn_bq", "L0_xattn_bk", "L0_xattn_bv", "L1_xattn_bq", "L1_xattn_bk", "L1_xattn_bv",
                               "L3_xattn_bq", "L3_xattn_bv", "L2_xattn_kp_b")):
            SMALL.append((brow[i:i + 1, :], a[n].rearrange("(o n) -> o n", o=1)))
        for i, l in enumerate((0, 1, 3)):
            SMALL.append((bo[0:1, i, :], a[f"L{l}_xattn_bo"].rearrange("(o n) -> o n", o=1)))
        SMALL = SMALL[:2] + SMALL[9:] + SMALL[2:9]
        LORA = []
        for i, w in enumerate("qkvo"):
            LORA.append((lora_a[:, i, :], a["L0_xattn_A" + w]))
            LORA.append((lora_b[:, i, :], a["L0_xattn_B" + w]))
        N_L0 = 16 * (len(LORA) + 5)
        N_SMALL = 16 * len(SMALL)

        @block.gpsimd
        def _(pool):
            pool.memset(neghalf[:, :], -0.5).then_inc(q["pool_set"], 1)
            pool.memset(e_base[:, :], float(np.e))
            pool.memset(ones_row[:, :], 1.0).then_inc(q["pool_set"], 1)
            pool.memset(ones_bf[:, :], 1.0).then_inc(q["pool_set"], 1)
            pool.memset(sw_nat[:, :, :], 0.0).then_inc(q["pool_set"], 1)
            pool.memset(gp[:, :, 4:10], LOW).then_inc(q["pool_set"], 1)
            pool.wait_ge(d_const, 16)
            pool.tensor_copy(ident_bf[:, :], ident).then_inc(q["pool_set"], 1)
            pool.tensor_copy(tri_bf[:, :], const[:, C_TRI:C_TRI + 128]).then_inc(q["pool_set"], 1)
            pool.tensor_copy(pair_sel[:, :, :], const[0:96, C_SEL:C_SEL + 32].unsqueeze(2).broadcast_to([96, 32, 64]),
                             saturate=False).then_inc(q["pool_set"], 1)
            pool.tensor_copy(sel16[:, :], const[0:48, C_SEL16:C_SEL16 + 16]).then_inc(q["pool_set"], 1)
            pool.tensor_copy(sel8[:, :], const[0:24, C_SEL8:C_SEL8 + 8]).then_inc(q["pool_set"], 1)
            def rsqrt(s, b):
                pool.wait_ge(q["veps_set"], norm_num(s, b))
                pool.tensor_tensor(rstd[:, :], veps[:, :], neghalf[:, :], ALU.pow).then_inc(q["rstd_set"], 1)

            pool.wait_ge(q["pool_set"], 1)
            rsqrt(0, 0)
            rsqrt(0, 1)
            pool.wait_ge(d_small, N_SMALL)
            pool.wait_ge(q["pool_set"], 4)
            pool.tensor_copy(sw_nat[0:64, 0:2, :], sw_bf[0:64, 0:2, :]).then_inc(q["pool_set"], 1)
            pool.tensor_copy(sw_nat[:, 2, 0:64], sw_bf[:, 2, 0:64]).then_inc(q["pool_set"], 1)
            pool.tensor_copy(rw_nat[:, 2, :], gw2_bf[:, :]).then_inc(q["pool_set"], 1)

            def split_low(r):
                slot, n, layer = quad(r)
                pool.wait_ge(q["whi_done"], r - NQ0 + 1)
                if layer == 2:
                    pool.sem_inc(q["stage_used"], 1)
                    return
                src = stage[:, r % 2, :].rearrange("p (c h) -> p c h", c=4)
                pool.tensor_tensor(wb_lo[:, slot:slot + 4, :], src, wb_hi[:, slot:slot + 4, :].bitcast(F32),
                                   ALU.subtract).then_inc(q["stage_used"], 1)

            def low(l, b, c):
                k = knum(l, b, c)
                pool.wait_ge(q["hhi_done"], k + 1)
                pool.tensor_tensor(h_lo[:, k % 3, :], hb[:, k % 4, :], h_hi[:, k % 3, :].bitcast(F32),
                                   ALU.subtract).then_inc(q["hlo_pool"], 1)

            def by_heads(dst, j, b):
                src = kt1[:, j, KEYS * b:KEYS * b + KEYS].unsqueeze(1).broadcast_to([128, HEADS, KEYS])
                hm = headmask.unsqueeze(2).broadcast_to([128, HEADS, KEYS])
                return pool.tensor_tensor(dst.rearrange("p (h t) -> p h t", h=HEADS), src, hm, ALU.mult)

            def kbd(b):
                if b >= 2:
                    pool.wait_ge(q["s_ps"], 4 * (b - 1))
                by_heads(kbd1[:, b % 2, :], 0, b).then_inc(q["kbd_done"], 1)

            def vbd(b):
                if b >= 1:
                    pool.wait_ge(q["v1_ps"], b)
                by_heads(vbd1, 1, b).then_inc(q["vbd_done"], 1)

            def router_exp(b, k):
                pool.wait_ge(q["rsm_sub"], b + 1)
                ins = pool.tensor_tensor(rt[:, k, 0:8], e_base[:, :], rt[:, k, 0:8], ALU.pow)
                if k == TB - 1:
                    ins.then_inc(q["score_done"], 1)

            def count2(b):
                pool.wait_ge(q["m_done"], b + 1)
                m_ = selm[:, :, 0:32]
                if b >= 1:
                    pool.tensor_copy(run[:, 0, :], run[:, TB, :]).then_inc(q["pool"], 1)
                for t in range(TB):
                    if b or t:
                        pool.wait_ge(q["pool"], 5 * b + t)
                    pool.tensor_tensor(run[:, t + 1, :], run[:, t, :], m_[:, t, :], ALU.add).then_inc(q["pool"], 1)
                pool.wait_ge(q["pool"], 5 * b + TB)
                pool.tensor_copy(run_bf[:, :, :], run[:, 0:TB, :]).then_inc(q["cum_need"], 1)

            def prob1(i):
                pool.wait_ge(q["s_rec"], i + 1)
                p = wk[:, i % 4, :].rearrange("p (h t) -> p h t", h=HEADS)
                pool.tensor_tensor(p, p, sm1[:, i % 2, :].unsqueeze(2).broadcast_to([128, HEADS, KEYS]),
                                   ALU.mult).then_inc(q["s_prob"], 1)

            for s in range(STAGES):
                l = s // 2
                if s == 2:
                    pool.wait_ge(q["x_done"], 8)
                    kbd(0)
                    vbd(0)
                    kbd(1)
                    for i in range(16):
                        b, k = divmod(i, TB)
                        if k == 1 and b + 2 < B:
                            rsqrt(s, b + 2)
                        prob1(i)
                        if k == 3 and b + 2 < B:
                            kbd(b + 2)
                        if k == 1 and b + 1 < B:
                            vbd(b + 1)
                        if i == 11:
                            rsqrt(s + 1, 0)
                    continue
                if s in (4, 6):
                    continue
                if s % 2 == 0:
                    for b in range(2, B):
                        rsqrt(s, b)
                    if s == 0:
                        rsqrt(1, 0)
                    continue
                if s == 3:
                    pool.wait_ge(q["x_done"], 8)
                    pool.wait_ge(q["prep_sb"], 10)
                    pool.tensor_copy(wa_hi[:, 48:51, :], sw_t[:, :, :]).then_inc(q["shared2"], 1)
                for b in range(B):
                    for c in range(NC[l]):
                        if low_on(l, c) == "pool":
                            low(l, b, c)
                        n = next3(l, b)
                        if n is not None:
                            if c == NORM_AT:
                                rsqrt(6, n)
                            if c == ADD3_AT:
                                rsqrt(7, n)
                        elif b + 1 < B and c == NORM_AT:
                            rsqrt(s, b + 1)
                        n, at = fft_steps(l, b)
                        if n is not None and c == at[0]:
                            rsqrt(4, n)
                        if l == 1 and b + 1 == B:
                            if c == PRE5[0]:
                                rsqrt(5, 0)
                            if c == PRE5[8]:
                                count2(0)
                        if l == 1 and b + 1 < B and c in range(SCORE_AT, SCORE_AT + 8, 2):
                            router_exp(b + 1, (c - SCORE_AT) // 2)
                        if l == 2 and b + 1 < B and c == COUNT_AT:
                            count2(b + 1)
                        if l == 0 and b + 1 == B:
                            if c == NORM_AT:
                                rsqrt(2, 0)
                            if c == NORM2_AT:
                                rsqrt(2, 1)
                        r = split_round(l, b, c)
                        if r is not None:
                            split_low(r)

        @block.scalar
        def _(act):
            for dst, src in LORA:
                act.dma_start(dst, src).then_inc(d_l0, 16)
            for dst, src in SMALL:
                act.dma_start(dst, src).then_inc(d_small, 16)
            act.wait_ge(d_small, N_SMALL)
            act.activation(tg[:, :], g_all[:, :], ACT.Tanh).then_inc(q["act"], 1)
            act.wait_ge(q["prep_sb"], 9)
            act.activation(rw_hi[:, :], rw[:, :], ACT.Copy).then_inc(q["prep_act"], 1)

            def weights0(r):
                act.wait_ge(q["l0w_ps"], r + 1)
                slot, n, _ = quad(r)
                act.activation(wa_hi[:, slot:slot + n, :], cols4(T)[:, 0:n, :], ACT.Copy).then_inc(q["l0w_hi"], 1)

            def xf(s, b):
                act.wait_ge(q["xt_ps"], tnum(s, b))
                act.activation(xt[:, 0 if s == 2 else b % 2, :], T[:, :], ACT.Copy).then_inc(q["T_free"], 1)

            def softmax_exp(l, b):
                i = softmax_num(l, b)
                n = KEYS * TB
                act.wait_ge(q["s_sub"], i + 1)
                act.activation(wk[:, 2 + b % 2, 0:n], wk[:, b % 2, 0:n], ACT.Exp).then_inc(q["s_exp"], 1)

            def prob_t(l, b):
                i = softmax_num(l, b)
                act.wait_ge(q["p_ps"], i + 1)
                act.wait_ge(q["pv_ps"], i - 1)
                act.activation(wk[0:KEYS, 4 + b % 2, :], T[0:KEYS, :], ACT.Copy).then_inc(q["T_free"], 1)

            def exp1(i):
                act.wait_ge(q["s_sub"], i + 1)
                act.activation(wk[:, i % 4, :], wk[:, i % 4, :], ACT.Exp).then_inc(q["s_exp"], 1)

            def prob_t1(i):
                act.wait_ge(q["p_ps"], i + 1)
                if i >= 2:
                    act.wait_ge(q["pv_ps"], i - 1)
                act.activation(wk[:, 4 + i % 2, :], W[i % 2][:, :], ACT.Copy).then_inc(q["p_sb"], 1)

            def query1(b):
                act.wait_ge(q["q1_ps"], b + 1)
                if b >= 2:
                    act.wait_ge(q["s_ps"], 4 * (b - 1))
                act.activation(q1t[:, b % 2, :], T[:, :], ACT.Identity, bias=bq1s[:, 0:1], scale=DK ** -0.5).then_inc(q["T_free"], 1)

            def value1(b):
                act.wait_ge(q["v1_ps"], b + 1)
                if b >= 2:
                    act.wait_ge(q["pv_ps"], 4 * (b - 1))
                act.activation(v1[:, b % 2, :], T[:, :], ACT.Copy).then_inc(q["T_free"], 1)

            def pre_x(l, b):
                s = 2 * l + 1
                act.wait_ge(q["xt_ps"], tnum(s, b))
                act.activation(xt_hi[:, b % 2, :], T[:, :], ACT.Copy).then_inc(q["xhi_done"], 1)

            def pre_score(l, b):
                act.wait_ge(q["logits_ps"], fnum(l, b))
                E = N_EXP[l]
                src = T[:, 0:TB * E].rearrange("p (k e) -> p k e", k=TB)
                if l == 1:
                    act.wait_ge(q["rsm_sub"], b + 1)
                    act.activation(rt[:, :, 0:E], rt[:, :, 0:E], ACT.Exp).then_inc(q["score_done"], 1)
                    return
                act.activation(rt[:, :, 0:E], src, ACT.Tanh, scale=0.5).then_inc(q["score_done"], 1)

            def pre_comb(l, b):
                rows = 3 * N_EXP[l]
                act.wait_ge(q["combt_ps"], fnum(l, b))
                act.activation(comb_t[0:rows, b % 2, :], T[:, :].bitcast(BF16)[0:rows, 0:S], ACT.Copy).then_inc(q["combt_done"], 1)

            def unit(l, b, c):
                k = knum(l, b, c)
                act.wait_ge(q["g_done"], k + 1)
                if k >= 4:
                    wait_low(act, k - 4)
                if l == 1:
                    act.activation(hb[:, k % 4, :], bank[k % 4][:, :], ACT.Gelu_apprx_tanh,
                                   bias=bfc[:, c:c + 1]).then_inc(q["sg_done"], 1)
                else:
                    act.activation(hb[:, k % 4, :], G[k % 2][:, :], ACT.Silu).then_inc(q["sg_done"], 1)

            def high(l, b, c):
                k = knum(l, b, c)
                act.wait_ge(q["h_done"], k + 1)
                if k >= 3:
                    act.wait_ge(q["down_done"], k - 2)
                act.activation(h_hi[:, k % 3, :], hb[:, k % 4, :], ACT.Copy).then_inc(q["hhi_done"], 1)

            def out_t(l, b):
                act.wait_ge(q["down_done"], knum(l, b, NC[l] - 1) + 1)
                act.activation(xt[:, b % 2, :], ACC[:, :], ACT.Copy).then_inc(q["outt_done"], 1)

            def split_high(r):
                slot, n, layer = quad(r)
                act.wait_ge(d_stage[r % 2], loaded(r))
                src = stage[:, r % 2, :]
                if layer == 2:
                    src = src.bitcast(BF16)[:, 0:512]
                dst = (wa_hi if layer == 2 else wb_hi)[:, slot:slot + 4, :]
                act.activation(dst, src.rearrange("p (c h) -> p c h", c=4), ACT.Copy).then_inc(q["whi_done"], 1)

            act.wait_ge(q["act"], 1)

            def project_out(b, j):
                act.wait_ge(q["z_proj"], 3 * b + j + 1)
                if j == 0:
                    ins = act.activation(hb[:, 2 * (b % 2), :], T[:, :], ACT.Identity, bias=bq0s[:, 0:1], scale=D ** -0.5)
                elif j == 1:
                    ins = act.activation(hb[:, 2 * (b % 2) + 1, :], T[:, :], ACT.Identity, bias=bcol[:, 1:2])
                else:
                    ins = act.activation(xt[:, b % 2, :], T[:, :], ACT.Copy)
                ins.then_inc(q["T_free"], 1)

            def exp0(i):
                act.wait_ge(q["z_max"], i + 1)
                if i >= 2:
                    act.wait_ge(q["z_tr"], i - 1)
                act.activation(p0[i % 2].rearrange("p (a n) -> p a n", a=2), psum[:, 2 * (i % 2):2 * (i % 2) + 2, 0:KEYS0 // 2],
                               ACT.Exp, bias=mx[:, i:i + 1], accum_out=zsum[:, i:i + 1]).then_inc(q["z_exp"], 1)

            def context_out(i):
                act.wait_ge(q["z_tr"], i + 1)
                if i >= 2:
                    act.wait_ge(q["z_pv"], i - 1)
                act.activation(ptc0[i % 2], bank[2 * (i % 2)][0:KEYS, 384:512], ACT.Copy).then_inc(q["z_pp"], 1)

            for s in range(STAGES):
                l = s // 2
                if s == 0:
                    xf(0, 0)
                    for j in range(3):
                        project_out(0, j)
                    exp0(0)
                    for i in range(16):
                        if i < NQ0:
                            weights0(i)
                        if i < 15:
                            exp0(i + 1)
                        context_out(i)
                        if i < 12:
                            if i % 4 == 0:
                                xf(0, i // 4 + 1)
                            else:
                                project_out(i // 4 + 1, i % 4 - 1)
                        if i == 12:
                            pre_x(0, 0)
                        if i == 14:
                            pre_score(0, 0)
                elif s in (4, 6):
                    continue
                elif s == 2:
                    query1(0)
                    value1(0)
                    xf(s, 1)
                    exp1(0)
                    exp1(1)
                    for i in range(16):
                        b, k = divmod(i, TB)
                        if i + 2 < 16:
                            exp1(i + 2)
                        prob_t1(i)
                        if b + 1 < B:
                            if k == 0:
                                query1(b + 1)
                            if k == 2:
                                value1(b + 1)
                        if b + 2 < B and k == 3:
                            xf(s, b + 2)
                        if i == 12:
                            pre_x(1, 0)
                        if i == 15:
                            pre_score(1, 0)
                else:
                    if l != 2:
                        pre_comb(l, 0)
                    for b in range(B):
                        for c in range(NC[l]):
                            unit(l, b, c)
                            if c == OUT_AT and b >= 1:
                                out_t(l, b - 1)
                            k = b * NC[l] + c
                            if k >= 1:
                                pb, pc = divmod(k - 1, NC[l])
                                high(l, pb, pc)
                            n = next3(l, b)
                            if n is not None:
                                if c == 4:
                                    xf(6, n)
                                if c == 6:
                                    softmax_exp(3, n)
                                if c == 8:
                                    prob_t(3, n)
                                if c == 12:
                                    pre_x(3, n)
                                if c == 14:
                                    pre_score(3, n)
                                if c == 18:
                                    pre_comb(3, n)
                            elif b + 1 < B:
                                if c == XHI_AT:
                                    pre_x(l, b + 1)
                                if c == SCORE_AT and l != 1:
                                    pre_score(l, b + 1)
                                if c == COMBT_AT[l]:
                                    pre_comb(l, b + 1)
                            elif s == 1 and c == XHI_AT:
                                xf(s + 1, 0)
                            if l == 1 and b + 1 == B:
                                if c == PRE5[3]:
                                    pre_x(2, 0)
                                if c == PRE5[6]:
                                    pre_score(2, 0)
                                if c == PRE5[12]:
                                    pre_comb(2, 0)
                            if l == 1 and b == 0:
                                if c == TAPW_AT:
                                    act.wait_ge(q["dwt_ps"], 1)
                                    act.activation(wk[:, 5, :], T[:, :], ACT.Copy).then_inc(q["T_free"], 1)
                                i = spectrum_at(c, 4)
                                if i is not None:
                                    act.wait_ge(q["w_ps"], i + 1)
                                    act.activation(wk[:, i, :], T[:, :], ACT.Copy).then_inc(q["w_sb"], 1)
                                    act.wait_ge(q["w_sb"], i + 1)
                                    act.sem_inc(q["T_free"], 1)
                            r = split_round(l, b, c)
                            if r is not None:
                                split_high(r)
                    high(l, B - 1, NC[l] - 1)
                    out_t(l, B - 1)

        @block.tensor
        def _(pe):
            t_uses = [0]

            def use_t():
                if t_uses[0]:
                    pe.wait_ge(q["T_free"], t_uses[0])
                t_uses[0] += 1

            def mm(o, l, r, start, stop):
                return pe.matmul(o, l, r, start=start, stop=stop, skip_group_check=True)

            pe.wait_ge(d_const, 16)
            pe.wait_ge(d_l0, N_L0)
            b0, b1, b2, b3, b4, b5 = [bank[i] for i in range(6)]
            for j, src in enumerate((wnat[:, 0, :], wnat[:, 1, :], ctx_nat, wnat[:, 3, :])):
                last = pe.transpose(b0[:, 128 * j:128 * j + 128], src, ident)
            last.then_inc(q["prep_ps"], 1)
            for j in range(4):
                last = pe.transpose(b3[0:R, 128 * j:128 * j + 128], lora_b[:, j, :], ident)
            last.then_inc(q["prep_ps"], 1)
            pe.wait_ge(q["prep_sb"], 3)
            for j in range(4):
                l, r = (lora_bt, lora_a) if j == 2 else (lora_a, lora_bt)
                last = mm(bank[6][:, 128 * j:128 * j + 128], l[:, j, :], r[:, j, :], True, True)
            last.then_inc(q["prep_ps"], 1)
            pe.wait_ge(q["pool_set"], 13)
            pe.wait_ge(d_wnat, 16 * 9)
            pe.wait_ge(d_small, N_SMALL)
            for j, src in enumerate((wnat[:, 5, :], wnat[:, 6, :], wnat[:, 7, :], kpw_nat)):
                last = pe.transpose(b1[:, 128 * j:128 * j + 128], src, ident)
            last.then_inc(q["prep_ps"], 1)
            for j, m in enumerate((9, 10, 11, 4)):
                last = pe.transpose(b2[:, 128 * j:128 * j + 128], wnat[:, m, :], ident)
            last.then_inc(q["prep_ps"], 1)
            pe.transpose(b4[:, 0:32], rw_nat[0:32, 0, :], ident[0:32, 0:32])
            pe.transpose(b4[:, 32:40], rw_nat[0:8, 1, :], ident[0:8, 0:8])
            pe.transpose(b4[:, 40:72], rw_nat[0:32, 2, :], ident[0:32, 0:32])
            pe.transpose(b4[:, 128:160], bfc_nat[:, :], ident[0:32, 0:32])
            pe.transpose(b4[:, 160:169], brow[:, :], ident[0:9, 0:9]).then_inc(q["prep_ps"], 1)
            for j in range(3):
                last = pe.transpose(b5[:, 128 * j:128 * j + 128], sw_nat[:, j, :], ident)
            last.then_inc(q["prep_ps"], 1)
            pe.wait_ge(q["prep_sb"], 12)
            mm(bank[7][:, 0:128], w0[:, 2, :], w0[:, 3, :], True, True)
            mm(bank[7][0:1, 128:256], bcol[:, 2:3], w0[:, 3, :], True, True)
            mm(bank[7][:, 256:384], w1t[:, 0, :], ctxt, True, True)
            mm(bank[7][:, 384:512], w1t[:, 1, :], ctxt, True, True).then_inc(q["prep_ps"], 1)
            mm(b0[:, 0:128], w3t[:, 0, :], ctxt, True, True)
            mm(b0[:, 128:256], w3t[:, 1, :], ctxt, True, True)
            mm(b0[:, 256:260], w1t[:, 3, :], ctx_mean[:, :], True, True).then_inc(q["prep_ps"], 1)
            pe.wait_ge(q["prep_sb"], 19)
            mm(b1[:, 256:384], wnat[:, 8, :], kv3[:, 0, :], True, True).then_inc(q["prep_ps"], 1)
            mm(b2[0:1, 256:384], bcol[:, 6:7], kv3[:, 0, :], True, True).then_inc(q["prep_ps"], 1)
            for b in range(B):
                mm(b3[0:KEYS, 128 * b:128 * b + 128], ctxt[:, KEYS * b:KEYS * b + KEYS], w0[:, 3, :], True, False)
                last = mm(b3[0:KEYS, 128 * b:128 * b + 128], ones_row[:, 0:KEYS], bo[:, 0, :], False, True)
            last.then_inc(q["prep_ps"], 1)
            for b in range(B):
                o = b4[0:KEYS, 128 * b:128 * b + 128]
                mm(o, kv3[:, 1, KEYS * b:KEYS * b + KEYS], w3t[:, 2, :], True, False)
                last = mm(o, ones_row[:, 0:KEYS], bo[:, 2, :], False, True)
            last.then_inc(q["prep_ps"], 1)
            pe.wait_ge(q["prep_sb"], 23)

            def weights0(r):
                pe.wait_ge(d_stage[r % 2], loaded(r))
                use_t()
                for j in range(quad(r)[1]):
                    last = pe.transpose(T[:, 128 * j:128 * j + 128], stage[:, r % 2, 128 * j:128 * j + 128], ident)
                last.then_inc(q["l0w_ps"], 1)

            def xt_in(s, b):
                pe.wait_ge(q["ln_done"], norm_num(s, b))
                use_t()
                for k in range(TB):
                    last = pe.transpose(T[:, 128 * k:128 * k + 128], xn[:, xn_rows(s, b) + k, :], ident)
                last.then_inc(q["xt_ps"], 1)

            def scores(b):
                use_t()
                row = crow[:, 32 * b:32 + 32 * b]
                mm(T[:, 0:TB * KEYS].rearrange("p (k n) -> p k n", k=TB), ones_row[:, :],
                   row.unsqueeze(1).broadcast_to([1, TB, KEYS]), True, False)
                for k in range(TB):
                    last = mm(T[:, KEYS * k:KEYS * k + KEYS], xt[:, b % 2, 128 * k:128 * k + 128], m3[:, b, :], False, k == TB - 1)
                last.then_inc(q["s_ps"], 1)

            def probs_t(b):
                pe.wait_ge(q["s_prob"], softmax_num(3, b) + 1)
                use_t()
                for k in range(TB):
                    last = pe.transpose(T[0:KEYS, 128 * k:128 * k + 128], wk[:, 2 + b % 2, KEYS * k:KEYS * k + KEYS], ident)
                last.then_inc(q["p_ps"], 1)

            def values(b):
                use_t()
                for k in range(TB):
                    last = mm(T[:, 128 * k:128 * k + 128], wk[0:KEYS, 4 + b % 2, 128 * k:128 * k + 128], v3[:, b, :], True, True)
                last.then_inc(q["pv_ps"], 1)

            def transform(n):
                pe.wait_ge(q["fft_in"], n + 1)
                use_t()
                for i, (m, j) in enumerate(((FWD_RE_E, 0), (FWD_IM_E, 0), (FWD_RE_O, 2), (FWD_IM_O, 2))):
                    o = T[:, 128 * i:128 * i + 128]
                    mm(o, dft[:, m, :], halves[:, j, :], True, False)
                    last = mm(o, dft[:, m + 1, :], halves[:, j + 1, :], False, True)
                last.then_inc(q["fft_ps"], 1)

            def inverse(n):
                pe.wait_ge(q["prod_done"], n + 1)
                use_t()
                for i, (re, im, j) in enumerate(((INV_RE_E, INV_IM_E, 0), (INV_RE_E + 1, INV_IM_E + 1, 0),
                                                 (INV_RE_O, INV_IM_O, 2), (INV_RE_O + 1, INV_IM_O + 1, 2))):
                    o = T[:, 128 * i:128 * i + 128]
                    mm(o, dft[:, re, :], freq[:, j, :], True, False)
                    last = mm(o, dft[:, im, :], freq[:, j + 1, :], False, True)
                last.then_inc(q["inv_ps"], 1)

            def query1(b):
                use_t()
                mm(T[:, :], wq1[:, :], xt[:, 0, :], True, True).then_inc(q["q1_ps"], 1)
                q1_base[b] = t_uses[0]

            def value1(b):
                pe.wait_ge(q["vbd_done"], b + 1)
                use_t()
                for j in range(4):
                    last = mm(T[:, 128 * j:128 * j + 128], vbd1[:, 128 * j:128 * j + 128], wo1t[:, :], True, True)
                last.then_inc(q["v1_ps"], 1)
                v1_base[b] = t_uses[0]

            q1_base, v1_base = {}, {}

            def scores1(i):
                b, k = divmod(i, TB)
                if k == 0:
                    pe.wait_ge(q["T_free"], q1_base[b])
                    pe.wait_ge(q["kbd_done"], b + 1)
                o = bank[i % 4]
                if i >= 4:
                    pe.wait_ge(q["s_sub"], i - 3)
                mm(o[:, :].rearrange("p (h t) -> p h t", h=HEADS), ident_bf[:, :],
                   mask_add[:, k, :].unsqueeze(1).broadcast_to([128, HEADS, KEYS]), True, False)
                mm(o[:, :], q1t[:, b % 2, 128 * k:128 * k + 128], kbd1[:, b % 2, :], False, True).then_inc(q["s_ps"], 1)

            def probs_t1(i):
                pe.wait_ge(q["s_prob"], i + 1)
                if i >= 2:
                    pe.wait_ge(q["p_sb"], i - 1)
                for j in range(4):
                    last = pe.transpose(W[i % 2][:, 128 * j:128 * j + 128], wk[:, i % 4, 128 * j:128 * j + 128], ident)
                last.then_inc(q["p_ps"], 1)

            def values1(i):
                b, k = divmod(i, TB)
                pe.wait_ge(q["p_sb"], i + 1)
                if k == 0:
                    pe.wait_ge(q["T_free"], v1_base[b])
                if k == 0 and b >= 1:
                    pe.wait_ge(q["x_done"], x_num(2, b - 1))
                o = ACC[:, 128 * k:128 * k + 128]
                mm(o, ones_row[:, :], bo[:, 1, :], True, False)
                for j in range(4):
                    last = mm(o, wk[:, 4 + i % 2, 128 * j:128 * j + 128], v1[:, b % 2, 128 * j:128 * j + 128], False, j == 3)
                last.then_inc(q["pv_ps"], 1)

            def logits(l, b):
                pe.wait_ge(q["xlo_done"], fnum(l, b))
                use_t()
                E, off = N_EXP[l], (0, 32, 40, 72)[l]
                for k in range(TB):
                    o = T[:, E * k:E * k + E]
                    hi, lo = (t[:, b % 2, 128 * k:128 * k + 128] for t in (xt_hi, xt_lo))
                    rh, rl = rw_hi[:, off:off + E], rw_lo[:, off:off + E]
                    mm(o, lo, rl, True, False)
                    mm(o, lo, rh, False, False)
                    mm(o, hi, rl, False, False)
                    last = mm(o, hi, rh, False, True)
                last.then_inc(q["logits_ps"], 1)

            def running(b):
                pe.wait_ge(q["cum_need"], b + 1)
                use_t()
                o = T[:, 0:128].rearrange("p (k e) -> p k e", k=TB)
                mm(o, tri_bf[:, :], sel_bf[:, :, :], True, False)
                mm(o, ones_bf[:, :], run_bf[:, :, :], False, True).then_inc(q["cum_ps"], 1)

            def comb_in(l, b):
                rows = 3 * N_EXP[l]
                pe.wait_ge(q["comb_done"], fnum(l, b))
                use_t()
                for k in range(TB):
                    last = pe.transpose(T[:, :].bitcast(BF16)[0:rows, 128 * k:128 * k + 128], chl[:, k, 0:rows], ident_bf[:, :])
                last.then_inc(q["combt_ps"], 1)

            def gu(l, b, c):
                k = knum(l, b, c)
                gs, us, _ = slots(l, c)
                wh, wl = (wa_hi, wa_lo) if l in (0, 2) else (wb_hi, wb_lo)
                hi, lo = xt_hi[:, b % 2, :], xt_lo[:, b % 2, :]
                def product(o, s):
                    mm(o, wh[:, s, :], hi, True, False)
                    if l != 2:
                        mm(o, wl[:, s, :], hi, False, False)
                    return mm(o, wh[:, s, :], lo, False, True)

                if l == 1:
                    if k - CB[1] >= 4:
                        pe.wait_ge(q["sg_done"], k - 3)
                    product(bank[k % 4][:, :], gs).then_inc(q["g_done"], 1)
                    if c % 4 == 0:
                        e = k // 4
                        if k - CB[1] >= 8:
                            pe.wait_ge(q["h_done"], k - 4)
                        if c == 0:
                            pe.wait_ge(q["combt_done"], fnum(l, b))
                        mm(W[e % 2][:, :], sel8[:, c // 4:c // 4 + 1].broadcast_to([24, 128]),
                           comb_t[0:24, b % 2, :], True, True).then_inc(q["u_done"], 1)
                    return
                if k - CB[l] >= 2 or l >= 2:
                    pe.wait_ge(q["sg_done"], max(k - 1, CB[2]) if l == 2 else k - 1)
                product(G[k % 2][:, :], gs).then_inc(q["g_done"], 1)
                if k - CB[l] >= 2 or l >= 2:
                    pe.wait_ge(q["h_done"], max(k - 1, CB[2]) if l == 2 else k - 1)
                last = product(U[k % 2][:, :], us)
                if c == 0:
                    pe.wait_ge(q["combt_done"], fnum(l, b))
                if c < ROUTED[l]:
                    if N_EXP[l] == 32:
                        pick = pair_sel[:, 2 * c:2 * c + 2, :].rearrange("p e i -> p (e i)")
                    else:
                        pick = sel16[:, c:c + 1].broadcast_to([48, 128])
                    last = mm(W[k % 2][:, :], pick, comb_t[0:3 * N_EXP[l], b % 2, :], True, True)
                last.then_inc(q["u_done"], 1)

            def down(l, b, c):
                k = knum(l, b, c)
                s = slots(l, c)[2]
                wh, wl = (wa_hi, wa_lo) if l in (0, 2) else (wb_hi, wb_lo)
                if c == 0:
                    if b or l >= 2:
                        pe.wait_ge(q["outt_done"], fnum(l, b) - 1)
                    else:
                        pe.wait_ge(q["x_done"], x_num(2 * l, B - 1))
                    if l == 1:
                        for j in range(3):
                            mm(ACC[:, :], bproj_bf[:, j, :], comb_t[0:24, b % 2, :], j == 0, False)
                wait_low(pe, k)
                mm(ACC[:, :], wh[:, s, :], h_hi[:, k % 3, :], c == 0 and l != 1, False)
                if l != 2:
                    mm(ACC[:, :], wl[:, s, :], h_hi[:, k % 3, :], False, False)
                last = mm(ACC[:, :], wh[:, s, :], h_lo[:, k % 3, :], False, c == NC[l] - 1)
                last.then_inc(q["down_done"], 1)

            def out_back(l, b):
                pe.wait_ge(q["outt_done"], fnum(l, b))
                use_t()
                for k in range(TB):
                    last = pe.transpose(T[:, 128 * k:128 * k + 128], xt[:, b % 2, 128 * k:128 * k + 128], ident)
                last.then_inc(q["outt_ps"], 1)

            ready0 = {}

            def project(b, j):
                xb = xt[:, b % 2, :]
                use_t()
                if j < 2:
                    last = mm(T[:, :], w0[:, j, :], xb, True, True)
                else:
                    mm(cols4(T), ones_row[:, :], v0row.unsqueeze(1).broadcast_to([1, TB, 128]), True, False)
                    for k in range(TB):
                        last = mm(T[:, 128 * k:128 * k + 128], xb[:, 128 * k:128 * k + 128], w0[:, 2, :], False, k == TB - 1)
                last.then_inc(q["z_proj"], 1)
                ready0[(b, j)] = t_uses[0]

            def scores0(i):
                b, k = divmod(i, TB)
                pe.wait_ge(q["T_free"], ready0[(b, 1)])
                if i >= 2:
                    pe.wait_ge(q["z_pp"], i - 1)
                qt, kt = hb[:, 2 * (b % 2), 128 * k:128 * k + 128], hb[:, 2 * (b % 2) + 1, :]
                a0, a1 = bank[2 * (i % 2)], bank[2 * (i % 2) + 1]
                mm(a0[:, 0:272], qt, kt[:, 0:272], True, True)
                mm(a1[:, 0:240], qt, kt[:, 272:512], True, True)
                mm(a1[:, 240:272], qt, ctx0[:, KEYS * b:KEYS * b + KEYS], True, True).then_inc(q["z_s"], 1)

            def transpose0(i):
                pe.wait_ge(q["z_exp"], i + 1)
                if i >= 2:
                    pe.wait_ge(q["z_pt"], i - 1)
                for j in range(4):
                    pe.transpose(W[i % 2][:, 128 * j:128 * j + 128], p0[i % 2][:, 128 * j:128 * j + 128], ident)
                pe.transpose(bank[2 * (i % 2)][0:KEYS, 384:512], p0[i % 2][:, 512:544], ident).then_inc(q["z_tr"], 1)

            def values0(i):
                b, k = divmod(i, TB)
                pe.wait_ge(q["z_pt"], i + 1)
                pe.wait_ge(q["z_pp"], i + 1)
                pe.wait_ge(q["T_free"], ready0[(b, 2)])
                if i >= 1:
                    pe.wait_ge(q["z_up"], i)
                o = ACC[:, 0:128]
                for j in range(4):
                    mm(o, pt0[i % 2][:, 128 * j:128 * j + 128], xt[:, b % 2, 128 * j:128 * j + 128], j == 0, False)
                mm(o, ptc0[i % 2], v0c[:, b, :], False, True).then_inc(q["z_pv"], 1)

            for s in range(STAGES):
                l = s // 2
                if s == 0:
                    xt_in(0, 0)
                    for j in range(3):
                        project(0, j)
                    scores0(0)
                    for i in range(16):
                        if i < 15:
                            scores0(i + 1)
                        if i < NQ0:
                            weights0(i)
                        transpose0(i)
                        if i >= 1:
                            values0(i - 1)
                        if i < 12:
                            if i % 4 == 0:
                                xt_in(0, i // 4 + 1)
                            else:
                                project(i // 4 + 1, i % 4 - 1)
                        if i == 12:
                            xt_in(1, 0)
                        if i == 13:
                            logits(0, 0)
                    values0(15)
                elif s in (4, 6):
                    continue
                elif s == 2:
                    query1(0)
                    value1(0)
                    xt_in(2, 1)
                    scores1(0)
                    scores1(1)
                    scores1(2)
                    for i in range(16):
                        b, k = divmod(i, TB)
                        if i + 3 < 16:
                            scores1(i + 3)
                        probs_t1(i)
                        if i >= 1:
                            values1(i - 1)
                        if b + 1 < B:
                            if k == 0:
                                query1(b + 1)
                            if k == 2:
                                value1(b + 1)
                        if b + 2 < B and k == 3:
                            xt_in(2, b + 2)
                        if i == 12:
                            xt_in(3, 0)
                        if i == 13:
                            logits(1, 0)
                    values1(15)
                else:
                    def pre(b, part):
                        if part == 0:
                            xt_in(s, b)
                        elif part == 1:
                            logits(l, b)
                        elif part == 2 and l == 2:
                            running(b)
                        elif part == 3:
                            comb_in(l, b)
                    if l != 2:
                        pre(0, 3)
                    pe.wait_ge(q["stage_used"], NQ if l == 3 else QBASE[l + 1])
                    if l == 2:
                        pe.wait_ge(q["shared2"], 1)
                    for c in range(AHEAD):
                        gu(l, 0, c)
                    for b in range(B):
                        for c in range(NC[l]):
                            k = b * NC[l] + c + AHEAD
                            if k < B * NC[l]:
                                gu(l, *divmod(k, NC[l]))
                            down(l, b, c)
                            if c == PE_BACK and b >= 1:
                                out_back(l, b - 1)
                            n = next3(l, b)
                            if n is not None:
                                if c == 1:
                                    xt_in(6, n)
                                if c == 2:
                                    scores(n)
                                if c == 5:
                                    probs_t(n)
                                if c == 6:
                                    values(n)
                                if c == 9:
                                    xt_in(7, n)
                                if c == 11:
                                    logits(3, n)
                                if c == 15 and l == 3:
                                    comb_in(3, n)
                            elif b + 1 < B:
                                for at, p in ((PE_XN, 0), (PE_LOGITS, 1), (PE_RUN, 2), (PE_COMB[l], 3)):
                                    if c == at:
                                        pre(b + 1, p)
                            elif s == 1 and c == PE_XN:
                                xt_in(s + 1, 0)
                            n, at = fft_steps(l, b)
                            if c == at[2]:
                                transform(n)
                            if c == at[4]:
                                inverse(n)
                            if l == 1 and b + 1 == B:
                                if c == PRE5[2]:
                                    xt_in(5, 0)
                                if c == PRE5[5]:
                                    logits(2, 0)
                                if c == PRE5[9]:
                                    running(0)
                                if c == PRE5[11]:
                                    comb_in(2, 0)
                            if l == 1 and b == 0:
                                if c == PE_TAP:
                                    pe.wait_ge(q["dw_done"], 1)
                                    use_t()
                                    for j in range(B):
                                        last = pe.transpose(T[:, 128 * j:128 * j + 128], xt[:, 0, 128 * j:128 * j + 128], ident)
                                    last.then_inc(q["dwt_ps"], 1)
                                i = spectrum_at(c, 0)
                                if i is not None:
                                    pe.wait_ge(d_dft, 16)
                                    use_t()
                                    m = (FWD_RE_E, W_IM_E, W_RE_E2, FWD_RE_O, FWD_IM_O)[i]
                                    mm(T[:, :], dft[:, m, :], wk[:, 5, :], True, True).then_inc(q["w_ps"], 1)
                    out_back(l, B - 1)

        @block.vector
        def _(dve):
            ch_ = Chain(dve, q["dve"])
            link = ch_.link
            ps = q["prep_sb"]

            def norm(s, b):
                moments(s, b)
                scale_rows(s, b)

            def moments(s, b):
                if norm_num(s, b) > 1:
                    dve.wait_ge(q["ln_done"], norm_num(s, b) - 1)
                if s == 0:
                    dve.wait_ge(d_x[b], 16)
                else:
                    dve.wait_ge(q["x_done"], x_num(s - 1, b))
                for k in range(TB):
                    last = dve.bn_stats(stats[:, k, :], x[:, TB * b + k, :])
                link(last)
                for k in range(TB):
                    last = dve.bn_aggr(mv[:, k, :], stats[:, k, :])
                link(last)
                dve.tensor_scalar(veps[:, :], mv[:, :, 1], EPS, None, ALU.add).then_inc(q["veps_set"], 1)

            def scale_rows(s, b):
                dve.wait_ge(q["rstd_set"], norm_num(s, b))
                before = [n for n in NORMS[:NORMS.index((s, b))] if xn_rows(*n) == xn_rows(s, b)][-1:]
                if before and before[0][0] != 4:
                    dve.wait_ge(q["xt_ps"], tnum(*before[0]))
                for k in range(TB):
                    last = dve.tensor_scalar(xn[:, xn_rows(s, b) + k, :], x[:, TB * b + k, :], mv[:, k, 0:1], rstd[:, k:k + 1],
                                             ALU.subtract, ALU.mult)
                last.then_inc(q["ln_done"], 1)

            def shift(b):
                i = softmax_num(3, b)
                dve.wait_ge(q["s_ps"], i + 1)
                if b >= 2:
                    dve.wait_ge(q["s_exp"], i - 1)
                src = T[:, 0:TB * KEYS].rearrange("p (g n) -> p g n", g=TB)
                dve.wait_ge(q["s_sub"], i)
                link(dve.tensor_reduce(mx[:, 0:TB], src, AX, ALU.max))
                dve.tensor_tensor(wk[:, b % 2, 0:TB * KEYS].rearrange("p (g n) -> p g n", g=TB), src,
                                  mx[:, 0:TB].unsqueeze(2).broadcast_to([128, TB, KEYS]), ALU.subtract).then_inc(q["s_sub"], 1)
                dve.wait_ge(q["s_sub"], i + 1)
                dve.sem_inc(q["T_free"], 1)

            def normalise(b):
                i = softmax_num(3, b)
                p = wk[:, 2 + b % 2, 0:TB * KEYS].rearrange("p (g n) -> p g n", g=TB)
                dve.wait_ge(q["s_exp"], i + 1)
                dve.wait_ge(q["s_prob"], i)
                link(dve.tensor_reduce(sm[:, 0:TB], p, AX, ALU.add))
                link(dve.reciprocal(sm1[:, 0, 0:TB], sm[:, 0:TB]))
                dve.tensor_tensor(p, p, sm1[:, 0, 0:TB].unsqueeze(2).broadcast_to([128, TB, KEYS]), ALU.mult).then_inc(q["s_prob"], 1)

            def shift1(i):
                dve.wait_ge(q["s_ps"], i + 1)
                if i >= 1:
                    dve.wait_ge(q["s_sub"], i)
                if i >= 4:
                    dve.wait_ge(q["p_ps"], i - 3)
                src = bank[i % 4][:, :].rearrange("p (h t) -> p h t", h=HEADS)
                link(dve.tensor_reduce(mx[:, :], src, AX, ALU.max))
                dve.tensor_tensor(wk[:, i % 4, :].rearrange("p (h t) -> p h t", h=HEADS), src,
                                  mx[:, :].unsqueeze(2).broadcast_to([128, HEADS, KEYS]), ALU.subtract).then_inc(q["s_sub"], 1)

            def sums1(i):
                dve.wait_ge(q["s_exp"], i + 1)
                link(dve.tensor_reduce(sm[:, :], wk[:, i % 4, :].rearrange("p (h t) -> p h t", h=HEADS), AX, ALU.add))
                link(dve.reciprocal(sm[:, :], sm[:, :]))
                if i >= 2:
                    dve.wait_ge(q["s_prob"], i - 1)
                dve.tensor_scalar(sm1[:, i % 2, :], sm[:, :], anykeep[:, i % TB:i % TB + 1], None, ALU.mult).then_inc(q["s_rec"], 1)
                dve.wait_ge(q["s_rec"], i + 1)

            def update(s, b, src, scale):
                dve.scalar_tensor_tensor(x[:, TB * b:TB * b + TB, :], cols4(src), scale, x[:, TB * b:TB * b + TB, :],
                                         ALU.mult, ALU.add).then_inc(q["x_done"], 1)

            def lo_x(l, b):
                dve.wait_ge(q["xhi_done"], fnum(l, b))
                dve.tensor_tensor(xt_lo[:, b % 2, :], T[:, :], xt_hi[:, b % 2, :].bitcast(F32), ALU.subtract).then_inc(q["xlo_done"], 1)
                dve.wait_ge(q["xlo_done"], fnum(l, b))
                dve.sem_inc(q["T_free"], 1)

            def top(vals, n, k, marked):
                top_values(vals, n, k)
                top_mark(vals, n, k, marked)

            def top_values(vals, n, k):
                w = n + 8 - k
                if k < 8:
                    dve.memset(vals[:, :, n:w], LOW)
                for t in range(TB):
                    last = dve.max(t8[:, t, :], vals[:, t, 0:w if k == 8 else n] if n >= 8 else vals[:, t, 0:w])
                link(last)
                if k < 8:
                    link(dve.memset(t8[:, :, k:8], LOW))

            def top_mark(vals, n, k, marked):
                w = n + 8 - k
                for t in range(TB):
                    last = dve.match_replace(marked[:, t, 0:w], t8[:, t, :], vals[:, t, 0:w], TAKEN)
                link(last)

            def route_shift(l, b):
                if l == 1:
                    E = N_EXP[l]
                    s_ = rt[:, :, 0:E]
                    dve.wait_ge(q["logits_ps"], fnum(l, b))
                    src = T[:, 0:TB * E].rearrange("p (k e) -> p k e", k=TB)
                    link(dve.tensor_reduce(wsum[:, :], src, AX, ALU.max))
                    dve.tensor_tensor(s_, src, wsum[:, :].unsqueeze(2).broadcast_to([128, TB, E]), ALU.subtract).then_inc(q["rsm_sub"], 1)
                    dve.wait_ge(q["rsm_sub"], b + 1)
                    dve.sem_inc(q["T_free"], 1)

            def route_scores(l, b):
                E = N_EXP[l]
                s_ = rt[:, :, 0:E]
                c_ = ch[:, :, 0:E]
                if fnum(l, b) > 1:
                    dve.wait_ge(q["comb_done"], fnum(l, b) - 1)
                if l == 1:
                    dve.wait_ge(q["score_done"], fnum(l, b))
                    link(dve.tensor_reduce(wsum[:, :], s_, AX, ALU.add))
                    link(dve.reciprocal(wrec[:, :], wsum[:, :]))
                    link(dve.tensor_tensor(c_, s_, wrec[:, :].unsqueeze(2).broadcast_to([128, TB, E]), ALU.mult))
                    s_ = c_
                else:
                    dve.wait_ge(q["score_done"], fnum(l, b))
                    dve.sem_inc(q["T_free"], 1)
                    off = {0: 0, 2: 32, 3: 64}[l]
                    link(dve.tensor_scalar(s_, s_, 0.5, 0.5, ALU.mult, ALU.add))
                    link(dve.tensor_tensor(c_, s_, rb[:, off:off + E].unsqueeze(1).broadcast_to([128, TB, E]), ALU.add))

            def route_pairs(l, b):
                if l == 0:
                    v = ch[:, :, 0:32].rearrange("p k (g j) -> p k g j", g=4)
                    u = tour[:, :, :].rearrange("p (k g) j -> p k g j", k=TB)
                    dve.tensor_tensor(u[:, :, :, 0:4], v[:, :, :, 0:4], v[:, :, :, 4:8], ALU.max)
                    link(dve.tensor_tensor(u[:, :, :, 4:8], v[:, :, :, 0:4], v[:, :, :, 4:8], ALU.min))
                    for first, second, n, o in ((0, 4, 2, 8), (8, 10, 1, 12)):
                        f0, f1 = u[:, :, :, first:first + n], u[:, :, :, first + n:first + 2 * n]
                        s0, s1 = u[:, :, :, second:second + n], u[:, :, :, second + n:second + 2 * n]
                        dve.tensor_tensor(u[:, :, :, o:o + n], f0, f1, ALU.max)
                        dve.tensor_tensor(u[:, :, :, 14:14 + n], f0, f1, ALU.min)
                        link(dve.tensor_tensor(u[:, :, :, o + n:o + 2 * n], s0, s1, ALU.max))
                        link(dve.tensor_tensor(u[:, :, :, o + n:o + 2 * n], u[:, :, :, o + n:o + 2 * n], u[:, :, :, 14:14 + n], ALU.max))

            def route_groups(l, b):
                c_ = ch[:, :, 0:N_EXP[l]]
                if l == 0:
                    v = ch[:, :, 0:32].rearrange("p k (g j) -> p k g j", g=4)
                    u = tour[:, :, :].rearrange("p (k g) j -> p k g j", k=TB)
                    link(dve.tensor_tensor(gp[:, :, 0:4], u[:, :, :, 12], u[:, :, :, 13], ALU.add))
                    for t in range(TB):
                        last = dve.max(t8[:, t, :], gp[:, t, :])
                    link(last)
                    link(dve.memset(t8[:, :, 2:8], LOW))
                    for t in range(TB):
                        last = dve.match_replace(gr[:, t, :], t8[:, t, :], gp[:, t, :], TAKEN)
                    link(last)
                    link(dve.tensor_scalar(gm[:, :, :], gr[:, :, 0:4], TAKEN / 2, None, ALU.is_gt))
                    link(dve.tensor_tensor(v, v, gm[:, :, :].unsqueeze(3).broadcast_to([128, TB, 4, 8]), ALU.mult))
                    link(dve.tensor_scalar(c_, c_, 0.0, None, ALU.add))

            def route_top(l, b):
                top_values(ch, N_EXP[l], TOP_K[l])

            def route_mark(l, b):
                top_mark(ch, N_EXP[l], TOP_K[l], mr)

            def route_chosen(l, b):
                E = N_EXP[l]
                s_ = (ch if l == 1 else rt)[:, :, 0:E]
                m_ = selm[:, :, 0:E]
                last = dve.tensor_scalar(m_, mr[:, :, 0:E], TAKEN / 2, None, ALU.is_gt)
                link(last)
                if l == 2:
                    dve.tensor_copy(sel_bf[:, :, :], m_).then_inc(q["m_done"], 1)
                w_ = wsel[:, :, 0:E]
                link(dve.tensor_tensor(w_, m_, s_, ALU.mult))

            def route_weigh(l, b):
                E = N_EXP[l]
                w_ = wsel[:, :, 0:E]
                if l != 3:
                    link(dve.tensor_reduce(wsum[:, :], w_, AX, ALU.add))
                    if l == 0:
                        link(dve.tensor_scalar(wsum[:, :], wsum[:, :], 1e-20, None, ALU.add))
                    if l == 2:
                        link(dve.tensor_scalar(wsum[:, :], wsum[:, :], 1e-12, None, ALU.max))
                    link(dve.reciprocal(wrec[:, :], wsum[:, :]))
                    if l == 0:
                        link(dve.tensor_scalar(wrec[:, :], wrec[:, :], 2.5, None, ALU.mult))
                    link(dve.tensor_tensor(w_, w_, wrec[:, :].unsqueeze(2).broadcast_to([128, TB, E]), ALU.mult))

            def route_end(l, b):
                E = N_EXP[l]
                m_, w_ = selm[:, :, 0:E], wsel[:, :, 0:E]
                if l == 2:
                    dve.wait_ge(q["cum_ps"], b + 1)
                    cum = T[:, 0:128].rearrange("p (k e) -> p k e", k=TB)
                    link(dve.tensor_scalar(m_, cum, CAPACITY + 0.5, None, ALU.is_lt))
                    dve.sem_inc(q["T_free"], 1)
                    link(dve.tensor_tensor(w_, w_, m_, ALU.mult))
                for j in range(2):
                    link(dve.tensor_copy(chl[:, :, E * j:E * j + E], w_))
                    rest = w_ if j == 0 else chl[:, :, 2 * E:3 * E]
                    last = dve.tensor_tensor(rest, w_, chl[:, :, E * j:E * j + E], ALU.subtract)
                    if j == 0:
                        link(last)
                last.then_inc(q["comb_done"], 1)

            def combt_free(l, b):
                dve.wait_ge(q["combt_done"], fnum(l, b))
                dve.sem_inc(q["T_free"], 1)

            def mult(l, b, c):
                k = knum(l, b, c)
                h = hb[:, k % 4, :]
                dve.wait_ge(q["sg_done"], k + 1)
                if l == 1:
                    dve.wait_ge(q["u_done"], UB[1] + (k - CB[1]) // 4 + 1)
                    dve.tensor_tensor(h, h, W[(k // 4) % 2][:, :], ALU.mult).then_inc(q["h_done"], 1)
                    return
                dve.wait_ge(q["u_done"], UB[l] + k - CB[l] + 1)
                if c < ROUTED[l]:
                    link(dve.tensor_tensor(h, h, U[k % 2][:, :], ALU.mult))
                    dve.tensor_tensor(h, h, W[k % 2][:, :], ALU.mult).then_inc(q["h_done"], 1)
                else:
                    dve.tensor_tensor(h, h, U[k % 2][:, :], ALU.mult).then_inc(q["h_done"], 1)

            def low(l, b, c):
                k = knum(l, b, c)
                dve.wait_ge(q["hhi_done"], k + 1)
                dve.tensor_tensor(h_lo[:, k % 3, :], hb[:, k % 4, :], h_hi[:, k % 3, :].bitcast(F32),
                                  ALU.subtract).then_inc(q["hlo_dve"], 1)

            def split_halves(n):
                dve.wait_ge(q["ln_done"], norm_num(4, n))
                dve.tensor_tensor(halves[:, 0:2, :], freq[:, 0:2, :], freq[:, 2:4, :], ALU.add)
                dve.tensor_tensor(halves[:, 2:4, :], freq[:, 0:2, :], freq[:, 2:4, :], ALU.subtract).then_inc(q["fft_in"], 1)

            def filter_products(n):
                dve.wait_ge(q["w_sb"], 5)
                dve.wait_ge(q["fft_ps"], n + 1)
                dve.wait_ge(q["fft_in"], n + 1)
                w = wk[:, 0:5, 128 * n:128 * n + 128]
                xr_e, xi_e, xr_o, xi_o = [T[:, 128 * i:128 * i + 128].unsqueeze(1).broadcast_to([128, 2, 128]) for i in range(4)]
                dve.tensor_tensor(freq[:, 0:2, :], w[:, 0:2, :], xr_e, ALU.mult)
                dve.tensor_tensor(prod2[:, 0:2, :], w[:, 1:3, :], xi_e, ALU.mult)
                dve.tensor_tensor(freq[:, 2:4, :], w[:, 3:5, :], xr_o, ALU.mult)
                dve.tensor_tensor(prod2[:, 2, :], w[:, 4, :], T[:, 384:512], ALU.mult)
                link(dve.tensor_tensor(prod2[:, 3, :], w[:, 3, :], T[:, 384:512], ALU.mult))
                dve.sem_inc(q["T_free"], 1)
                dve.tensor_tensor(freq[:, 0:4:2, :], freq[:, 0:4:2, :], prod2[:, 0:4:2, :], ALU.subtract)
                dve.tensor_tensor(freq[:, 1:4:2, :], freq[:, 1:4:2, :], prod2[:, 1:4:2, :], ALU.add).then_inc(q["prod_done"], 1)

            def fft_update(n):
                if n == 0:
                    link(dve.tensor_scalar(tgn[:, :], tg[:, 2:3], -1.0, None, ALU.mult))
                xv = x[:, TB * n:TB * n + TB, :].rearrange("p (h k) d -> p h k d", h=2)
                even, odd = cols4(T)[:, 0:2, :], cols4(T)[:, 2:4, :]
                dve.wait_ge(q["inv_ps"], n + 1)
                for h in range(2):
                    last = dve.scalar_tensor_tensor(xv[:, h], even, tg[:, 2:3], xv[:, h], ALU.mult, ALU.add)
                link(last)
                dve.scalar_tensor_tensor(xv[:, 0], odd, tg[:, 2:3], xv[:, 0], ALU.mult, ALU.add)
                dve.scalar_tensor_tensor(xv[:, 1], odd, tgn[:, 0:1], xv[:, 1], ALU.mult, ALU.add).then_inc(q["x_done"], 1)
                dve.wait_ge(q["x_done"], x_num(4, n))
                dve.sem_inc(q["T_free"], 1)

            def weights0(r):
                slot, n, _ = quad(r)
                dve.wait_ge(q["l0w_hi"], r + 1)
                dve.tensor_tensor(wa_lo[:, slot:slot + n, :], cols4(T)[:, 0:n, :], wa_hi[:, slot:slot + n, :].bitcast(F32),
                                  ALU.subtract).then_inc(q["l0w_lo"], 1)
                dve.wait_ge(q["l0w_lo"], r + 1)
                dve.sem_inc(q["T_free"], 1)
                dve.sem_inc(q["stage_used"], 1)

            def max0(i):
                dve.wait_ge(q["z_s"], i + 1)
                dve.tensor_reduce(mx[:, i:i + 1], psum[:, 2 * (i % 2):2 * (i % 2) + 2, 0:KEYS0 // 2], mybir.AxisListType.XY,
                                  ALU.max, negate=True).then_inc(q["z_max"], 1)

            def probs0_out(i):
                dve.wait_ge(q["z_tr"], i + 1)
                if i >= 2:
                    dve.wait_ge(q["z_pv"], i - 1)
                dve.tensor_copy(pt0[i % 2], W[i % 2][:, :]).then_inc(q["z_pt"], 1)

            def update0(i):
                dve.wait_ge(q["z_pv"], i + 1)
                if i:
                    dve.wait_ge(q["z_up"], i)
                link(dve.reciprocal(sm1[:, 0, 0:1], zsum[:, i:i + 1]))
                link(dve.tensor_scalar(sm[:, 0:1], sm1[:, 0, 0:1], tg[:, 0:1], None, ALU.mult))
                dve.scalar_tensor_tensor(x[:, i, :], ACC[:, 0:128], sm[:, 0:1], x[:, i, :],
                                         ALU.mult, ALU.add).then_inc(q["z_up"], 1)
                if i % TB == TB - 1:
                    dve.wait_ge(q["z_up"], i + 1)
                    dve.sem_inc(q["x_done"], 1)

            dve.wait_ge(q["prep_ps"], 1)
            dve.tensor_copy(w0t[:, 0:4:3, :], cols4(bank[0])[:, 0:4:3, :])
            dve.tensor_copy(w0t[:, 1, :], bank[0][:, 128:256]).then_inc(ps, 1)
            dve.tensor_copy(ctxt, bank[0][:, 256:384]).then_inc(ps, 1)
            dve.wait_ge(q["prep_ps"], 2)
            dve.tensor_copy(lora_bt[:, :, :], cols4(bank[3])[0:R]).then_inc(ps, 1)
            norm(0, 0)
            dve.wait_ge(q["prep_ps"], 3)
            dve.scalar_tensor_tensor(w0, cols4(bank[6]), 2.0, w0t, ALU.mult, ALU.add).then_inc(ps, 1)
            norm(0, 1)
            dve.wait_ge(q["prep_ps"], 5)
            dve.tensor_copy(w1t, cols4(bank[1])).then_inc(ps, 1)
            dve.tensor_copy(wq1[:, :], bank[2][:, 384:512])
            dve.tensor_copy(w3t, cols4(bank[2])[:, 0:3, :]).then_inc(ps, 1)
            dve.wait_ge(q["prep_ps"], 7)
            dve.tensor_copy(rw[:, 0:72], bank[4][:, 0:72]).then_inc(ps, 1)
            dve.tensor_copy(bfc[:, :], bank[4][:, 128:160]).then_inc(ps, 1)
            dve.tensor_copy(bcol[:, :], bank[4][:, 160:169]).then_inc(ps, 1)
            dve.tensor_copy(sw_t[:, :, :], cols4(bank[5])[:, 0:3, :]).then_inc(ps, 1)
            dve.wait_ge(ps, 2)
            dve.tensor_reduce(ctx_mean[:, :], ctxt.rearrange("p (b t) -> p b t", b=B), AX, ALU.add).then_inc(q["dve"], 1)
            ch_.n += 1
            dve.wait_ge(q["dve"], ch_.n)
            link(dve.tensor_scalar(ctx_mean[:, :], ctx_mean[:, :], 1.0 / KEYS, None, ALU.mult))
            dve.wait_ge(ps, 10)
            dve.tensor_copy(wo1t[:, :], w1t[:, 2, :])
            dve.tensor_copy(ctx0, ctxt).then_inc(ps, 1)
            dve.tensor_scalar(bq1s[:, :], bcol[:, 3:4], DK ** -0.5, None, ALU.mult)
            dve.tensor_scalar(bq0s[:, :], bcol[:, 0:1], D ** -0.5, None, ALU.mult).then_inc(ps, 1)
            dve.wait_ge(q["prep_ps"], 8)
            dve.tensor_copy(w0[:, 2, :], bank[7][:, 0:128]).then_inc(ps, 1)
            dve.tensor_tensor(v0row, bank[7][0:1, 128:256], bo[:, 0, :], ALU.add).then_inc(ps, 1)
            dve.tensor_scalar(kt1[:, 0, :], bank[7][:, 256:384], bcol[:, 4:5], None, ALU.add).then_inc(ps, 1)
            dve.tensor_scalar(kt1[:, 1, :], bank[7][:, 384:512], bcol[:, 5:6], None, ALU.add).then_inc(ps, 1)
            dve.wait_ge(q["prep_ps"], 9)
            dve.tensor_copy(kv3[:, 0, :], bank[0][:, 0:128]).then_inc(ps, 1)
            dve.tensor_scalar(kv3[:, 1, :], bank[0][:, 128:256], bcol[:, 7:8], None, ALU.add).then_inc(ps, 1)
            dve.tensor_scalar(kmod[:, :], bank[0][:, 256:260], bcol[:, 8:9], None, ALU.add).then_inc(ps, 1)
            dve.wait_ge(q["prep_ps"], 10)
            sc = D ** -0.5
            dve.tensor_scalar(m3[:, :, :], bank[1][:, 256:384].rearrange("p (b n) -> p b n", b=B), sc, None, ALU.mult).then_inc(ps, 1)
            dve.wait_ge(q["prep_ps"], 11)
            dve.tensor_scalar(crow[:, :], bank[2][0:1, 256:384], sc, None, ALU.mult).then_inc(ps, 1)
            dve.wait_ge(q["prep_ps"], 13)
            dve.tensor_copy(v0c, cols4(bank[3])[0:KEYS]).then_inc(ps, 1)
            dve.tensor_copy(v3[:, :, :], cols4(bank[4])[0:KEYS]).then_inc(ps, 1)
            for j in range(3):
                link(dve.tensor_copy(bproj_bf[:, j, :], bproj))
                if j < 2:
                    link(dve.tensor_tensor(bproj, bproj, bproj_bf[:, j, :], ALU.subtract))
            link(dve.tensor_scalar(mask_add[:, :, :], mask_i[:, :, :], 0.0, NO_KEY, ALU.is_equal, ALU.mult))
            link(dve.tensor_reduce(anykeep[:, :], mask_add[:, :, :], AX, ALU.max))
            link(dve.tensor_scalar(anykeep[:, :], anykeep[:, :], NO_KEY / 2, None, ALU.is_gt))
            dve.wait_ge(q["prep_act"], 1)
            dve.tensor_tensor(rw_lo[:, :], rw[:, :], rw_hi[:, :].bitcast(F32), ALU.subtract)
            link(dve.memset(run[:, :, :], 0.0))

            dve.wait_ge(q["act"], 1)
            for s in range(STAGES):
                l = s // 2
                if s == 0:
                    max0(0)
                    for i in range(16):
                        if i < 15:
                            max0(i + 1)
                        if i < NQ0:
                            weights0(i)
                        if i == 13:
                            lo_x(0, 0)
                        probs0_out(i)
                        if i >= 1:
                            update0(i - 1)
                        if i % 4 == 2 and i < 8:
                            norm(0, i // 4 + 2)
                        if i == 9:
                            moments(1, 0)
                        if i == 10:
                            scale_rows(1, 0)
                        if i == 14:
                            route_scores(0, 0)
                            route_pairs(0, 0)
                        if i == 15:
                            route_groups(0, 0)
                            route_top(0, 0)
                            route_mark(0, 0)
                            route_chosen(0, 0)
                    update0(15)
                    route_weigh(0, 0)
                    route_end(0, 0)
                elif s in (4, 6):
                    continue
                elif s == 2:
                    shift1(0)
                    shift1(1)
                    for i in range(16):
                        b, k = divmod(i, TB)
                        sums1(i)
                        if i + 2 < 16:
                            shift1(i + 2)
                        if k == 1 and b >= 1:
                            dve.wait_ge(q["pv_ps"], 4 * b)
                            update(s, b - 1, ACC, tg[:, 1:2])
                        if k == 1 and b + 2 < B:
                            moments(s, b + 2)
                        if k == 2 and b + 2 < B:
                            scale_rows(s, b + 2)
                        if i == 13:
                            lo_x(1, 0)
                        if i == 10:
                            moments(3, 0)
                        if i == 11:
                            scale_rows(3, 0)
                        if i == 14:
                            route_shift(1, 0)
                        if i == 15:
                            route_scores(1, 0)
                            route_top(1, 0)
                            route_mark(1, 0)
                            route_chosen(1, 0)
                            route_weigh(1, 0)
                            route_end(1, 0)
                    dve.wait_ge(q["pv_ps"], 16)
                    update(s, 3, ACC, tg[:, 1:2])
                else:
                    if l != 2:
                        combt_free(l, 0)
                    for b in range(B):
                        for c in range(NC[l]):
                            mult(l, b, c)
                            if (b or c) and low_on(l, (c - 1) % NC[l]) == "dve":
                                low(l, *divmod(b * NC[l] + c - 1, NC[l]))
                            if c == ADD_AT and b >= 1:
                                dve.wait_ge(q["outt_ps"], fnum(l, b - 1))
                                update(s, b - 1, T, tg[:, 4 + l:5 + l])
                                dve.wait_ge(q["x_done"], x_num(s, b - 1))
                                dve.sem_inc(q["T_free"], 1)
                            n = next3(l, b)
                            if n is not None:
                                if c == NORM_AT:
                                    moments(6, n)
                                if c == 2:
                                    scale_rows(6, n)
                                if c == 5:
                                    shift(n)
                                if c == 7:
                                    normalise(n)
                                if c == ADD3_AT:
                                    dve.wait_ge(q["pv_ps"], softmax_num(3, n) + 1)
                                    update(6, n, T, tg[:, 3:4])
                                    dve.wait_ge(q["x_done"], x_num(6, n))
                                    dve.sem_inc(q["T_free"], 1)
                                    moments(7, n)
                                if c == 11:
                                    scale_rows(7, n)
                                if c == 13:
                                    lo_x(3, n)
                                if c == 14:
                                    route_scores(3, n)
                                    route_top(3, n)
                                if c == 15:
                                    route_mark(3, n)
                                if c == 16:
                                    route_chosen(3, n)
                                    route_weigh(3, n)
                                if c == (16 if l == 2 else 17):
                                    route_end(3, n)
                                if c == 18:
                                    combt_free(3, n)
                            elif b + 1 < B:
                                if c == NORM_AT:
                                    moments(s, b + 1)
                                if c == XN_AT:
                                    scale_rows(s, b + 1)
                                if c == XLO_AT:
                                    lo_x(l, b + 1)
                                if c == SCORE_AT:
                                    route_shift(l, b + 1)
                                for part, at in zip((route_scores, route_pairs, route_groups, route_top, route_mark, route_chosen, route_weigh), ROUTE_AT[l]):
                                    if c == at:
                                        part(l, b + 1)
                                if c == WEIGH_AT[l]:
                                    route_end(l, b + 1)
                                if c == COMBT_AT[l]:
                                    combt_free(l, b + 1)
                            n, at = fft_steps(l, b)
                            if c == at[0]:
                                moments(4, n)
                            if c == at[1]:
                                scale_rows(4, n)
                                split_halves(n)
                            if c == at[3]:
                                filter_products(n)
                            if c == at[5]:
                                fft_update(n)
                            if l == 0 and b + 1 == B:
                                if c == NORM_AT:
                                    moments(2, 0)
                                if c == XN_AT:
                                    scale_rows(2, 0)
                                if c == NORM2_AT:
                                    moments(2, 1)
                                if c == XN2_AT:
                                    scale_rows(2, 1)
                            if l == 1 and b == 0 and c == TAP_AT:
                                for j in range(B):
                                    last = dve.tensor_scalar(xt[:, 0, 128 * j:128 * j + 128], w2conv[:, :], kmod[:, j:j + 1], None, ALU.mult)
                                last.then_inc(q["dw_done"], 1)
                            if l == 1 and b + 1 == B:
                                if c == PRE5[0]:
                                    moments(5, 0)
                                if c == PRE5[1]:
                                    scale_rows(5, 0)
                                if c == PRE5[4]:
                                    lo_x(2, 0)
                                if c == PRE5[6]:
                                    route_scores(2, 0)
                                if c == PRE5[7]:
                                    route_top(2, 0)
                                    route_mark(2, 0)
                                if c == PRE5[8]:
                                    route_chosen(2, 0)
                                    route_weigh(2, 0)
                                if c == PRE5[10]:
                                    route_end(2, 0)
                                if c == PRE5[12]:
                                    combt_free(2, 0)
                    if low_on(l, NC[l] - 1) == "dve":
                        low(l, B - 1, NC[l] - 1)
                    dve.wait_ge(q["outt_ps"], fnum(l, B - 1))
                    update(s, B - 1, T, tg[:, 4 + l:5 + l])
                    dve.wait_ge(q["x_done"], x_num(s, B - 1))
                    dve.sem_inc(q["T_free"], 1)
    return nc


def _inputs():
    return ["x", "ctx_1024", "mask_1x1xSxS2_ik0", "g_xattn", "g_ffn"] + [
        f"L0_xattn_{k}{w}" for w in "qkvo" for k in "WbAB"] + [
        "L0_ffn_" + n for n in ("gate_w", "gate_bias", "expert_gate", "expert_up", "expert_down", "shared_gate", "shared_up", "shared_down")] + [
        f"L1_xattn_{k}{w}" for w in "qkvo" for k in "Wb"] + [
        "L1_ffn_" + n for n in ("router_w", "w_fc", "b_fc", "w_proj", "b_proj")] + [
        "L2_xattn_" + n for n in ("weight", "kp_w", "kp_b")] + [
        "L2_ffn_" + n for n in ("gate_w", "bias", "W1", "W3", "W2", "sw1", "sw3", "sw2")] + [
        "L3_xattn_" + n for n in ("Wk", "Wv", "bv", "Wq", "bq", "Wo", "bo")] + [
        "L3_ffn_" + n for n in ("router_w", "expert_bias", "shared_w1", "shared_w2", "shared_w3", "routed_w1", "routed_w2", "routed_w3")]


def kernel(**inputs):
    import concourse.bacc as bacc
    from concourse.bass_utils import run_bass_kernel_spmd

    nc = bacc.Bacc("TRN2", target_bir_lowering=False, num_devices=1)
    arrays, a = {}, {}
    for name in _inputs():
        arrays["in_" + name] = np.ascontiguousarray(inputs[name])
    arrays["in_consts"] = constants()
    for name, v in arrays.items():
        a[name[3:]] = nc.dram_tensor(name, v.shape, mybir.dt.from_np(v.dtype), kind="ExternalInput").ap()
    out = nc.dram_tensor("out", (B, S, D), F32, kind="ExternalOutput").ap()
    build(nc, a, out)
    r = run_bass_kernel_spmd(nc, [arrays], core_ids=[0])
    return r.results[0]["out"]
```
